# Optimizing a Trainium2 kernel written in Bass

```python
import numpy as np
import jax
import jax.numpy as jnp

def _softmax(x, axis=-1):
    return jax.nn.softmax(x, axis=axis)

def _gelu(x):
    return jax.nn.gelu(x, approximate=True)

def _silu(x):
    return jax.nn.silu(x)

def _sigmoid(x):
    return jax.nn.sigmoid(x)

def _layernorm(x, axis=-1, eps=1e-05):
    m = jnp.mean(x, axis=axis, keepdims=True)
    v = jnp.var(x, axis=axis, keepdims=True)
    return (x - m) / jnp.sqrt(v + eps)

def _scatter_add(tgt, idx, src, axis=0):
    return tgt.at[idx].add(src)

def _segment_sum(src, seg, n):
    return jax.ops.segment_sum(src, seg, n)
kernel_name = 'mk_xattn_ffn_d2_seqx_r8_57e738'

def setup_inputs(seed: int=0):
    np.random.seed(seed)
    _w = jnp.asarray

    def _rec_inputs():
        import jax
        import jax.numpy as jnp
        _rk = jax.random.key(seed)
        x = -0.000125 + 0.9999 * jax.random.normal(jax.random.fold_in(_rk, 1), (2, 512, 128), jnp.float32)
        _lenS = 512 - jax.random.randint(jax.random.fold_in(_rk, 7), (2,), 0, max(1, 512 // 4) + 1, jnp.int32)
        _lenS2 = 154 - jax.random.randint(jax.random.fold_in(_rk, 8), (2,), 0, max(1, 154 // 4) + 1, jnp.int32)
        _ctx_768P = jax.random.normal(jax.random.fold_in(_rk, 11), (2, 16, 96), jnp.float32)
        _ctx_768c = jax.random.dirichlet(jax.random.fold_in(_rk, 511), 0.3 * jnp.ones((16,), jnp.float32), (2, 154))
        _ctx_768t = jnp.einsum('bsk,bkd->bsd', _ctx_768c, _ctx_768P)
        _ctx_768t = _ctx_768t * jax.lax.rsqrt(jnp.mean(jnp.square(_ctx_768t)) + 1e-12) * 0.953939
        ctx_768 = 0.00272024 + 0.999456 * (_ctx_768t + 0.3 * jax.random.normal(jax.random.fold_in(_rk, 611), (2, 154, 96), jnp.float32))
        return (x, ctx_768)
    x, ctx_768 = _rec_inputs()

    def _L0_xattn_setup():
        import jax, jax.numpy as jnp
        import numpy as np
        QUERY_DIM = 128
        CONTEXT_DIM = 96
        HEADS = 8
        DIM_HEAD = 64
        INNER = HEADS * DIM_HEAD
        key = jax.random.key(seed)
        ks = jax.random.split(key, 7)
        B, S, L = (8, 512, 77)
        x = jax.random.normal(ks[0], (B, S, QUERY_DIM), dtype=jnp.float32)
        context = jax.random.normal(ks[1], (B, L, CONTEXT_DIM), dtype=jnp.float32)
        Wq = jax.random.normal(ks[2], (QUERY_DIM, INNER), dtype=jnp.float32) * QUERY_DIM ** (-0.5)
        Wk = jax.random.normal(ks[3], (CONTEXT_DIM, INNER), dtype=jnp.float32) * CONTEXT_DIM ** (-0.5)
        Wv = jax.random.normal(ks[4], (CONTEXT_DIM, INNER), dtype=jnp.float32) * CONTEXT_DIM ** (-0.5)
        Wo = jax.random.normal(ks[5], (INNER, QUERY_DIM), dtype=jnp.float32) * INNER ** (-0.5)
        bo = jax.random.normal(ks[6], (QUERY_DIM,), dtype=jnp.float32) * 0.01
        return {'x': x, 'context': context, 'Wq': Wq, 'Wk': Wk, 'Wv': Wv, 'Wo': Wo, 'bo': bo}
    _L0_xattn_all = _L0_xattn_setup()
    _L0_xattn_in = {k: v for k, v in _L0_xattn_all.items() if k in ('Wq', 'Wk', 'Wv', 'Wo', 'bo')}
    del _L0_xattn_all

    def _L0_ffn_setup():
        import jax, jax.numpy as jnp
        import numpy as np
        B, S, H = (2, 128, 128)
        E, F = (16, 64)
        G, TOPK_G, TOPK = (4, 2, 4)
        N_SHARED = 2
        ROUTE_SCALE = 1.0
        FS = N_SHARED * F

        def _gate(x, w_gate):
            T = x.shape[0]
            scores = jax.nn.sigmoid(x @ w_gate.T)
            sv = scores.reshape(T, G, E // G)
            group_scores = jax.lax.top_k(sv, 2)[0].sum(-1)
            top_groups = jax.lax.top_k(group_scores, TOPK_G)[1]
            allowed = jnp.zeros((T, G), dtype=bool).at[jnp.arange(T)[:, None], top_groups].set(True)
            masked = jnp.where(allowed[:, :, None], sv, -jnp.inf).reshape(T, E)
            _, idx = jax.lax.top_k(masked, TOPK)
            w = jnp.take_along_axis(scores, idx, axis=1)
            w = w / (w.sum(-1, keepdims=True) + 1e-06) * ROUTE_SCALE
            return (w, idx)

        def _swiglu(x, w1, w3, w2):
            return jax.nn.silu(x @ w1.T) * (x @ w3.T) @ w2.T
        key = jax.random.key(seed)
        ks = jax.random.split(key, 8)
        scale = 0.02
        return {'hidden_states': jax.random.normal(ks[0], (B, S, H), dtype=jnp.float32), 'w_gate': jax.random.normal(ks[1], (E, H), dtype=jnp.float32) * scale, 'w1_e': jax.random.normal(ks[2], (E, F, H), dtype=jnp.float32) * scale, 'w3_e': jax.random.normal(ks[3], (E, F, H), dtype=jnp.float32) * scale, 'w2_e': jax.random.normal(ks[4], (E, H, F), dtype=jnp.float32) * scale, 'w1_s': jax.random.normal(ks[5], (FS, H), dtype=jnp.float32) * scale, 'w3_s': jax.random.normal(ks[6], (FS, H), dtype=jnp.float32) * scale, 'w2_s': jax.random.normal(ks[7], (H, FS), dtype=jnp.float32) * scale}
    _L0_ffn_all = _L0_ffn_setup()
    _L0_ffn_in = {k: v for k, v in _L0_ffn_all.items() if k in ('w_gate', 'w1_e', 'w3_e', 'w2_e', 'w1_s', 'w3_s', 'w2_s')}
    del _L0_ffn_all

    def _L1_xattn_setup():
        import jax, jax.numpy as jnp
        import numpy as np
        NUM_HEADS = 16
        EMB_DIM = 128
        CTX_DIM = 96
        D_HEAD = EMB_DIM // NUM_HEADS
        key = jax.random.key(seed)
        ks = jax.random.split(key, 6)
        B, SQ, SKV = (4, 256, 256)
        x = jax.random.normal(ks[0], (B, SQ, EMB_DIM), dtype=jnp.float32)
        ctx = jax.random.normal(ks[1], (B, SKV, CTX_DIM), dtype=jnp.float32)
        sc_q = 1.0 / np.sqrt(EMB_DIM)
        sc_kv = 1.0 / np.sqrt(CTX_DIM)
        Wq = jax.random.normal(ks[2], (EMB_DIM, EMB_DIM), dtype=jnp.float32) * sc_q
        Wk = jax.random.normal(ks[3], (CTX_DIM, EMB_DIM), dtype=jnp.float32) * sc_kv
        Wv = jax.random.normal(ks[4], (CTX_DIM, EMB_DIM), dtype=jnp.float32) * sc_kv
        Wo = jax.random.normal(ks[5], (EMB_DIM, EMB_DIM), dtype=jnp.float32) * sc_q
        return {'x': x, 'contenoised_img': ctx, 'Wq': Wq, 'Wk': Wk, 'Wv': Wv, 'Wo': Wo}
    _L1_xattn_all = _L1_xattn_setup()
    _L1_xattn_in = {k: v for k, v in _L1_xattn_all.items() if k in ('Wq', 'Wk', 'Wv', 'Wo')}
    del _L1_xattn_all

    def _L1_ffn_setup():
        import jax, jax.numpy as jnp
        import numpy as np
        D, H, E, K, S = (128, 256, 8, 2, 1)
        B, L = (4, 256)
        key = jax.random.key(seed)
        ks = jax.random.split(key, 9)
        std = 0.02
        return {'x': jax.random.normal(ks[0], (B, L, D), dtype=jnp.float32), 'router_w': jax.random.normal(ks[1], (E, D), dtype=jnp.float32) * std, 'experts_bias': jnp.zeros((E,), dtype=jnp.float32), 'w1': jax.random.normal(ks[2], (E, D, H), dtype=jnp.float32) * std, 'w3': jax.random.normal(ks[3], (E, D, H), dtype=jnp.float32) * std, 'w2': jax.random.normal(ks[4], (E, H, D), dtype=jnp.float32) * std, 'sw1': jax.random.normal(ks[5], (S, D, H), dtype=jnp.float32) * std, 'sw3': jax.random.normal(ks[6], (S, D, H), dtype=jnp.float32) * std, 'sw2': jax.random.normal(ks[7], (S, H, D), dtype=jnp.float32) * std}
    _L1_ffn_all = _L1_ffn_setup()
    _L1_ffn_in = {k: v for k, v in _L1_ffn_all.items() if k in ('router_w', 'experts_bias', 'w1', 'w3', 'w2', 'sw1', 'sw3', 'sw2')}
    del _L1_ffn_all
    return {'x': x, 'ctx_768': ctx_768, 'L0_xattn_Wq': _L0_xattn_in['Wq'], 'L0_xattn_Wk': _L0_xattn_in['Wk'], 'L0_xattn_Wv': _L0_xattn_in['Wv'], 'L0_xattn_Wo': _L0_xattn_in['Wo'], 'L0_xattn_bo': _L0_xattn_in['bo'], 'L0_ffn_w_gate': _L0_ffn_in['w_gate'], 'L0_ffn_w1_e': _L0_ffn_in['w1_e'], 'L0_ffn_w3_e': _L0_ffn_in['w3_e'], 'L0_ffn_w2_e': _L0_ffn_in['w2_e'], 'L0_ffn_w1_s': _L0_ffn_in['w1_s'], 'L0_ffn_w3_s': _L0_ffn_in['w3_s'], 'L0_ffn_w2_s': _L0_ffn_in['w2_s'], 'L1_xattn_Wq': _L1_xattn_in['Wq'], 'L1_xattn_Wk': _L1_xattn_in['Wk'], 'L1_xattn_Wv': _L1_xattn_in['Wv'], 'L1_xattn_Wo': _L1_xattn_in['Wo'], 'L1_ffn_router_w': _L1_ffn_in['router_w'], 'L1_ffn_experts_bias': _L1_ffn_in['experts_bias'], 'L1_ffn_w1': _L1_ffn_in['w1'], 'L1_ffn_w3': _L1_ffn_in['w3'], 'L1_ffn_w2': _L1_ffn_in['w2'], 'L1_ffn_sw1': _L1_ffn_in['sw1'], 'L1_ffn_sw3': _L1_ffn_in['sw3'], 'L1_ffn_sw2': _L1_ffn_in['sw2']}

def reference(x, ctx_768, L0_xattn_Wq, L0_xattn_Wk, L0_xattn_Wv, L0_xattn_Wo, L0_xattn_bo, L0_ffn_w_gate, L0_ffn_w1_e, L0_ffn_w3_e, L0_ffn_w2_e, L0_ffn_w1_s, L0_ffn_w3_s, L0_ffn_w2_s, L1_xattn_Wq, L1_xattn_Wk, L1_xattn_Wv, L1_xattn_Wo, L1_ffn_router_w, L1_ffn_experts_bias, L1_ffn_w1, L1_ffn_w3, L1_ffn_w2, L1_ffn_sw1, L1_ffn_sw3, L1_ffn_sw2):
    import jax
    import jax.numpy as jnp

    def _L0_xattn_ref(x, context, Wq, Wk, Wv, Wo, bo):
        import jax, jax.numpy as jnp
        import numpy as np
        QUERY_DIM = 128
        CONTEXT_DIM = 96
        HEADS = 8
        DIM_HEAD = 64
        INNER = HEADS * DIM_HEAD
        B, S, _ = x.shape
        L = context.shape[1]
        scale = DIM_HEAD ** (-0.5)
        q = (x @ Wq).reshape(B, S, HEADS, DIM_HEAD).transpose(0, 2, 1, 3)
        k = (context @ Wk).reshape(B, L, HEADS, DIM_HEAD).transpose(0, 2, 1, 3)
        v = (context @ Wv).reshape(B, L, HEADS, DIM_HEAD).transpose(0, 2, 1, 3)
        attn = jnp.einsum('bhsd,bhld->bhsl', q, k) * scale
        attn = jax.nn.softmax(attn, axis=-1)
        out = jnp.einsum('bhsl,bhld->bhsd', attn, v)
        out = out.transpose(0, 2, 1, 3).reshape(B, S, INNER)
        return out @ Wo + bo

    def _L0_ffn_ref(hidden_states, w_gate, w1_e, w3_e, w2_e, w1_s, w3_s, w2_s):
        import jax, jax.numpy as jnp
        import numpy as np
        B, S, H = (2, 128, 128)
        E, F = (16, 64)
        G, TOPK_G, TOPK = (4, 2, 4)
        N_SHARED = 2
        ROUTE_SCALE = 1.0
        FS = N_SHARED * F

        def _gate(x, w_gate):
            T = x.shape[0]
            scores = jax.nn.sigmoid(x @ w_gate.T)
            sv = scores.reshape(T, G, E // G)
            group_scores = jax.lax.top_k(sv, 2)[0].sum(-1)
            top_groups = jax.lax.top_k(group_scores, TOPK_G)[1]
            allowed = jnp.zeros((T, G), dtype=bool).at[jnp.arange(T)[:, None], top_groups].set(True)
            masked = jnp.where(allowed[:, :, None], sv, -jnp.inf).reshape(T, E)
            _, idx = jax.lax.top_k(masked, TOPK)
            w = jnp.take_along_axis(scores, idx, axis=1)
            w = w / (w.sum(-1, keepdims=True) + 1e-06) * ROUTE_SCALE
            return (w, idx)

        def _swiglu(x, w1, w3, w2):
            return jax.nn.silu(x @ w1.T) * (x @ w3.T) @ w2.T
        shape = hidden_states.shape
        x = hidden_states.reshape(-1, H)
        weights, idx = _gate(x, w_gate)
        combine = (jax.nn.one_hot(idx, E, dtype=x.dtype) * weights[..., None]).sum(1)
        g = jax.nn.silu(jnp.einsum('th,efh->tef', x, w1_e))
        u = jnp.einsum('th,efh->tef', x, w3_e)
        routed = jnp.einsum('tef,ehf,te->th', g * u, w2_e, combine)
        shared = _swiglu(x, w1_s, w3_s, w2_s)
        return (routed + shared).reshape(shape)

    def _L1_xattn_ref(x, contenoised_img, Wq, Wk, Wv, Wo):
        import jax, jax.numpy as jnp
        import numpy as np
        NUM_HEADS = 16
        EMB_DIM = 128
        CTX_DIM = 96
        D_HEAD = EMB_DIM // NUM_HEADS
        B, SQ, E = x.shape
        SKV = contenoised_img.shape[1]
        q = x @ Wq
        k = contenoised_img @ Wk
        v = contenoised_img @ Wv
        q = q.reshape(B, SQ, NUM_HEADS, D_HEAD).transpose(0, 2, 1, 3)
        k = k.reshape(B, SKV, NUM_HEADS, D_HEAD).transpose(0, 2, 1, 3)
        v = v.reshape(B, SKV, NUM_HEADS, D_HEAD).transpose(0, 2, 1, 3)
        scale = 1.0 / jnp.sqrt(jnp.asarray(D_HEAD, dtype=q.dtype))
        scores = jnp.einsum('bhqd,bhkd->bhqk', q, k) * scale
        weights = jax.nn.softmax(scores, axis=-1)
        out = jnp.einsum('bhqk,bhkd->bhqd', weights, v)
        out = out.transpose(0, 2, 1, 3).reshape(B, SQ, E)
        return out @ Wo

    def _L1_ffn_ref(x, router_w, experts_bias, w1, w3, w2, sw1, sw3, sw2):
        import jax, jax.numpy as jnp
        import numpy as np
        D, H, E, K, S = (128, 256, 8, 2, 1)
        B, L = (4, 256)
        b, l, d = x.shape
        xf = x.reshape(-1, d)
        sg = jnp.einsum('td,sdh->tsh', xf, sw1)
        su = jnp.einsum('td,sdh->tsh', xf, sw3)
        shared_out = jnp.einsum('tsh,shd->td', jax.nn.silu(sg) * su, sw2)
        logits = xf @ router_w.T + experts_bias
        rw, sel = jax.lax.top_k(logits, K)
        rw = jax.nn.softmax(rw.astype(jnp.float32), axis=-1).astype(x.dtype)
        cw = (jax.nn.one_hot(sel, E, dtype=x.dtype) * rw[..., None]).sum(axis=1)
        g = jnp.einsum('td,edh->teh', xf, w1)
        u = jnp.einsum('td,edh->teh', xf, w3)
        eo = jax.nn.silu(g) * u
        moe_out = jnp.einsum('te,teh,ehd->td', cw, eo, w2)
        return (moe_out + shared_out).reshape(b, l, d)
    x = x + _L0_xattn_ref(_layernorm(x, axis=-1), ctx_768, L0_xattn_Wq, L0_xattn_Wk, L0_xattn_Wv, L0_xattn_Wo, L0_xattn_bo)
    x = x + _L0_ffn_ref(_layernorm(x, axis=-1), L0_ffn_w_gate, L0_ffn_w1_e, L0_ffn_w3_e, L0_ffn_w2_e, L0_ffn_w1_s, L0_ffn_w3_s, L0_ffn_w2_s)
    x = x + _L1_xattn_ref(_layernorm(x, axis=-1), ctx_768, L1_xattn_Wq, L1_xattn_Wk, L1_xattn_Wv, L1_xattn_Wo)
    x = x + _L1_ffn_ref(_layernorm(x, axis=-1), L1_ffn_router_w, L1_ffn_experts_bias, L1_ffn_w1, L1_ffn_w3, L1_ffn_w2, L1_ffn_sw1, L1_ffn_sw3, L1_ffn_sw2)
    return x

_drawn_inputs = setup_inputs


def setup_inputs(seed=0):
    import zlib

    import numpy as np

    out = dict(_drawn_inputs(seed))
    spreads = {'L1_ffn_experts_bias': (0.0, 0.8)}
    factors = {'L0_xattn_bo': 6.753,
     'L0_ffn_w_gate': 8.0,
     'L0_ffn_w1_e': 8.0,
     'L0_ffn_w3_e': 8.0,
     'L0_ffn_w2_e': 8.0,
     'L0_ffn_w1_s': 8.0,
     'L0_ffn_w3_s': 8.0,
     'L0_ffn_w2_s': 8.0,
     'L1_ffn_router_w': 8.0,
     'L1_ffn_w1': 8.0,
     'L1_ffn_w3': 8.0,
     'L1_ffn_w2': 8.0,
     'L1_ffn_sw1': 8.0,
     'L1_ffn_sw3': 8.0,
     'L1_ffn_sw2': 8.0}
    for name, (base, spread) in spreads.items():
        noise = np.random.default_rng([zlib.crc32(name.encode()), seed]).standard_normal(out[name].shape)
        drawn = base * np.exp(spread * noise) if base else spread * noise
        out[name] = jnp.asarray(drawn.astype(out[name].dtype))
    for name, factor in factors.items():
        out[name] = (out[name] * factor).astype(out[name].dtype)
    return out
```

```python
from contextlib import ExitStack

import numpy as np

import concourse.bass as bass
from concourse import mybir

F32 = mybir.dt.float32
F32R = mybir.dt.float32r
ACT = mybir.ActivationFunctionType
ALU = mybir.AluOpType
AX = mybir.AxisListType.X

P = 128
B = 2
T = 4
TOK = T * P
CTX, CD = 154, 96
REST = CTX - P
PAD = 32
CP = P + PAD
EPS = 1e-5

H0, DH0 = 8, 64
PAIRS = H0 // 2
H1, DH1 = 16, 8
G1 = H1 // 4
E0, F0 = 16, 64
E1, F1 = 8, 256
NG, TOPK0, TOPK1 = 4, 4, 2
N_HID = {1: 1 + E0 * F0 // P, 3: 2 + E1 * F1 // P}
N_SHARED = {1: 1, 3: 2}
EXPERTS = {1: E0, 3: E1}
SLOTS = 8
CHUNK = 6
OUT_NAME = "out"


def make_order():
    o = []

    def scores(b, t):
        o.extend(("score", b, t, p) for p in range(PAIRS))

    def probs(b, t):
        o.append(("norm", b, t))
        o.extend(("pT", b, t, k) for k in range(3))

    def ffn(s, b, extra, done=0):
        n = N_HID[s]
        for i in range(n + 2):
            o.extend(extra.get(i, []))
            if done <= i < n:
                o.append(("hid", s, b, i))
            if i >= 2:
                o.append(("down", s, b, i - 2))
        o.append(("res", s, b))

    o += [("split", "wq0", 0), ("lnA", 0, 0), ("lnA", 0, 1)]
    o += [("kT", p) for p in range(PAIRS)]
    o += [("lnB", 0, 0), ("xT", 0, 0), ("lnB", 0, 1)]
    o += [("q", 0, p) for p in range(PAIRS)]
    o += [("xT", 0, 1), ("split", "gates", 0)]
    scores(0, 0)
    o += [("bo", 0), ("bo", 1), ("vf", 0)]
    scores(0, 1)
    probs(0, 0)
    o += [("vs", 0)]
    scores(0, 2)
    probs(0, 1)
    o += [("q", 1, p) for p in range(PAIRS)]
    scores(0, 3)
    probs(0, 2)
    scores(1, 0)
    probs(0, 3)
    o += [("vf", 1), ("vs", 1)]
    o += [("pv", 0, p) for p in range(PAIRS)]
    scores(1, 1)
    o += [("wo", 0)]
    probs(1, 0)
    o += [("lnA", 1, 0)]
    scores(1, 2)
    o += [("lnB", 1, 0)]
    probs(1, 1)
    o += [("xT", 1, 0), ("gate", 1, 0)]
    scores(1, 3)
    probs(1, 2)
    o += [("route", 1, 0)]
    o += [("split", "w13_0", c) for c in range(2 * N_HID[1] // CHUNK)]
    probs(1, 3)
    o += [("cwT", 1, 0)]
    o += [("pv", 1, p) for p in range(PAIRS)]
    o += [("wo", 1)]
    sp1 = [("split", "w13_1", c) for c in range(2 * N_HID[3] // CHUNK)]
    ctx1 = [("clear1",), ("split", "wq1", 0)] + [("k1", g) for g in range(G1)]
    v1 = [("vf1", b) for b in range(B)] + [("vs1", b) for b in range(B)]
    ffn(1, 0, {1: [("lnA", 1, 1)], 2: [("lnB", 1, 1), ("xT", 1, 1), ("gate", 1, 1)],
               3: [("route", 1, 1)], 5: [("cwT", 1, 1)], 6: ctx1, 8: v1})
    score1 = lambda b, t: [("score1", b, t, g, h) for g in range(G1) for h in range(2)]
    ffn(1, 1, {1: [("lnA", 2, 0)], 2: [("lnB", 2, 0), ("xT", 2, 0)],
               3: [("q1", 0, g) for g in range(G1)], 4: score1(0, 0), 5: score1(0, 1),
               6: sp1[:2], 7: score1(0, 2), 8: score1(0, 3), 9: [("mT", 0)]})
    o += [("lnA", 2, 1)]
    back = []
    for b in range(B):
        for g in range(G1):
            o += [("expT", b, g, j) for j in range(5)]
            if b == 0:
                if g == 0:
                    o += [("lnB", 2, 1), ("xT", 2, 1)] + [("q1", 1, k) for k in range(G1)]
                o += score1(1, g)
            o += back
            back = [("pv1", b, g), ("oT", b, g)]
            if b == 0 and g == 3:
                o += [("mT", 1)]
            if b == 1 and g == 0:
                o += [("onT", 0), ("wo1", 0), ("lnA", 3, 0)]
            if b == 1 and g == 1:
                o += [("lnB", 3, 0), ("xT", 3, 0), ("gate", 3, 0)]
            if b == 1 and g == 2:
                o += [("route", 3, 0)] + sp1[2:4]
    o += [("cwT", 3, 0)] + back + [("hid", 3, 0, 0), ("hid", 3, 0, 1), ("onT", 1), ("split", "w13_1", 4), ("wo1", 1)]
    ffn(3, 0, {2: [("split", "w13_1", 5), ("lnA", 3, 1)], 3: [("lnB", 3, 1), ("xT", 3, 1), ("gate", 3, 1)],
               4: [("route", 3, 1)], 6: [("cwT", 3, 1)]}, done=2)
    ffn(3, 1, {})
    return o


RING = {
    "score": (0, 1, 2, 3), "hid1": (0, 1, 2, 3), "hid3": (0, 1, 2, 3), "score1": (0, 1, 2, 3), "expT": (0, 1, 2, 3),
    "kT": (4, 5), "vf": (4, 5), "vs": (4, 5), "xT": (4, 5), "q": (4, 5), "pT": (4, 5), "gate": (4, 5),
    "cwT": (4, 5), "k1": (4, 5), "vf1": (4, 5), "vs1": (4, 5), "q1": (4, 5), "mT": (4, 5), "oT": (4, 5), "onT": (4, 5),
    "pv": (6, 7), "wo": (6, 7), "y": (6, 7), "pv1": (6, 7), "wo1": (6, 7),
}


def count_uses(order):
    uses, turn, count = {}, {}, {}
    for step in order:
        kind = step[0]
        if kind == "hid":
            keys = [("hid1",) + step[1:], ("hid3",) + step[1:]]
            if step[3] == 0:
                keys.append(("y",) + step[1:3])
        else:
            keys = [step] if kind in RING else []
        for key in keys:
            ring = RING[key[0]]
            n = turn.get(ring, 0)
            turn[ring] = n + 1
            bank = ring[n % len(ring)]
            count[bank] = count.get(bank, 0) + 1
            uses[key] = (bank, count[bank])
    return uses


def build(nc, a, out):
    order = make_order()
    uses = count_uses(order)
    position = {}
    seen = {}
    for step in order:
        seen[step[0]] = seen.get(step[0], 0) + 1
        position[step] = seen[step[0]]

    with ExitStack() as ctx:
        def sb(name, shape, dt=F32, at=ctx):
            return at.enter_context(nc.sbuf_tensor(name, shape, dt))

        def sem(name):
            return ctx.enter_context(nc.semaphore(name))

        psum = ctx.enter_context(nc.psum_tensor("psum", [P, 8, 512], F32))

        X = sb("X", [P, B * T, P])
        xn = sb("xn", [P, B, T, P])
        xT_hi = sb("xT_hi", [P, B, TOK], F32R)
        xT_lo = sb("xT_lo", [P, B, TOK], F32R)
        w_src = sb("w_src", [P, N_HID[1] * 2, P])
        spread = sb("spread", [P, SLOTS, TOK])
        act_s = sb("act_s", [P, 2, TOK])
        gated_u = sb("gated_u", [P, 2, TOK])
        hid = sb("hid", [P, 3, TOK])
        ident = sb("ident", [P, P])
        bo = sb("bo", [P, P])
        ctxT = sb("ctxT", [CD + 1, B, CP])
        ctxT_rest = sb("ctxT_rest", [CD + 1, B, P])
        gates_src = sb("gates_src", [P, E0 + E1])
        gates_hi = sb("gates_hi", [P, E0 + E1], F32R)
        gates_lo = sb("gates_lo", [P, E0 + E1], F32R)
        gate_bias = sb("gate_bias", [P, E1])
        lower_first = sb("lower_first", [P, NG, NG])
        lo_rows = sb("lo_rows", [P, 2])
        stats = sb("stats", [P, B, T, 6])
        mv = sb("mv", [P, B, T, 2])
        vareps = sb("vareps", [P, B, T])
        rstd = sb("rstd", [P, B, T])
        minus_half = sb("minus_half", [P, T])
        neg_max0 = sb("neg_max0", [P, B, T, H0])
        row_sum = sb("row_sum", [P, B, T, H0])
        row_inv = sb("row_inv", [P, B, T, H0])
        neg_max1 = sb("neg_max1", [P, B, T, 4, G1])
        den_inv = sb("den_inv", [P, 2, T, 4])
        e_neg = sb("e_neg", [P, T, E0])
        sc = sb("sc", [P, T, E0])
        pair_max = sb("pair_max", [P, T * NG, 2])
        pair_sum = sb("pair_sum", [P, T * NG, 2])
        g_score = sb("g_score", [P, T, NG])
        g_cross = sb("g_cross", [P, T, NG])
        beats = sb("beats", [P, T * NG, NG])
        ties = sb("ties", [P, T * NG, NG])
        rank = sb("rank", [P, T, NG])
        allowed = sb("allowed", [P, T, NG])
        penalty = sb("penalty", [P, T, NG])
        cand = sb("cand", [P, T, E0 + 8])
        replaced = sb("replaced", [P, T, E0 + 8])
        top = sb("top", [P, T, 8])
        chosen = sb("chosen", [P, T, E0])
        diff = sb("diff", [P, T, E1])
        e_diff = sb("e_diff", [P, T, E1])
        w_un = sb("w_un", [P, T, E0])
        w_sum = sb("w_sum", [P, T])
        w_inv = sb("w_inv", [P, T])
        cw = sb("cw", [P, B, T, E0])
        cwT_sb = sb("cwT_sb", [E0, B, TOK])

        with ExitStack() as r:
            w13_hi0 = sb("w13_hi0", [P, 2 * N_HID[1], P], F32R, r)
            w13_lo0 = sb("w13_lo0", [P, 2 * N_HID[1], P], F32R, r)
            w2_0 = sb("w2_0", [P, N_HID[1], P], F32, r)
            with ExitStack() as r2:
                wk0 = sb("wk0", [CD, H0 * DH0], F32, r2)
                wv0 = sb("wv0", [CD, H0 * DH0], F32, r2)
                wo0 = sb("wo0", [P, PAIRS, P], F32, r2)
                q_hi = sb("q_hi", [P, B, PAIRS, TOK], F32R, r2)
                q_lo = sb("q_lo", [P, B, PAIRS, TOK], F32R, r2)
                k_hi = sb("k_hi", [P, PAIRS, B, 2, CP], F32R, r2)
                k_lo = sb("k_lo", [P, PAIRS, B, 2, CP], F32R, r2)
                v0 = sb("v0", [P, B, H0 * DH0], F32, r2)
                vs0 = sb("vs0", [P, B, PAIRS, P], F32, r2)
                prob = sb("prob", [P, 2, H0, CTX], F32, r2)
                prob_n = sb("prob_n", [P, 2, H0 * CP], F32, r2)
                probT0 = sb("probT0", [P, H0 + 2, TOK], F32, r2)
                with ExitStack() as r3:
                    wq_src0 = sb("wq_src0", [P, H0 * DH0], F32, r3)
                    wq_hi0 = sb("wq_hi0", [P, H0 * DH0], F32R, r3)
                    wq_lo0 = sb("wq_lo0", [P, H0 * DH0], F32R, r3)
                outT0 = sb("outT0", [P, PAIRS, TOK], F32, r2)
            with ExitStack() as r2:
                w13_hi1 = sb("w13_hi1", [P, 2 * N_HID[3], P], F32R, r2)
                w13_lo1 = sb("w13_lo1", [P, 2 * N_HID[3], P], F32R, r2)
                w2_1 = sb("w2_1", [P, N_HID[3], P], F32, r2)
                wq_hi1 = sb("wq_hi1", [P, G1 * P], F32R, r2)
                wq_lo1 = sb("wq_lo1", [P, G1 * P], F32R, r2)
                wk1 = sb("wk1", [CD + 1, G1, P], F32, r2)
                wv1 = sb("wv1", [CD + 1, G1 * P], F32, r2)
                wo1 = sb("wo1", [P, P], F32, r2)
                k1 = sb("k1", [P, B, G1, 4, CTX], F32R, r2)
                k1s = sb("k1s", [P, B, G1, 4, PAD], F32R, r2)
                q1 = sb("q1", [P, B, G1, TOK], F32R, r2)
                rounded = sb("rounded", [P, 2, TOK], F32R, r2)
                v1 = sb("v1", [P, B, G1 * P], F32, r2)
                vs1 = sb("vs1", [P, B, G1, P], F32, r2)
                nmT_hi = sb("nmT_hi", [H1, TOK], F32R, r2)
                nmT_lo = sb("nmT_lo", [H1, TOK], F32R, r2)
                with ExitStack() as r3:
                    wq_src1 = sb("wq_src1", [P, G1 * P], F32, r3)
                od = sb("od", [P, 2, TOK], F32, r2)
                on = sb("on", [P, T, P], F32, r2)
        with ExitStack() as r:
            probT1 = sb("probT1", [P, 2, 5, TOK], F32, r)
            onT = sb("onT", [P, TOK], F32, r)

        cw_dram = {(s, b): nc.dram_tensor(f"cw_{s}_{b}", (EXPERTS[s], TOK), F32).ap() for s in (1, 3) for b in range(B)}

        bank_ready = [sem(f"bank_ready{k}") for k in range(8)]
        bank_read = [sem(f"bank_read{k}") for k in range(8)]
        loaded = {n: sem(f"loaded_{n}") for n in (
            "x0", "x1", "const", "ctx", "ctxv", "wq0", "w13_0", "w2_0", "wo0", "wqkv1", "w13_1", "w2_1")}
        hi_of = {n: sem(f"hi_{n}") for n in ("wq0", "gates", "w13_0", "wq1", "w13_1")}
        lo_of = {n: sem(f"lo_{n}") for n in ("wq0", "gates", "w13_0", "wq1", "w13_1")}
        cleared0 = sem("cleared0")
        cleared1 = sem("cleared1")
        var_ready = sem("var_ready")
        rstd_ready = sem("rstd_ready")
        xn_ready = sem("xn_ready")
        xT_rounded = sem("xT_rounded")
        bo_added = sem("bo_added")
        kT_rounded = sem("kT_rounded")
        q_rounded = sem("q_rounded")
        negmax_ready = sem("negmax_ready")
        rowinv_ready = sem("rowinv_ready")
        prob_normed = sem("prob_normed")
        diff_ready = sem("diff_ready")
        e_diff_ready = sem("e_diff_ready")
        cw_ready = sem("cw_ready")
        cw_stored = sem("cw_stored")
        spread_loaded = [sem(f"spread_loaded{c}") for c in range(SLOTS // 2)]
        hid_ready = sem("hid_ready")
        hid_used = sem("hid_used")
        k1_rounded = sem("k1_rounded")
        q1_rounded = sem("q1_rounded")
        nm_rounded = sem("nm_rounded")
        nm_placed = [sem(f"nm_placed{b}") for b in range(B)]
        out_stored = sem("out_stored")
        dve_step = sem("dve_step")
        pool_step = sem("pool_step")

        def bank(key):
            return psum[:, uses[key][0], :]

        def wait_filled(eng, key):
            k, n = uses[key]
            eng.wait_ge(bank_ready[k], n)

        def wait_moved(eng, key):
            k, n = uses[key]
            eng.wait_ge(bank_read[k], n)

        def wait_bank_free(eng, key):
            k, n = uses[key]
            if n > 1:
                eng.wait_ge(bank_read[k], n - 1)

        def filled(ins, key):
            ins.then_inc(bank_ready[uses[key][0]], 1)

        def moved(ins, key):
            ins.then_inc(bank_read[uses[key][0]], 1)

        HEAD_SCALE0 = float(DH0) ** -0.5
        HEAD_SCALE1 = float(DH1) ** -0.5
        splits = {"wq0": (wq_src0, wq_hi0, wq_lo0), "gates": (gates_src, gates_hi, gates_lo), "wq1": (wq_src1, wq_hi1, wq_lo1)}
        w13 = {1: (w13_hi0, w13_lo0, w2_0, "w13_0"), 3: (w13_hi1, w13_lo1, w2_1, "w13_1")}
        n_src = 2 * N_HID[1] // CHUNK

        def split_aps(name, c):
            if name in splits:
                s, h, l = splits[name]
                return s[:, :], h[:, :], l[:, :]
            h, l = w13[1 if name == "w13_0" else 3][:2]
            at = slice(c * CHUNK, (c + 1) * CHUNK)
            cs = c % n_src
            return w_src[:, cs * CHUNK:(cs + 1) * CHUNK, :], h[:, at, :], l[:, at, :]

        def wait_split_source(eng, name, c):
            if name == "w13_1":
                eng.wait_ge(loaded[name], 16 * (c // n_src + 1))
            else:
                eng.wait_ge(loaded[{"gates": "const", "wq1": "wqkv1"}.get(name, name)],
                            {"gates": 16 * N_CONST, "wq1": 16 * 4}.get(name, 16))

        N_CONST = 6
        hid_index = {}
        for step in order:
            if step[0] == "hid":
                hid_index[step[1:]] = len(hid_index)
        tiles = list(hid_index)

        def wait_hid_used(eng, n):
            s, b, i = tiles[n]
            if i == N_HID[s] - 1:
                wait_filled(eng, ("y", s, b))
            else:
                eng.wait_ge(hid_used, sum(t[2] < N_HID[t[0]] - 1 for t in tiles[:n + 1]))

        def slot_of(s, i):
            e = i - N_SHARED[s]
            return e if s == 1 else e // 2

        def spread_count(s, b):
            return 16 * (2 * (b + 1) if s == 1 else 2 * B + b + 1)

        block = ctx.enter_context(nc.Block())

        @block.sync
        def _(sp):
            def load(dst, src, name):
                sp.dma_start(dst, src).then_inc(loaded[name], 16)

            load(X[:, 0:T, :], a["x"][:, 0:T, :], "x0")
            load(ctxT[:, :, :], a["ctxT"], "ctx")
            load(wk0[:, :], a["wk0"], "ctx")
            load(wq_src0[:, :], a["wq0"], "wq0")
            load(X[:, T:2 * T, :], a["x"][:, T:2 * T, :], "x1")
            for dst, name in ((ident[:, :], "ident"), (bo[:, :], "bo"), (gates_src[:, :], "gates"),
                              (gate_bias[:, :], "gate_bias"), (lower_first[:, :, :], "lower_first"),
                              (lo_rows[:, :], "lo_rows")):
                load(dst, a[name], "const")
            load(ctxT_rest[:, :, :], a["ctxT_rest"], "ctxv")
            load(wv0[:, :], a["wv0"], "ctxv")
            load(wo0[:, :, :], a["wo0"], "wo0")
            load(w_src[:, :, :], a["w13_0"], "w13_0")
            load(w2_0[:, :, :], a["w2_0"], "w2_0")

            def spread_weights(s, b):
                wait_moved(sp, ("cwT", s, b))
                sp.dma_start(cw_dram[s, b], cwT_sb[0:EXPERTS[s], b, :]).then_inc(cw_stored, 16)
                sp.wait_ge(cw_stored, 16 * position[("cwT", s, b)])
                for c in range(SLOTS // 2):
                    last = {(1, 0): None, (1, 1): (1, 0, 2 * c + 2), (3, 0): (1, 1, 2 * c + 2),
                            (3, 1): (3, 0, 2 + 4 * c + 3)}[s, b]
                    if last is not None:
                        wait_moved(sp, ("hid3",) + last)
                    for half in range(2 if s == 1 else 1):
                        if s == 1:
                            rows = cw_dram[s, b].rearrange("(i two) n -> two i n", two=2)[half, 2 * c:2 * c + 2, :]
                            dst = spread[64 * half:64 * half + 64, 2 * c:2 * c + 2, :]
                            src = rows.unsqueeze(0).broadcast_to((64, 2, TOK))
                        else:
                            rows = cw_dram[s, b][2 * c:2 * c + 2, :]
                            dst = spread[:, 2 * c:2 * c + 2, :]
                            src = rows.unsqueeze(0).broadcast_to((P, 2, TOK))
                        sp.dma_start(dst, src).then_inc(spread_loaded[c], 16)

            for step in order:
                if step == ("wo", 1):
                    wait_filled(sp, ("wo", 1))
                    load(wq_src1[:, :], a["wq1"], "wqkv1")
                    load(wk1[:, :, :], a["wk1"], "wqkv1")
                    load(wv1[:, :], a["wv1"], "wqkv1")
                    load(wo1[:, :], a["wo1"], "wqkv1")
                    sp.wait_ge(lo_of["w13_0"], n_src)
                    load(w_src[:, :, :], a["w13_1"][:, 0:2 * N_HID[1], :], "w13_1")
                    load(w2_1[:, :, :], a["w2_1"], "w2_1")
                if step == ("split", "w13_1", n_src - 1):
                    sp.wait_ge(lo_of["w13_1"], n_src)
                    load(w_src[:, :, :], a["w13_1"][:, 2 * N_HID[1]:, :], "w13_1")
                if step[0] == "cwT":
                    spread_weights(*step[1:])
                if step[0] == "mT":
                    b = step[1]
                    wait_moved(sp, step)
                    for part, rows in ((0, nmT_hi), (1, nmT_lo)):
                        for j in range(4):
                            r = PAD * j + 3 * DH1 + part
                            sp.dma_start(q1[r:r + 1, b, :, :].bitcast(F32), rows[G1 * j:G1 * (j + 1), :].bitcast(F32)).then_inc(nm_placed[b], 16)
                if step[0] == "res" and step[1] == 3:
                    b = step[2]
                    wait_moved(sp, ("y", 3, b))
                    sp.dma_start(out[:, b * T:(b + 1) * T, :], X[:, b * T:(b + 1) * T, :]).then_inc(out_stored, 16)
            sp.wait_ge(out_stored, 16 * B)

        @block.gpsimd
        def _(pool):
            steps = [0]

            def chain(ins):
                ins.then_inc(pool_step, 1)
                steps[0] += 1
                pool.wait_ge(pool_step, steps[0])

            pool.memset(minus_half[:, :], -0.5).then_inc(cleared0, 1)
            pool.memset(k_hi[:, :, :, :, :].bitcast(F32), 0.0).then_inc(cleared0, 1)
            pool.memset(k_lo[:, :, :, :, :].bitcast(F32), 0.0).then_inc(cleared0, 1)
            rest = prob_n[:, :, H0 * P:].rearrange("p r (h c) -> p r h c", h=H0)
            pool.memset(rest[:, :, :, REST:PAD], 0.0).then_inc(cleared0, 1)
            pool.memset(vs0[:, :, :, :], 0.0).then_inc(cleared0, 1)

            for step in order:
                kind = step[0]
                if kind == "split":
                    name, c = step[1:]
                    src, hi, lo = split_aps(name, c)
                    pool.wait_ge(hi_of[name], c + 1)
                    pool.tensor_tensor(lo, src, hi.bitcast(F32), ALU.subtract).then_inc(lo_of[name], 1)
                elif kind == "lnA":
                    b = step[2]
                    pool.wait_ge(cleared0, 1)
                    pool.wait_ge(var_ready, position[step])
                    pool.tensor_tensor(rstd[:, b, :], vareps[:, b, :], minus_half[:, :], ALU.pow).then_inc(rstd_ready, 1)
                elif kind == "bo":
                    b = step[1]
                    pool.wait_ge(loaded["const"], 16 * N_CONST)
                    pool.wait_ge(xn_ready, position[("lnB", 0, b)])
                    xb = X[:, b * T:(b + 1) * T, :]
                    pool.tensor_tensor(xb, xb, bo[:, :].unsqueeze(1).broadcast_to((P, T, P)), ALU.add).then_inc(bo_added, 1)
                elif kind == "norm":
                    b, t = step[1:]
                    r = (b * T + t) % 2
                    pool.wait_ge(rowinv_ready, position[step])
                    pool.wait_ge(cleared0, 4)
                    if b * T + t >= 2:
                        wait_filled(pool, ("pT", (b * T + t - 2) // T, (b * T + t - 2) % T, 2))
                    for dst, cols in ((prob_n[:, r, 0:H0 * P].rearrange("p (h c) -> p h c", h=H0), slice(0, P)),
                                      (rest[:, r, :, 0:REST], slice(P, CTX))):
                        w = cols.stop - cols.start
                        ins = pool.tensor_tensor(dst, prob[:, r, :, cols],
                                                 row_inv[:, b, t, :].unsqueeze(2).broadcast_to((P, H0, w)), ALU.mult)
                    ins.then_inc(prob_normed, 1)
                elif kind == "clear1":
                    wait_filled(pool, ("wo", 1))
                    pool.memset(k1[:, :, :, :, :].bitcast(F32), 0.0).then_inc(cleared1, 1)
                    pool.memset(vs1[:, :, :, :], 0.0).then_inc(cleared1, 1)
                    pool.memset(k1s[:, :, :, :, :].bitcast(F32), 0.0).then_inc(cleared1, 1)
                elif kind == "hid":
                    n = hid_index[step[1:]]
                    wait_moved(pool, ("hid1",) + step[1:])
                    wait_moved(pool, ("hid3",) + step[1:])
                    if n >= 3:
                        wait_hid_used(pool, n - 3)
                    pool.tensor_tensor(hid[:, n % 3, :], act_s[:, n % 2, :], gated_u[:, n % 2, :], ALU.mult)\
                        .then_inc(hid_ready, 1)

        @block.scalar
        def _(act):
            for step in order:
                kind = step[0]
                if kind == "split":
                    name, c = step[1:]
                    src, hi, lo = split_aps(name, c)
                    wait_split_source(act, name, c)
                    act.copy(hi, src).then_inc(hi_of[name], 1)
                elif kind == "xT":
                    b = step[2]
                    wait_filled(act, step)
                    act.copy(xT_hi[:, b, :], bank(step)).then_inc(xT_rounded, 1)
                elif kind == "kT":
                    p = step[1]
                    wait_filled(act, step)
                    act.wait_ge(cleared0, 2)
                    for j in range(2):
                        rows = slice(64 * j, 64 * j + 64)
                        act.copy(k_hi[rows, p, :, j, :], bank(step)[rows, 0:B * CP].rearrange("p (b c) -> p b c", b=B))\
                            .then_inc(kT_rounded, 1)
                elif kind == "q":
                    b, p = step[1:]
                    wait_filled(act, step)
                    act.mul(q_hi[:, b, p, :], bank(step), HEAD_SCALE0).then_inc(q_rounded, 1)
                elif kind == "score":
                    b, t, p = step[1:]
                    r = (b * T + t) % 2
                    act.wait_ge(negmax_ready, position[step])
                    if b * T + t >= 2 and p == 0:
                        act.wait_ge(prob_normed, b * T + t - 1)
                    for j in range(2):
                        h = 2 * p + j
                        ins = act.activation(prob[:, r, h, 0:CTX], bank(step)[:, j * CTX:(j + 1) * CTX], ACT.Exp,
                                             bias=neg_max0[:, b, t, h:h + 1], accum_out=row_sum[:, b, t, h:h + 1])
                    moved(ins, step)
                elif kind == "pT" and step[3] == 2:
                    b, t = step[1:3]
                    wait_filled(act, step)
                    if b == 1 and t == 0:
                        wait_filled(act, ("pv", 0, PAIRS - 1))
                    moved(act.copy(probT0[:, H0:H0 + 2, t * P:(t + 1) * P],
                                   bank(step)[:, 0:2 * P].rearrange("p (g n) -> p g n", g=2)), step)
                elif kind == "pv":
                    b, p = step[1:]
                    wait_filled(act, step)
                    if b == 1:
                        wait_filled(act, ("wo", 0))
                    moved(act.copy(outT0[:, p, :], bank(step)), step)
                elif kind == "gate" and step[1] == 1:
                    wait_filled(act, step)
                    if step[2] > 0:
                        act.wait_ge(cw_ready, 1)
                    moved(act.activation(e_neg[:, :, :], bank(step)[:, 0:T * E0].rearrange("p (t e) -> p t e", t=T),
                                         ACT.Exp, scale=-1.0), step)
                elif kind == "route" and step[1] == 3:
                    b = step[2]
                    act.wait_ge(diff_ready, b + 1)
                    act.activation(e_diff[:, :, :], diff[:, :, :], ACT.Exp).then_inc(e_diff_ready, 1)
                elif kind == "cwT":
                    s, b = step[1:]
                    wait_filled(act, step)
                    if s == 3:
                        act.wait_ge(cw_stored, 16 * position[("cwT", 1, b)])
                    moved(act.copy(cwT_sb[0:EXPERTS[s], b, :], bank(step)[0:EXPERTS[s], :]), step)
                elif kind == "hid":
                    n = hid_index[step[1:]]
                    key = ("hid1",) + step[1:]
                    wait_filled(act, key)
                    if n >= 2:
                        act.wait_ge(hid_ready, n - 1)
                    moved(act.activation(act_s[:, n % 2, :], bank(key), ACT.Silu), key)
                elif kind == "k1":
                    g = step[1]
                    wait_filled(act, step)
                    if g >= 2:
                        wait_moved(act, ("k1", g - 2))
                    act.copy(rounded[:, g % 2, 0:B * CP], bank(step)[:, 0:B * CP]).then_inc(k1_rounded, 1)
                elif kind == "q1":
                    b, g = step[1:]
                    wait_filled(act, step)
                    if (b, g) == (0, 0):
                        wait_moved(act, ("k1", G1 - 2))
                        wait_moved(act, ("k1", G1 - 1))
                    if g >= 2:
                        wait_moved(act, ("q1", b, g - 2))
                    elif b == 1:
                        wait_moved(act, ("q1", 0, g + 2))
                    act.copy(rounded[:, g % 2, :], bank(step)).then_inc(q1_rounded, 1)
                elif kind == "mT":
                    b = step[1]
                    wait_filled(act, step)
                    if b == 1:
                        act.wait_ge(nm_placed[0], 16 * 8)
                    act.copy(nmT_hi[:, :], bank(step)[0:H1, :]).then_inc(nm_rounded, 1)
                elif kind == "expT":
                    b, g, j = step[1:]
                    wait_filled(act, step)
                    n = b * G1 + g
                    if n >= 2:
                        wait_filled(act, ("pv1", (n - 2) // G1, (n - 2) % G1))
                    else:
                        wait_filled(act, ("y", 1, 1))
                    moved(act.activation(probT1[:, n % 2, j, :], bank(step), ACT.Exp, scale=HEAD_SCALE1), step)
                elif kind == "onT":
                    b = step[1]
                    wait_filled(act, step)
                    if b == 1:
                        wait_filled(act, ("wo1", 0))
                    moved(act.copy(onT[:, :], bank(step)), step)

        @block.vector
        def _(dve):
            steps = [0]

            def chain(ins):
                ins.then_inc(dve_step, 1)
                steps[0] += 1
                dve.wait_ge(dve_step, steps[0])

            def note(ins):
                ins.then_inc(dve_step, 1)
                steps[0] += 1

            def settle():
                dve.wait_ge(dve_step, steps[0])

            for step in order:
                kind = step[0]
                if kind == "lnA":
                    s, b = step[1:]
                    if s == 0:
                        dve.wait_ge(loaded[f"x{b}"], 16)
                    settle()
                    for t in range(T):
                        note(dve.bn_stats(stats[:, b, t, :], X[:, b * T + t, :]))
                    settle()
                    for t in range(T):
                        note(dve.bn_aggr(mv[:, b, t, :], stats[:, b, t, :]))
                    settle()
                    dve.tensor_scalar(vareps[:, b, :], mv[:, b, :, 1], EPS, None, ALU.add).then_inc(var_ready, 1)
                elif kind == "lnB":
                    s, b = step[1:]
                    dve.wait_ge(rstd_ready, position[("lnA", s, b)])
                    for t in range(T):
                        ins = dve.tensor_scalar(xn[:, b, t, :], X[:, b * T + t, :], mv[:, b, t, 0:1], rstd[:, b, t:t + 1],
                                                ALU.subtract, ALU.mult)
                    ins.then_inc(xn_ready, 1)
                elif kind == "xT":
                    b = step[2]
                    dve.wait_ge(xT_rounded, position[step])
                    moved(dve.tensor_tensor(xT_lo[:, b, :], bank(step), xT_hi[:, b, :].bitcast(F32), ALU.subtract), step)
                elif kind == "kT":
                    p = step[1]
                    dve.wait_ge(cleared0, 3)
                    for j in range(2):
                        dve.wait_ge(kT_rounded, 2 * p + j + 1)
                        rows = slice(64 * j, 64 * j + 64)
                        ins = dve.tensor_tensor(
                            k_lo[rows, p, :, j, :], bank(step)[rows, 0:B * CP].rearrange("p (b c) -> p b c", b=B),
                            k_hi[rows, p, :, j, :].bitcast(F32), ALU.subtract)
                    moved(ins, step)
                elif kind == "q":
                    b, p = step[1:]
                    dve.wait_ge(q_rounded, position[step])
                    moved(dve.scalar_tensor_tensor(q_lo[:, b, p, :], bank(step), HEAD_SCALE0,
                                                   q_hi[:, b, p, :].bitcast(F32), ALU.mult, ALU.subtract), step)
                elif kind in ("vf", "vf1"):
                    b = step[1]
                    wait_filled(dve, step)
                    moved(dve.tensor_copy((v0 if kind == "vf" else v1)[:, b, :], bank(step)), step)
                elif kind == "vs":
                    b = step[1]
                    wait_filled(dve, step)
                    dve.wait_ge(cleared0, 5)
                    src = bank(step).rearrange("p (q c) -> p q c", q=PAIRS)
                    for j in range(4):
                        rows, cols = slice(PAD * j, PAD * j + REST), slice(64 * (j % 2), 64 * (j % 2) + 64)
                        ins = dve.tensor_copy(vs0[rows, b, j // 2::2, cols], src[rows, j // 2::2, cols])
                    moved(ins, step)
                elif kind == "vs1":
                    b = step[1]
                    wait_filled(dve, step)
                    dve.wait_ge(cleared1, 2)
                    src = bank(step).rearrange("p (g c) -> p g c", g=G1)
                    for j in range(4):
                        rows, cols = slice(PAD * j, PAD * j + REST), slice(PAD * j, PAD * j + PAD)
                        ins = dve.tensor_copy(vs1[rows, b, :, cols], src[rows, :, cols])
                    moved(ins, step)
                elif kind == "score":
                    b, t, p = step[1:]
                    wait_filled(dve, step)
                    dve.tensor_reduce(neg_max0[:, b, t, 2 * p:2 * p + 2],
                                      bank(step)[:, 0:2 * CTX].rearrange("p (j c) -> p j c", j=2), AX, ALU.max, negate=True)\
                        .then_inc(negmax_ready, 1)
                elif kind == "norm":
                    b, t = step[1:]
                    for p in range(PAIRS):
                        wait_moved(dve, ("score", b, t, p))
                    dve.reciprocal(row_inv[:, b, t, :], row_sum[:, b, t, :]).then_inc(rowinv_ready, 1)
                elif kind == "pT" and step[3] < 2:
                    b, t, k = step[1:]
                    wait_filled(dve, step)
                    if b == 1 and t == 0:
                        wait_filled(dve, ("pv", 0, PAIRS - 1))
                    moved(dve.tensor_copy(probT0[:, 4 * k:4 * k + 4, t * P:(t + 1) * P],
                                          bank(step).rearrange("p (h n) -> p h n", h=4)), step)
                elif kind in ("wo", "wo1", "res"):
                    b = step[-1]
                    key = ("y",) + step[1:] if kind == "res" else step
                    wait_filled(dve, key)
                    if kind == "wo":
                        dve.wait_ge(bo_added, position[("bo", b)])
                    xb = X[:, b * T:(b + 1) * T, :]
                    settle()
                    moved(dve.tensor_tensor(xb, bank(key).rearrange("p (t d) -> p t d", t=T), xb, ALU.add), key)
                    wait_moved(dve, key)
                elif kind == "gate" and step[1] == 3:
                    b = step[2]
                    wait_filled(dve, step)
                    dve.wait_ge(loaded["const"], 16 * N_CONST)
                    settle()
                    moved(dve.tensor_tensor(cand[:, :, 0:E1], bank(step)[:, 0:T * E1].rearrange("p (t e) -> p t e", t=T),
                                            gate_bias[:, :].unsqueeze(1).broadcast_to((P, T, E1)), ALU.add), step)
                    wait_moved(dve, step)
                elif kind == "route":
                    s, b = step[1:]
                    if s == 1:
                        wait_moved(dve, ("gate", s, b))
                        dve.wait_ge(loaded["const"], 16 * N_CONST)
                        chain(dve.tensor_scalar(e_neg[:, :, :], e_neg[:, :, :], 1.0, None, ALU.add))
                        chain(dve.reciprocal(sc[:, :, :], e_neg[:, :, :]))
                        quad = sc[:, :, :].rearrange("p t (g h w) -> p (t g) h w", g=NG, w=2)
                        note(dve.tensor_tensor(pair_max[:, :, :], quad[:, :, :, 0], quad[:, :, :, 1], ALU.max))
                        note(dve.tensor_tensor(pair_sum[:, :, :], quad[:, :, :, 0], quad[:, :, :, 1], ALU.add))
                        settle()
                        gs = g_score[:, :, :].rearrange("p t g -> p (t g)")
                        gc = g_cross[:, :, :].rearrange("p t g -> p (t g)")
                        note(dve.tensor_tensor(gc, pair_max[:, :, 0], pair_max[:, :, 1], ALU.add))
                        note(dve.tensor_tensor(gs, pair_sum[:, :, 0], pair_sum[:, :, 1], ALU.max))
                        settle()
                        chain(dve.tensor_tensor(gs, gs, gc, ALU.max))
                        own = g_score[:, :, :].unsqueeze(3).broadcast_to((P, T, NG, NG))
                        other = g_score[:, :, :].unsqueeze(2).broadcast_to((P, T, NG, NG))
                        bt = beats[:, :, :].rearrange("p (t g) h -> p t g h", t=T)
                        ti = ties[:, :, :].rearrange("p (t g) h -> p t g h", t=T)
                        first = lower_first[:, :, :].unsqueeze(1).broadcast_to((P, T, NG, NG))
                        note(dve.tensor_tensor(bt, other, own, ALU.is_gt))
                        note(dve.tensor_tensor(ti, other, own, ALU.is_equal))
                        settle()
                        chain(dve.tensor_tensor(ti, ti, first, ALU.mult))
                        chain(dve.tensor_tensor(beats[:, :, :], beats[:, :, :], ties[:, :, :], ALU.add))
                        chain(dve.tensor_reduce(rank[:, :, :].rearrange("p t g -> p (t g)"), beats[:, :, :], AX, ALU.add))
                        chain(dve.tensor_scalar(allowed[:, :, :], rank[:, :, :], 2.0, None, ALU.is_lt))
                        note(dve.tensor_scalar(penalty[:, :, :], allowed[:, :, :], -1.0, None, ALU.add))
                        wide = lambda x: x[:, :, :].unsqueeze(3).broadcast_to((P, T, NG, E0 // NG))
                        cg = cand[:, :, 0:E0].rearrange("p t (g e) -> p t g e", g=NG)
                        chain(dve.tensor_tensor(cg, sc[:, :, :].rearrange("p t (g e) -> p t g e", g=NG), wide(allowed), ALU.mult))
                        note(dve.tensor_tensor(cg, cg, wide(penalty), ALU.add))
                        n_e, topk, sentinel, gone = E0, TOPK0, -2.0, -3.0
                    else:
                        n_e, topk, sentinel, gone = E1, TOPK1, -3.0e38, -3.2e38
                    note(dve.memset(cand[:, :, n_e:n_e + 8], sentinel))
                    settle()
                    for t in range(T):
                        note(dve.max(top[:, t, :], cand[:, t, 0:n_e]))
                    settle()
                    if s == 3:
                        dve.tensor_tensor(diff[:, :, :], cand[:, :, 0:E1], top[:, :, 0:1].broadcast_to((P, T, E1)), ALU.subtract)\
                            .then_inc(diff_ready, 1)
                    note(dve.memset(top[:, :, topk:8], sentinel))
                    settle()
                    for t in range(T):
                        note(dve.match_replace(replaced[:, t, 0:n_e + 8], top[:, t, :], cand[:, t, 0:n_e + 8], gone))
                    settle()
                    chain(dve.tensor_tensor(chosen[:, :, 0:n_e], replaced[:, :, 0:n_e], cand[:, :, 0:n_e], ALU.not_equal))
                    if s == 3:
                        dve.wait_ge(e_diff_ready, b + 1)
                    weight = sc[:, :, :] if s == 1 else e_diff[:, :, :]
                    chain(dve.tensor_tensor(w_un[:, :, 0:n_e], weight, chosen[:, :, 0:n_e], ALU.mult))
                    chain(dve.tensor_reduce(w_sum[:, :], w_un[:, :, 0:n_e], AX, ALU.add))
                    if s == 1:
                        chain(dve.tensor_scalar(w_sum[:, :], w_sum[:, :], 1e-6, None, ALU.add))
                    chain(dve.reciprocal(w_inv[:, :], w_sum[:, :]))
                    dve.tensor_tensor(cw[:, b, :, 0:n_e], w_un[:, :, 0:n_e],
                                      w_inv[:, :].unsqueeze(2).broadcast_to((P, T, n_e)), ALU.mult).then_inc(cw_ready, 1)
                    dve.wait_ge(cw_ready, position[step])
                elif kind == "hid":
                    s, b, i = step[1:]
                    n = hid_index[step[1:]]
                    key = ("hid3", s, b, i)
                    if n >= 2:
                        dve.wait_ge(hid_ready, n - 1)
                    wait_filled(dve, key)
                    if i < N_SHARED[s]:
                        ins = dve.tensor_copy(gated_u[:, n % 2, :], bank(key))
                    else:
                        slot = slot_of(s, i)
                        dve.wait_ge(spread_loaded[slot // 2], spread_count(s, b))
                        ins = dve.tensor_tensor(gated_u[:, n % 2, :], bank(key), spread[:, slot, :], ALU.mult)
                    moved(ins, key)
                elif kind == "k1":
                    g = step[1]
                    dve.wait_ge(k1_rounded, g + 1)
                    dve.wait_ge(cleared1, 3)
                    for j in range(4):
                        rows = slice(PAD * j, PAD * j + PAD)
                        hi = rounded[rows, g % 2, 0:B * CP].bitcast(F32).rearrange("p (b c) -> p b c", b=B)
                        k = bank(step)[rows, 0:B * CP].rearrange("p (b c) -> p b c", b=B)
                        for dst, cols in ((k1, slice(0, CTX)), (k1s, slice(P, CP))):
                            ins = dve.scalar_tensor_tensor(dst[rows, :, g, j, :], hi[:, :, cols], lo_rows[rows, 1:2],
                                                           k[:, :, cols], ALU.mult, ALU.add)
                    moved(ins, step)
                elif kind == "q1":
                    b, g = step[1:]
                    dve.wait_ge(q1_rounded, position[step])
                    moved(dve.scalar_tensor_tensor(q1[:, b, g, :], rounded[:, g % 2, :].bitcast(F32), lo_rows[:, 0:1],
                                                   bank(step), ALU.mult, ALU.add), step)
                elif kind == "score1":
                    b, t, g, half = step[1:]
                    wait_filled(dve, step)
                    moved(dve.tensor_reduce(neg_max1[:, b, t, 2 * half:2 * half + 2, g],
                                            bank(step)[:, 0:2 * CTX].rearrange("p (j c) -> p j c", j=2), AX, ALU.max, negate=True),
                          step)
                elif kind == "mT":
                    b = step[1]
                    dve.wait_ge(nm_rounded, b + 1)
                    moved(dve.tensor_tensor(nmT_lo[:, :], bank(step)[0:H1, :], nmT_hi[:, :].bitcast(F32), ALU.subtract), step)
                elif kind == "pv1":
                    b, g = step[1:]
                    wait_filled(dve, step)
                    if b * G1 + g >= 2:
                        n = b * G1 + g - 2
                        wait_filled(dve, ("oT", n // G1, n % G1))
                    moved(dve.tensor_copy(od[:, g % 2, :], bank(step)), step)
                elif kind == "oT":
                    b, g = step[1:]
                    wait_filled(dve, step)
                    if b == 1 and g == 0:
                        wait_filled(dve, ("onT", 0))
                    v = bank(step).rearrange("p (t j c) -> p t j c", t=T, j=4)
                    settle()
                    chain(dve.reciprocal(den_inv[:, g % 2, :, :], v[:, :, :, DH1]))
                    moved(dve.tensor_tensor(on[:, :, g * 32:(g + 1) * 32].rearrange("p t (j c) -> p t j c", j=4),
                                            v[:, :, :, 0:DH1],
                                            den_inv[:, g % 2, :, :].unsqueeze(3).broadcast_to((P, T, 4, DH1)), ALU.mult), step)

        @block.tensor
        def _(pe):
            def product3(dst, w_hi, w_lo, m_hi, m_lo):
                pe.matmul(dst, w_hi, m_hi, start=True, stop=False)
                pe.matmul(dst, w_hi, m_lo, start=False, stop=False)
                return pe.matmul(dst, w_lo, m_hi, start=False, stop=True)

            for step in order:
                kind = step[0]
                if kind in RING:
                    wait_bank_free(pe, step)
                if kind == "kT":
                    p = step[1]
                    pe.wait_ge(loaded["ctx"], 32)
                    filled(pe.matmul(bank(step)[:, 0:B * CP], wk0[:, p * P:(p + 1) * P],
                                     ctxT[0:CD, :, :].rearrange("k b c -> k (b c)"), start=True, stop=True), step)
                elif kind in ("vf", "vf1", "vs", "vs1"):
                    b = step[1]
                    if kind in ("vf", "vs"):
                        pe.wait_ge(loaded["ctx"], 32)
                        pe.wait_ge(loaded["ctxv"], 32)
                        w, k = wv0[:, :], CD
                    else:
                        pe.wait_ge(loaded["wqkv1"], 64)
                        w, k = wv1[:, :], CD + 1
                    rows = ctxT[0:k, b, 0:P] if kind in ("vf", "vf1") else ctxT_rest[0:k, b, :]
                    filled(pe.matmul(bank(step), rows, w, start=True, stop=True), step)
                elif kind == "xT":
                    s, b = step[1:]
                    pe.wait_ge(loaded["const"], 16 * N_CONST)
                    pe.wait_ge(xn_ready, position[step])
                    for t in range(T):
                        ins = pe.transpose(bank(step)[:, t * P:(t + 1) * P], xn[:, b, t, :], ident[:, :])
                    filled(ins, step)
                elif kind == "q":
                    b, p = step[1:]
                    pe.wait_ge(lo_of["wq0"], 1)
                    wait_moved(pe, ("xT", 0, b))
                    c = slice(p * P, (p + 1) * P)
                    filled(product3(bank(step), wq_hi0[:, c], wq_lo0[:, c], xT_hi[:, b, :], xT_lo[:, b, :]), step)
                elif kind == "score":
                    b, t, p = step[1:]
                    wait_moved(pe, ("q", b, p))
                    wait_moved(pe, ("kT", p))
                    c = slice(t * P, (t + 1) * P)
                    dst = bank(step)[:, 0:2 * CTX].rearrange("p (j c) -> p j c", j=2)
                    filled(product3(dst, q_hi[:, b, p, c], q_lo[:, b, p, c], k_hi[:, p, b, :, 0:CTX], k_lo[:, p, b, :, 0:CTX]), step)
                elif kind == "pT":
                    b, t, k = step[1:]
                    r = (b * T + t) % 2
                    pe.wait_ge(prob_normed, position[("norm", b, t)])
                    for m in range(4 if k < 2 else 2):
                        at = (4 * k + m) * P if k < 2 else H0 * P + 4 * m * PAD
                        src = prob_n[:, r, at:at + P]
                        ins = pe.transpose(bank(step)[:, m * P:(m + 1) * P], src, ident[:, :])
                    filled(ins, step)
                elif kind == "pv":
                    b, p = step[1:]
                    for k in range(3):
                        wait_moved(pe, ("pT", b, T - 1, k))
                    wait_moved(pe, ("vf", b))
                    wait_moved(pe, ("vs", b))
                    pe.matmul(bank(step), vs0[:, b, p, :], probT0[:, H0 + p // 2, :], start=True, stop=False, skip_group_check=True)
                    for j in range(2):
                        h = 2 * p + j
                        ins = pe.matmul(bank(step)[64 * j:64 * j + 64, :], v0[:, b, h * DH0:(h + 1) * DH0], probT0[:, h, :],
                                        start=False, stop=True, skip_group_check=True)
                    filled(ins, step)
                elif kind == "wo":
                    b = step[1]
                    pe.wait_ge(loaded["wo0"], 16)
                    for p in range(PAIRS):
                        wait_moved(pe, ("pv", b, p))
                        for t in range(T):
                            ins = pe.matmul(bank(step)[:, t * P:(t + 1) * P], outT0[:, p, t * P:(t + 1) * P], wo0[:, p, :],
                                            start=(p == 0 and t == 0), stop=(p == PAIRS - 1), skip_group_check=True)
                    filled(ins, step)
                elif kind == "gate":
                    s, b = step[1:]
                    wait_moved(pe, ("xT", s, b))
                    pe.wait_ge(lo_of["gates"], 1)
                    n_e = EXPERTS[s]
                    c = slice(0, E0) if s == 1 else slice(E0, E0 + E1)
                    for t in range(T):
                        x = slice(t * P, (t + 1) * P)
                        ins = product3(bank(step)[:, t * n_e:(t + 1) * n_e], xT_hi[:, b, x], xT_lo[:, b, x],
                                       gates_hi[:, c], gates_lo[:, c])
                    filled(ins, step)
                elif kind == "cwT":
                    s, b = step[1:]
                    pe.wait_ge(cw_ready, position[step])
                    for t in range(T):
                        ins = pe.transpose(bank(step)[0:EXPERTS[s], t * P:(t + 1) * P], cw[:, b, t, 0:EXPERTS[s]], ident[:, :])
                    filled(ins, step)
                elif kind == "hid":
                    s, b, i = step[1:]
                    hi, lo, _, name = w13[s]
                    wait_moved(pe, ("xT", s, b))
                    for m, half in enumerate(("hid1", "hid3")):
                        key = (half, s, b, i)
                        wait_bank_free(pe, key)
                        w = 2 * i + m
                        pe.wait_ge(lo_of[name], w // CHUNK + 1)
                        filled(product3(bank(key), hi[:, w, :], lo[:, w, :], xT_hi[:, b, :], xT_lo[:, b, :]), key)
                elif kind == "down":
                    s, b, i = step[1:]
                    n = hid_index[(s, b, i)]
                    key = ("y", s, b)
                    pe.wait_ge(loaded["w2_0" if s == 1 else "w2_1"], 16)
                    pe.wait_ge(hid_ready, n + 1)
                    if i == 0:
                        wait_bank_free(pe, key)
                    for t in range(T):
                        last = i == N_HID[s] - 1
                        ins = pe.matmul(bank(key)[:, t * P:(t + 1) * P], hid[:, n % 3, t * P:(t + 1) * P], w13[s][2][:, i, :],
                                        start=(i == 0 and t == 0), stop=last, skip_group_check=True)
                    if last:
                        filled(ins, key)
                    else:
                        ins.then_inc(hid_used, 1)
                elif kind == "k1":
                    g = step[1]
                    pe.wait_ge(loaded["wqkv1"], 64)
                    filled(pe.matmul(bank(step)[:, 0:B * CP], wk1[:, g, :], ctxT[:, :, :].rearrange("k b c -> k (b c)"),
                                     start=True, stop=True), step)
                elif kind == "q1":
                    b, g = step[1:]
                    wait_moved(pe, ("xT", 2, b))
                    pe.wait_ge(lo_of["wq1"], 1)
                    c = slice(g * P, (g + 1) * P)
                    filled(product3(bank(step), wq_hi1[:, c], wq_lo1[:, c], xT_hi[:, b, :], xT_lo[:, b, :]), step)
                elif kind == "score1":
                    b, t, g, half = step[1:]
                    wait_moved(pe, ("q1", b, g))
                    wait_moved(pe, ("k1", g))
                    filled(pe.matmul(bank(step)[:, 0:2 * CTX].rearrange("p (j c) -> p j c", j=2), q1[:, b, g, t * P:(t + 1) * P],
                                     k1[:, b, g, 2 * half:2 * half + 2, 0:CTX], start=True, stop=True), step)
                elif kind == "mT":
                    b = step[1]
                    for g in range(G1):
                        for half in range(2):
                            wait_moved(pe, ("score1", b, T - 1, g, half))
                    for t in range(T):
                        ins = pe.transpose(bank(step)[0:H1, t * P:(t + 1) * P],
                                           neg_max1[:, b, t, :, :].rearrange("p j g -> p (j g)"), ident[:, :])
                    filled(ins, step)
                elif kind == "expT":
                    b, g, j = step[1:]
                    pe.wait_ge(nm_placed[b], 16 * 8)
                    w = k1[:, b, g, j, 0:P] if j < 4 else k1s[:, b, g, :, :].rearrange("p j c -> p (j c)")
                    filled(pe.matmul(bank(step), w, q1[:, b, g, :], start=True, stop=True), step)
                elif kind == "pv1":
                    b, g = step[1:]
                    r = (b * G1 + g) % 2
                    wait_moved(pe, ("vf1", b))
                    wait_moved(pe, ("vs1", b))
                    wait_moved(pe, ("expT", b, g, 4))
                    pe.matmul(bank(step), vs1[:, b, g, :], probT1[:, r, 4, :], start=True, stop=False, skip_group_check=True)
                    for j in range(4):
                        wait_moved(pe, ("expT", b, g, j))
                        rows = slice(PAD * j, PAD * j + PAD)
                        ins = pe.matmul(bank(step)[rows, :], v1[:, b, g * P + PAD * j:g * P + PAD * (j + 1)], probT1[:, r, j, :],
                                        start=False, stop=True, skip_group_check=True, tile_position=(0, PAD * j))
                    filled(ins, step)
                elif kind == "oT":
                    b, g = step[1:]
                    wait_moved(pe, ("pv1", b, g))
                    for t in range(T):
                        ins = pe.transpose(bank(step)[:, t * P:(t + 1) * P], od[:, g % 2, t * P:(t + 1) * P], ident[:, :])
                    filled(ins, step)
                elif kind == "onT":
                    b = step[1]
                    wait_moved(pe, ("oT", b, G1 - 1))
                    wait_moved(pe, ("oT", b, G1 - 2))
                    for t in range(T):
                        ins = pe.transpose(bank(step)[:, t * P:(t + 1) * P], on[:, t, :], ident[:, :])
                    filled(ins, step)
                elif kind == "wo1":
                    b = step[1]
                    wait_moved(pe, ("onT", b))
                    for t in range(T):
                        ins = pe.matmul(bank(step)[:, t * P:(t + 1) * P], onT[:, t * P:(t + 1) * P], wo1[:, :],
                                        start=(t == 0), stop=True, skip_group_check=True)
                    filled(ins, step)


def lay_out(x, ctx_768, L0_xattn_Wq, L0_xattn_Wk, L0_xattn_Wv, L0_xattn_Wo, L0_xattn_bo, L0_ffn_w_gate, L0_ffn_w1_e,
            L0_ffn_w3_e, L0_ffn_w2_e, L0_ffn_w1_s, L0_ffn_w3_s, L0_ffn_w2_s, L1_xattn_Wq, L1_xattn_Wk, L1_xattn_Wv,
            L1_xattn_Wo, L1_ffn_router_w, L1_ffn_experts_bias, L1_ffn_w1, L1_ffn_w3, L1_ffn_w2, L1_ffn_sw1, L1_ffn_sw3,
            L1_ffn_sw2):
    f = np.float32
    d = {}
    d["x"] = x.reshape(B * T, P, P).transpose(1, 0, 2)
    ctxT = np.ones((CD + 1, B, CP), f)
    ctxT[:CD, :, :CTX] = ctx_768.transpose(2, 0, 1)
    ctxT[:CD, :, CTX:] = ctxT[:CD, :, CTX - 1:CTX]
    d["ctxT"] = ctxT
    d["ctxT_rest"] = np.tile(ctxT[:, :, P:], (1, 1, 4))
    d["wq0"], d["wk0"], d["wv0"] = L0_xattn_Wq, L0_xattn_Wk, L0_xattn_Wv
    d["wo0"] = L0_xattn_Wo.reshape(PAIRS, P, P).transpose(1, 0, 2)
    d["bo"] = np.broadcast_to(L0_xattn_bo, (P, P))
    d["gates"] = np.concatenate([L0_ffn_w_gate.T, L1_ffn_router_w.T], axis=1)
    d["gate_bias"] = np.broadcast_to(L1_ffn_experts_bias, (P, E1))
    d["ident"] = np.eye(P, dtype=f)
    d["lower_first"] = np.broadcast_to(np.tril(np.ones((NG, NG), f), -1), (P, NG, NG))
    lo_rows = np.zeros((4, PAD, 2), f)
    lo_rows[:, DH1:2 * DH1, 0] = -1.0
    lo_rows[:, 2 * DH1:3 * DH1, 1] = -1.0
    d["lo_rows"] = lo_rows.reshape(P, 2)

    def hidden(shared1, shared3, expert1, expert3):
        w = [np.concatenate(pair, axis=1).reshape(P, -1, P) for pair in ((shared1, expert1), (shared3, expert3))]
        return np.stack(w, axis=2).reshape(P, -1, P)

    d["w13_0"] = hidden(L0_ffn_w1_s.T, L0_ffn_w3_s.T, L0_ffn_w1_e.transpose(2, 0, 1).reshape(P, -1),
                        L0_ffn_w3_e.transpose(2, 0, 1).reshape(P, -1))
    d["w2_0"] = np.concatenate([L0_ffn_w2_s.T, L0_ffn_w2_e.transpose(0, 2, 1).reshape(-1, P)]).reshape(-1, P, P).transpose(1, 0, 2)
    d["w13_1"] = hidden(L1_ffn_sw1[0], L1_ffn_sw3[0], L1_ffn_w1.transpose(1, 0, 2).reshape(P, -1),
                        L1_ffn_w3.transpose(1, 0, 2).reshape(P, -1))
    d["w2_1"] = np.concatenate([L1_ffn_sw2[0], L1_ffn_w2.reshape(-1, P)]).reshape(-1, P, P).transpose(1, 0, 2)

    def groups(w, copies, ones_at):
        rows = w.shape[0] + (1 if ones_at else 0)
        g = np.zeros((rows, H1, PAD), f)
        for r in range(copies):
            g[:w.shape[0], :, r * DH1:(r + 1) * DH1] = w.reshape(w.shape[0], H1, DH1)
        for c in ones_at:
            g[-1, :, c] = 1.0
        return g.reshape(rows, G1 * P)

    d["wq1"] = groups(L1_xattn_Wq, 3, ())
    d["wk1"] = groups(L1_xattn_Wk, 3, (3 * DH1, 3 * DH1 + 1)).reshape(CD + 1, G1, P)
    d["wv1"] = groups(L1_xattn_Wv, 1, (DH1,))
    d["wo1"] = L1_xattn_Wo
    return {k: np.ascontiguousarray(v) for k, v in d.items()}


def kernel(**inputs):
    import concourse.bacc as bacc
    from concourse.bass_utils import run_bass_kernel_spmd

    nc = bacc.Bacc("TRN2", target_bir_lowering=False, num_devices=1)
    arrays = {"in_" + k: v for k, v in lay_out(**{k: np.asarray(v) for k, v in inputs.items()}).items()}
    aps = {k[3:]: nc.dram_tensor(k, v.shape, mybir.dt.from_np(v.dtype), kind="ExternalInput").ap() for k, v in arrays.items()}
    out = nc.dram_tensor(OUT_NAME, (P, B * T, P), F32, kind="ExternalOutput").ap()
    build(nc, aps, out)
    got = run_bass_kernel_spmd(nc, [arrays], core_ids=[0]).results[0][OUT_NAME]
    return got.transpose(1, 0, 2).reshape(B, TOK, P)
```

```python
from contextlib import ExitStack

import numpy as np

import concourse.bass as bass
from concourse import mybir

F32 = mybir.dt.float32
F32R = mybir.dt.float32r
ACT = mybir.ActivationFunctionType
ALU = mybir.AluOpType
AX = mybir.AxisListType.X

P = 128
B = 2
T = 4
TOK = T * P
CTX, CD = 154, 96
REST = CTX - P
PAD = 32
CP = P + PAD
EPS = 1e-5

H0, DH0 = 8, 64
PAIRS = H0 // 2
H1, DH1 = 16, 8
G1 = H1 // 4
E0, F0 = 16, 64
E1, F1 = 8, 256
NG, TOPK0, TOPK1 = 4, 4, 2
N_HID = {1: 1 + E0 * F0 // P, 3: 2 + E1 * F1 // P}
N_SHARED = {1: 1, 3: 2}
EXPERTS = {1: E0, 3: E1}
SLOTS = 8
LAG = 2
HIDS = 3
CHUNK = 6
OUT_NAME = "out"


def weave(main, extra):
    o, done = [], 0
    for i, step in enumerate(main):
        o.append(step)
        upto = (i + 1) * len(extra) // len(main)
        o += extra[done:upto]
        done = upto
    return [step for step in o if step is not None]


def make_order():
    def scores(b, t):
        return [("score", b, t, p) for p in range(PAIRS)]

    def probs(b, t):
        return [("pT", b, t, k) for k in range(3)]

    def scores1(b, t):
        return [("score1", b, t, g, h) for g in range(G1) for h in range(2)]

    def finish(s, b):
        return ([("ycopy", s, b), ("yT", s, b)] if s == 3 else []) + [("res", s, b)]

    def ffn(s, b, first, last, before=None):
        o = []
        n = N_HID[s]
        for i in range(first, last):
            if i < n:
                o += [("h1", s, b, i), ("h3", s, b, i)]
                if s == 3:
                    o.append(("hsplit", s, b, i))
            if i >= LAG:
                o.append(("down", s, b, i - LAG))
            elif before is not None:
                o.append(("down", s, before, n + i - LAG))
                if i == LAG - 1:
                    o += finish(s, before)
        if last == n + LAG:
            o += finish(s, b)
        return o

    def route(s, b):
        return [("route", s, b, part) for part in range(ROUTE_PARTS[s])]

    o = [("lnA", 0, 0), ("split", "wq0", 0), ("kT", 0), ("lnB", 0, 0), ("xT", 0, 0), ("kT", 1), ("lnA", 0, 1)]
    o += [("q", 0, 0), ("kT", 2), ("q", 0, 1), ("kT", 3), ("q", 0, 2), ("score", 0, 0, 0), ("q", 0, 3), ("score", 0, 0, 1)]
    o += [("lnB", 0, 1), ("score", 0, 0, 2), ("score", 0, 0, 3), ("bo", 0), ("vf", 0), ("bo", 1), ("split", "gates", 0)]
    w13_0 = [("split", "w13_0", c) for c in range(2 * N_HID[1] // CHUNK)]
    o += weave(scores(0, 1), [("vs", 0), ("xT", 0, 1)] + w13_0[0:1]) + [("norm", 0, 0)]
    o += weave(scores(0, 2), [("q", 1, 0), ("q", 1, 1)]) + [("norm", 0, 1)] + probs(0, 0) + w13_0[1:2]
    o += weave(scores(0, 3), [("q", 1, 2), ("q", 1, 3)]) + [("norm", 0, 2)] + probs(0, 1) + w13_0[2:3]
    o += weave(scores(1, 0), [None, ("vf", 1)]) + [("norm", 0, 3)] + probs(0, 2)
    o += weave(scores(1, 1), [None, ("vs", 1)]) + [("norm", 1, 0)] + probs(0, 3)
    o += weave(scores(1, 2), [None, ("pv", 0, 0), None, ("pv", 0, 1)]) + [("norm", 1, 1)] + [("pv", 0, 2), ("pv", 0, 3)]
    o += scores(1, 3) + [("wo", 0), ("lnA", 1, 0)] + probs(1, 0) + [("norm", 1, 2)] + probs(1, 1) + [("lnB", 1, 0), ("norm", 1, 3)]
    o += [("xT", 1, 0)] + probs(1, 2) + [("gate", 1, 0)] + probs(1, 3)
    o += weave([("pv", 1, p) for p in range(PAIRS)], route(1, 0))
    o += [("wo", 1), ("cwT", 1, 0), ("lnA", 1, 1)]
    k1 = [("k1", g) for g in range(G1)]
    place = [("place_k1", g, j) for g in range(G1) for j in range(4)]
    o += [("place_k1s", g) for g in range(G1)]
    w2_1 = [("split", "w2_1", c) for c in range(N_HID[3] // CHUNK)]
    v1 = [("vf1", b) for b in range(B)] + [("vs1", b) for b in range(B)]
    splits = [("split", "w13_1", c) for c in range(2 * N_HID[3] // CHUNK)]
    o += ffn(1, 0, 0, 1) + [("lnB", 1, 1)] + ffn(1, 0, 1, 2) + [("xT", 1, 1)]
    o += weave(ffn(1, 0, 2, 9), [None, ("gate", 1, 1), ("split", "wq1", 0)] + route(1, 1)[:2] + k1[:1] + route(1, 1)[2:] + [("cwT", 1, 1)]
               + k1[1:2] + place[0:4] + k1[2:3] + place[4:8])
    o += ffn(1, 0, 9, 9 + LAG) + [("lnA", 2, 0)]
    o += weave(ffn(1, 1, 0, 3), k1[3:] + place[8:16] + [("lnB", 2, 0)] + v1[:1])
    o += [("xT", 2, 0)] + weave(ffn(1, 1, 3, 5), v1[1:] + [("q1", 0, g) for g in range(G1)])
    o += weave(ffn(1, 1, 5, 9 + LAG), scores1(0, 0) + scores1(0, 1) + scores1(0, 2))
    o += weave([("lnA", 2, 1)] + scores1(0, 3) + [("lnB", 2, 1), ("mT", 0), ("xT", 2, 1)], splits[0:2])
    o += weave([("q1", 1, g) for g in range(G1)] + scores1(1, 0) + scores1(1, 1), [])

    def heads1(b, back):
        o = []
        for g in range(G1):
            o += [("expT", b, g, j) for j in range(3)] + back[:1] + [("expT", b, g, j) for j in range(3, 5)] + back[1:]
            back = [("pv1", b, g), ("oT", b, g)]
        return o, back

    o1, back = heads1(0, [])
    o += weave(o1[:-6], scores1(1, 2) + scores1(1, 3) + [("mT", 1)]) + o1[-6:]
    o += back[:1] + splits[2:3] + back[1:] + [("onT", 0), ("wo1", 0), ("lnA", 3, 0)]
    o1, back = heads1(1, [])
    o += weave(o1, [None, ("lnB", 3, 0), None, ("xT", 3, 0), None, ("gate", 3, 0)] + route(3, 0) + [None, splits[3], ("cwT", 3, 0)])
    o += back[:1] + ffn(3, 0, 0, 1) + back[1:] + splits[4:5] + ffn(3, 0, 1, 2) + [("onT", 1), ("wo1", 1), ("lnA", 3, 1)] + splits[5:] + w2_1
    o += weave(ffn(3, 0, 2, 10), [None, ("lnB", 3, 1), None, ("xT", 3, 1), None, ("gate", 3, 1)] + route(3, 1) + [("cwT", 3, 1)])
    o += ffn(3, 0, 10, 18) + ffn(3, 1, 0, 18 + LAG, before=0)
    return o


ROUTE_PARTS = {1: 4, 3: 2}

PROGRAM = {
    "PE":
        "kT kT xT kT kT xT q q vf q score vf " + 2 * "vs score q q " + 4 * "score " + "q " + 5 * "score " + "pT " +
        2 * "score pT pT score " + "score " + 2 * "pT score score pT " + "score score pT " + 2 * "pT score score " +
        "pv pT pT pv pv pv " + 4 * "score " + "wo score " + 6 * "pT " +
        "xT pT pT pT h3 gate h1 h1 h1 pT h3 h3 pv pv cwT pv pv h1 h3 wo down h3 h1 down h1 h1 h1 h1 xT vs1 down h3 "
        "gate h3 down k1 k1 down down h3 k1 k1 h3 h3 h1 down h1 h1 down cwT down h3 h1 down vs1 vf1 h1 h1 xT vf1 q1 "
        "q1 h3 q1 down q1 h3 score1 down h3 " + 3 * "score1 " + "down score1 score1 h3 down " + 3 * "score1 " +
        2 * "h3 score1 " + "score1 h3 down " + 3 * "score1 score1 h1 " + 3 * "score1 " + 2 * "down score1 " +
        "score1 score1 down " + 7 * "score1 " + "xT mT q1 q1 " + 2 * "q1 score1 score1 " + "score1 score1 expT " +
        3 * "expT score1 " + 3 * "score1 " + 2 * "expT score1 " + 3 * "score1 expT " + "score1 pv1 " + 3 * "score1 " +
        4 * "expT " + "oT score1 " + 2 * "score1 expT expT " + 2 * "score1 expT score1 " + 4 * "score1 " +
        "pv1 mT pv1 expT oT pv1 oT oT expT expT onT expT expT wo1 " + 3 * "expT " + "pv1 expT expT oT expT expT xT " +
        3 * "expT " +
        "pv1 expT expT gate oT expT expT pv1 expT expT cwT h1 oT pv1 h1 h3 oT h3 h3 onT h3 h1 wo1 h1 down h1 down "
        "h1 h3 h3 h3 h3 down " + 3 * "down h1 h1 " +
        "down down h3 h3 xT gate h3 down h3 h3 h1 down h1 h1 cwT h3 h3 h3 down h3 down h3 " + 5 * "h1 down " +
        "h3 h3 down h3 h3 h1 h1 h1 down h1 h3 h3 h3 h3 h1 h1 down h1 down h1 h3 h3 down down h3 yT h3 h1 h1 down "
        "down h1 h1 down h3 h3 down h3 down h3 h3 down h1 down h3 h1 down down h1 h1 " + 4 * "down " + "yT ",
    "ACT":
        "split kT kT split xT kT kT xT q " + 3 * "split " + 2 * "q q score " + "q score q " + 5 * "score " + "q " +
        4 * "score score score pT score " + 3 * "score " + "pv pv pv pv " + 4 * "score " +
        "pT score pT xT pT gate h1 pT h1 h1 pv pv cwT pv pv h1 h1 " + 3 * "split " +
        "xT h1 split h1 gate h1 k1 k1 h1 " + 3 * "place_k1 " + "k1 k1 " + 8 * "place_k1 " +
        "h1 h1 split cwT split split h1 " + 5 * "place_k1 " + "xT q1 q1 h1 q1 q1 " + 5 * "h1 " + "xT mT q1 q1 q1 q1 " +
        16 * "expT " + "mT " + 4 * "expT " + 3 * "split " + "expT expT onT " + 9 * "expT " + "xT " + 7 * "expT " +
        "route expT expT cwT h1 h1 onT " + 8 * "hsplit h1 " + "xT " + 2 * "hsplit h1 " +
        "route h1 h1 hsplit hsplit cwT h1 hsplit " + 5 * "hsplit h1 " + "ycopy " + 3 * "hsplit h1 " +
        "h1 h1 h1 hsplit " + 4 * "hsplit h1 " + "hsplit hsplit h1 h1 " + 3 * "hsplit " + 4 * "h1 hsplit " +
        "hsplit ycopy ",
    "DVE":
        "lnA lnA lnB kT kT lnB xT kT kT xT q vf score q vf " + 2 * "q vs score q " + "score score q score norm " +
        5 * "score " + "norm q " + 2 * "pT score score " + "norm pT pT " + 4 * "score " + "norm pT pT " + 4 * "score " +
        "norm pT pT " + 4 * "score " + "norm pT " + 4 * "score " +
        "pT norm wo score lnA pT pT norm lnB pT pT xT pT pT h3 " + 4 * "route " +
        "wo h3 h3 lnA h3 h3 lnB xT vs1 h3 h3 route route k1 k1 route h3 h3 k1 route k1 h3 res lnA vs1 lnB vf1 xT "
        "vf1 h3 q1 q1 h3 q1 h3 q1 score1 h3 " + 5 * "score1 " + "h3 " + 3 * "score1 " + "h3 h3 " + 10 * "score1 " +
        "h3 " + 6 * "score1 " + "res score1 lnA " + 4 * "score1 " + "lnB score1 score1 xT mT " +
        2 * "q1 q1 score1 score1 score1 " + 12 * "score1 " + "pv1 " + 3 * "score1 " + "oT " + 11 * "score1 " +
        "pv1 mT pv1 oT pv1 oT oT wo1 lnA pv1 lnB oT xT pv1 gate route oT route pv1 oT pv1 h3 oT h3 h3 hsplit h3 wo1 "
        "hsplit lnA hsplit hsplit h3 lnB h3 " + 2 * "h3 hsplit " +
        "hsplit hsplit h3 h3 xT hsplit gate route h3 hsplit h3 route h3 h3 hsplit hsplit h3 " + 2 * "h3 hsplit " +
        "hsplit h3 " + 3 * "hsplit " + "h3 h3 " + 2 * "h3 hsplit " + "hsplit h3 h3 " + 2 * "h3 h3 hsplit hsplit " +
        "res h3 h3 hsplit " + 4 * "hsplit h3 " + "hsplit " + 2 * "hsplit h3 " + 3 * "hsplit " + "res ",
    "Pool":
        "lnA split lnA bo split bo " + 3 * "split " + 7 * "norm " + "lnA norm h3 h3 h3 lnA " + 4 * "h3 split " +
        2 * "place_k1s " + "h3 h3 " + 2 * "place_k1s " + "h3 split lnA split split " + 8 * "h3 " + "lnA " +
        3 * "split " + 2 * "lnA h3 h3 h3 h3 " + 28 * "h3 ",
    "SP":
        "cwT wo split cwT split mT mT cwT cwT res res ",
}


def takes(engine, step):
    kind = step[0]
    if engine == "SP":
        return kind in ("cwT", "mT") or step in (("wo", 1), ("split", "w13_1", 2), ("split", "w2_1", 0)) or (kind == "res" and step[1] == 3)
    if engine == "PE":
        return True
    if kind == "pT":
        return (engine == "ACT") == (step[3] == 2)
    if kind == "gate":
        return (engine == "ACT") == (step[1] == 1)
    if kind == "route":
        return engine == "DVE" or step[1:] == (3, step[2], 0)
    return True


def order_of(engine, order):
    steps = {}
    for step in order:
        if takes(engine, step):
            steps.setdefault(step[0], []).append(step)
    steps = {kind: iter(s) for kind, s in steps.items()}
    return [next(steps[kind]) for kind in PROGRAM[engine].split()]


RING = {
    "score": (0, 1, 2, 3), "h1": (0, 1, 2, 3), "h3": (0, 1, 2, 3), ("expT", 0): (0, 1, 2, 3), ("q1", 1): (0, 1, 2, 3),
    "kT": (4, 5), "pT": (4, 5), "gate": (4, 5), "cwT": (4, 5), "k1": (4, 5), "v1": (4, 5), "vf1": (4, 5), "vs1": (4, 5), "mT": (4, 5), "onT": (4, 5), "q": (4, 5), "yT": (4, 5), ("q1", 0): (4, 5), ("oT", 1): (4, 5),
    "xT": (6,), "wo1": (6,), ("oT", 0): (6,), ("pv1", 1): (6,),
    "vf": (6, 7), "vs": (6, 7), "pv": (6, 7), "wo": (6, 7), ("pv1", 0): (6, 7),
    "y": (7,),
    ("score1", 0): (4, 5, 6),
    ("score1", 1): (4, 5, 7),
    ("expT", 1): (0, 1),
}


def count_uses(order):
    uses, turn, count = {}, {}, {}
    for step in order:
        key = step
        if step[0] == "down":
            if step[3] > 0:
                continue
            key = ("y",) + step[1:3]
        ring = RING.get(key[:2], RING.get(key[0]))
        if ring is not None:
            n = turn.get(ring, 0)
            turn[ring] = n + 1
            bank = ring[n % len(ring)]
            count[bank] = count.get(bank, 0) + 1
            uses[key] = (bank, count[bank])
    return uses


def build(nc, a, out):
    order = make_order()
    uses = count_uses(order_of("PE", order))
    position = {}
    seen = {}
    for step in order:
        seen[step[0]] = seen.get(step[0], 0) + 1
        position[step] = seen[step[0]]

    with ExitStack() as ctx:
        def sb(name, shape, dt=F32, at=ctx):
            return at.enter_context(nc.sbuf_tensor(name, shape, dt))

        def sem(name):
            return ctx.enter_context(nc.semaphore(name))

        psum = ctx.enter_context(nc.psum_tensor("psum", [P, 8, 512], F32))

        X = sb("X", [P, B * T, P])
        xn = sb("xn", [P, B, T, P])
        xT_hi = sb("xT_hi", [P, B, TOK], F32R)
        xT_lo = sb("xT_lo", [P, B, TOK], F32R)
        w_src = sb("w_src", [P, N_HID[1] * 2, P])
        spread = sb("spread", [P, SLOTS, TOK])
        act_s = sb("act_s", [P, 2, TOK])
        gated_u = sb("gated_u", [P, 2, TOK])
        hid = sb("hid", [P, HIDS, TOK])
        ident = sb("ident", [P, P])
        bo = sb("bo", [P, P])
        ctxT = sb("ctxT", [CD + 1, B, CP])
        ctxT_rest = sb("ctxT_rest", [CD + 1, B, P])
        gates_src = sb("gates_src", [P, E0 + E1])
        gates_hi = sb("gates_hi", [P, E0 + E1], F32R)
        gates_lo = sb("gates_lo", [P, E0 + E1], F32R)
        gate_bias = sb("gate_bias", [P, E1])
        vs0_mask = sb("vs0_mask", [P, 2, P])
        vs1_mask = sb("vs1_mask", [P, P])
        head_rows = sb("head_rows", [P, 4])
        lower_first = sb("lower_first", [P, NG, NG])
        lo_rows = sb("lo_rows", [P, 2])
        stats = sb("stats", [P, B, T, 6])
        mv = sb("mv", [P, B, T, 2])
        vareps = sb("vareps", [P, B, T])
        rstd = sb("rstd", [P, B, T])
        minus_half = sb("minus_half", [P, T])
        neg_max0 = sb("neg_max0", [P, B, T, H0])
        row_sum = sb("row_sum", [P, B, T, H0])
        row_inv = sb("row_inv", [P, B, T, H0])
        neg_max1 = sb("neg_max1", [P, B, T, 4, G1])
        den_inv = sb("den_inv", [P, 2, T, 4])
        e_neg = sb("e_neg", [P, T, E0])
        sc = sb("sc", [P, T, E0])
        pair_max = sb("pair_max", [P, T * NG, 2])
        pair_sum = sb("pair_sum", [P, T * NG, 2])
        g_score = sb("g_score", [P, T, NG])
        g_cross = sb("g_cross", [P, T, NG])
        beats = sb("beats", [P, T * NG, NG])
        ties = sb("ties", [P, T * NG, NG])
        rank = sb("rank", [P, T, NG])
        allowed = sb("allowed", [P, T, NG])
        penalty = sb("penalty", [P, T, NG])
        cand = sb("cand", [P, T, E0 + 8])
        replaced = sb("replaced", [P, T, E0 + 8])
        top = sb("top", [P, T, 8])
        chosen = sb("chosen", [P, T, E0])
        diff = sb("diff", [P, T, E1])
        e_diff = sb("e_diff", [P, T, E1])
        w_un = sb("w_un", [P, T, E0])
        w_sum = sb("w_sum", [P, T])
        w_inv = sb("w_inv", [P, T])
        cw = sb("cw", [P, B, T, E0])
        cwT_sb = sb("cwT_sb", [E0, B, TOK])

        with ExitStack() as r:
            w13_hi0 = sb("w13_hi0", [P, 2 * N_HID[1], P], F32R, r)
            w13_lo0 = sb("w13_lo0", [P, 2 * N_HID[1], P], F32R, r)
            w2_0 = sb("w2_0", [P, N_HID[1], P], F32, r)
            with ExitStack() as r2:
                wk0 = sb("wk0", [CD, H0 * DH0], F32, r2)
                wv0 = sb("wv0", [CD, H0 * DH0], F32, r2)
                wo0 = sb("wo0", [P, PAIRS, P], F32, r2)
                q_hi = sb("q_hi", [P, B, PAIRS, TOK], F32R, r2)
                q_lo = sb("q_lo", [P, B, PAIRS, TOK], F32R, r2)
                k_hi = sb("k_hi", [P, PAIRS, B, 2, CP], F32R, r2)
                k_lo = sb("k_lo", [P, PAIRS, B, 2, CP], F32R, r2)
                v0 = sb("v0", [P, B, H0 * DH0], F32, r2)
                vs0 = sb("vs0", [P, B, PAIRS, P], F32, r2)
                prob = sb("prob", [P, 2, H0, CTX], F32, r2)
                prob_n = sb("prob_n", [P, 2, H0 * CP], F32, r2)
                probT0 = sb("probT0", [P, H0 + 2, TOK], F32, r2)
                with ExitStack() as r3:
                    wq_src0 = sb("wq_src0", [P, H0 * DH0], F32, r3)
                    wq_hi0 = sb("wq_hi0", [P, H0 * DH0], F32R, r3)
                    wq_lo0 = sb("wq_lo0", [P, H0 * DH0], F32R, r3)
                outT0 = sb("outT0", [P, PAIRS, TOK], F32, r2)
            with ExitStack() as r2:
                w13_hi1 = sb("w13_hi1", [P, 2 * N_HID[3], P], F32R, r2)
                w13_lo1 = sb("w13_lo1", [P, 2 * N_HID[3], P], F32R, r2)
                w2_lo1 = sb("w2_lo1", [P, N_HID[3], P], F32R, r2)
                wq_hi1 = sb("wq_hi1", [P, G1 * P], F32R, r2)
                wq_lo1 = sb("wq_lo1", [P, G1 * P], F32R, r2)
                wk1 = sb("wk1", [CD + 1, G1, P], F32, r2)
                wv1 = sb("wv1", [CD + 1, G1 * P], F32, r2)
                wo1 = sb("wo1", [P, P], F32, r2)
                k1 = sb("k1", [P, B, G1, 4, CTX], F32R, r2)
                k1s = sb("k1s", [P, B, G1, 4, PAD], F32R, r2)
                q1 = sb("q1", [P, B, G1, TOK], F32R, r2)
                rounded = sb("rounded", [P, 2, TOK], F32R, r2)
                v1 = sb("v1", [P, B, G1 * P], F32, r2)
                vs1 = sb("vs1", [P, B, G1, P], F32, r2)
                nmT_hi = sb("nmT_hi", [H1, TOK], F32R, r2)
                nmT_lo = sb("nmT_lo", [H1, TOK], F32R, r2)
                with ExitStack() as r3:
                    wq_src1 = sb("wq_src1", [P, G1 * P], F32, r3)
                with ExitStack() as r3:
                    k_stack = sb("k_stack", [P, 2, B * CP], F32R, r3)
                od = sb("od", [P, 2, TOK], F32, r2)
                on = sb("on", [P, T, P], F32, r2)
        with ExitStack() as r:
            probT1 = sb("probT1", [P, 2, 5, TOK], F32, r)
            onT = sb("onT", [P, TOK], F32, r)

        w2_hi1 = k1[:, 0, :, :, :].rearrange("p g j c -> p (g j c)")[:, 0:N_HID[3] * P].rearrange("p (i d) -> p i d", d=P)
        hid_hi, hid_lo = q1[:, 0, 0:2, :], q1[:, 0, 2:4, :]
        yT = onT

        cw_dram = {(s, b): nc.dram_tensor(f"cw_{s}_{b}", (EXPERTS[s], TOK), F32).ap() for s in (1, 3) for b in range(B)}

        bank_ready = [sem(f"bank_ready{k}") for k in range(8)]
        bank_read = [sem(f"bank_read{k}") for k in range(8)]
        loaded = {n: sem(f"loaded_{n}") for n in (
            "x0", "x1", "ident", "const", "ctx", "ctxv", "wq0", "w13_0", "w2_0", "wo0", "wqkv1", "w13_1", "w2_1")}
        hi_of = {n: sem(f"hi_{n}") for n in ("wq0", "gates", "w13_0", "wq1", "w13_1", "w2_1")}
        lo_of = {n: sem(f"lo_{n}") for n in ("wq0", "gates", "w13_0", "wq1", "w13_1", "w2_1")}
        cleared0 = sem("cleared0")
        var_ready = sem("var_ready")
        rstd_ready = sem("rstd_ready")
        xn_ready = sem("xn_ready")
        xT_rounded = sem("xT_rounded")
        bo_added = sem("bo_added")
        kT_rounded = sem("kT_rounded")
        q_rounded = sem("q_rounded")
        negmax_ready = sem("negmax_ready")
        rowinv_ready = sem("rowinv_ready")
        prob_normed = sem("prob_normed")
        diff_ready = sem("diff_ready")
        e_diff_ready = sem("e_diff_ready")
        cw_ready = sem("cw_ready")
        cw_stored = sem("cw_stored")
        spread_loaded = [sem(f"spread_loaded{c}") for c in range(SLOTS // 2)]
        hid_ready = sem("hid_ready")
        hid_used = sem("hid_used")
        hid_rounded = sem("hid_rounded")
        hid_split = sem("hid_split")
        k1_rounded = sem("k1_rounded")
        k1_placed = sem("k1_placed")
        k1s_placed = sem("k1s_placed")
        q1_rounded = sem("q1_rounded")
        nm_rounded = sem("nm_rounded")
        nm_placed = [sem(f"nm_placed{b}") for b in range(B)]
        out_stored = sem("out_stored")
        dve_step = sem("dve_step")
        pool_step = sem("pool_step")

        def bank(key):
            return psum[:, uses[key][0], :]

        def wait_filled(eng, key):
            k, n = uses[key]
            eng.wait_ge(bank_ready[k], n)

        def wait_moved(eng, key):
            k, n = uses[key]
            eng.wait_ge(bank_read[k], n)

        def wait_bank_free(eng, key):
            k, n = uses[key]
            if n > 1:
                eng.wait_ge(bank_read[k], n - 1)

        def filled(ins, key):
            ins.then_inc(bank_ready[uses[key][0]], 1)

        def moved(ins, key):
            ins.then_inc(bank_read[uses[key][0]], 1)

        HEAD_SCALE0 = float(DH0) ** -0.5
        HEAD_SCALE1 = float(DH1) ** -0.5
        splits = {"wq0": (wq_src0, wq_hi0, wq_lo0), "gates": (gates_src, gates_hi, gates_lo), "wq1": (wq_src1, wq_hi1, wq_lo1)}
        w13 = {1: (w13_hi0, w13_lo0, "w13_0"), 3: (w13_hi1, w13_lo1, "w13_1")}
        n_src = 2 * N_HID[1] // CHUNK

        def split_aps(name, c):
            if name in splits:
                s, h, l = splits[name]
                return s[:, :], h[:, :], l[:, :]
            h, l = {"w13_0": (w13_hi0, w13_lo0), "w13_1": (w13_hi1, w13_lo1), "w2_1": (w2_hi1, w2_lo1)}[name]
            at = slice(c * CHUNK, (c + 1) * CHUNK)
            cs = c % n_src
            return w_src[:, cs * CHUNK:(cs + 1) * CHUNK, :], h[:, at, :], l[:, at, :]

        def wait_split_source(eng, name, c):
            if name == "w13_1":
                eng.wait_ge(loaded[name], 16 * (c // n_src + 1))
            else:
                eng.wait_ge(loaded[{"gates": "const", "wq1": "wqkv1"}.get(name, name)],
                            {"gates": 16 * N_CONST, "wq1": 16 * 4}.get(name, 16))

        N_CONST = 8
        hid_index = {}
        for step in order:
            if step[0] == "h1":
                hid_index[step[1:]] = len(hid_index)
        tiles = list(hid_index)
        first_split = hid_index[(3, 0, 0)]

        def wait_hid_used(eng, n):
            s, b, i = tiles[n]
            if i == N_HID[s] - 1:
                wait_filled(eng, ("y", s, b))
            else:
                eng.wait_ge(hid_used, sum(t[2] < N_HID[t[0]] - 1 for t in tiles[:n + 1]))

        def slot_of(s, i):
            e = i - N_SHARED[s]
            return e if s == 1 else e // 2

        def spread_count(s, b):
            return 16 * (2 * (b + 1) if s == 1 else 2 * B + b + 1)

        block = ctx.enter_context(nc.Block())

        @block.sync
        def _(sp):
            def load(dst, src, name):
                sp.dma_start(dst, src).then_inc(loaded[name], 16)

            load(X[:, 0:T, :], a["x"][:, 0:T, :], "x0")
            load(ident[:, :], a["ident"], "ident")
            load(ctxT[:, :, :], a["ctxT"], "ctx")
            load(wk0[:, :], a["wk0"], "ctx")
            load(wq_src0[:, :], a["wq0"], "wq0")
            load(X[:, T:2 * T, :], a["x"][:, T:2 * T, :], "x1")
            for dst, name in ((bo[:, :], "bo"), (gates_src[:, :], "gates"),
                              (gate_bias[:, :], "gate_bias"), (lower_first[:, :, :], "lower_first"),
                              (lo_rows[:, :], "lo_rows"), (vs0_mask[:, :, :], "vs0_mask"), (vs1_mask[:, :], "vs1_mask"),
                              (head_rows[:, :], "head_rows")):
                load(dst, a[name], "const")
            load(ctxT_rest[:, :, :], a["ctxT_rest"], "ctxv")
            load(wv0[:, :], a["wv0"], "ctxv")
            load(wo0[:, :, :], a["wo0"], "wo0")
            load(w_src[:, :, :], a["w13_0"], "w13_0")
            load(w2_0[:, :, :], a["w2_0"], "w2_0")

            def spread_weights(s, b):
                wait_moved(sp, ("cwT", s, b))
                sp.dma_start(cw_dram[s, b], cwT_sb[0:EXPERTS[s], b, :]).then_inc(cw_stored, 16)
                sp.wait_ge(cw_stored, 16 * position[("cwT", s, b)])
                for c in range(SLOTS // 2):
                    last = {(1, 0): None, (1, 1): (1, 0, 2 * c + 2), (3, 0): (1, 1, 2 * c + 2),
                            (3, 1): (3, 0, 2 + 4 * c + 3)}[s, b]
                    if last is not None:
                        wait_moved(sp, ("h3",) + last)
                    for half in range(2 if s == 1 else 1):
                        if s == 1:
                            rows = cw_dram[s, b].rearrange("(i two) n -> two i n", two=2)[half, 2 * c:2 * c + 2, :]
                            dst = spread[64 * half:64 * half + 64, 2 * c:2 * c + 2, :]
                            src = rows.unsqueeze(0).broadcast_to((64, 2, TOK))
                        else:
                            rows = cw_dram[s, b][2 * c:2 * c + 2, :]
                            dst = spread[:, 2 * c:2 * c + 2, :]
                            src = rows.unsqueeze(0).broadcast_to((P, 2, TOK))
                        sp.dma_start(dst, src).then_inc(spread_loaded[c], 16)

            for step in order_of("SP", order):
                if step == ("wo", 1):
                    wait_filled(sp, ("wo", 1))
                    load(wq_src1[:, :], a["wq1"], "wqkv1")
                    load(wk1[:, :, :], a["wk1"], "wqkv1")
                    load(wv1[:, :], a["wv1"], "wqkv1")
                    load(wo1[:, :], a["wo1"], "wqkv1")
                    sp.wait_ge(lo_of["w13_0"], n_src)
                    load(w_src[:, :, :], a["w13_1"][:, 0:2 * N_HID[1], :], "w13_1")
                if step == ("split", "w13_1", n_src - 1):
                    sp.wait_ge(lo_of["w13_1"], n_src)
                    load(w_src[:, :, :], a["w13_1"][:, 2 * N_HID[1]:, :], "w13_1")
                if step == ("split", "w2_1", 0):
                    sp.wait_ge(lo_of["w13_1"], 2 * n_src)
                    load(w_src[:, :, :], a["w2_1"], "w2_1")
                if step[0] == "cwT":
                    spread_weights(*step[1:])
                if step[0] == "mT":
                    b = step[1]
                    wait_moved(sp, step)
                    for part, rows in ((0, nmT_hi), (1, nmT_lo)):
                        for j in range(4):
                            r = PAD * j + 3 * DH1 + part
                            sp.dma_start(q1[r:r + 1, b, :, :].bitcast(F32), rows[G1 * j:G1 * (j + 1), :].bitcast(F32)).then_inc(nm_placed[b], 16)
                if step[0] == "res" and step[1] == 3:
                    b = step[2]
                    wait_moved(sp, ("yT", 3, b))
                    sp.dma_start(out[:, b * T:(b + 1) * T, :], X[:, b * T:(b + 1) * T, :]).then_inc(out_stored, 16)
            sp.wait_ge(out_stored, 16 * B)

        @block.gpsimd
        def _(pool):
            steps = [0]

            def chain(ins):
                ins.then_inc(pool_step, 1)
                steps[0] += 1
                pool.wait_ge(pool_step, steps[0])

            pool.memset(minus_half[:, :], -0.5).then_inc(cleared0, 1)
            pool.memset(k_hi[:, :, :, :, :].bitcast(F32), 0.0).then_inc(cleared0, 1)
            pool.memset(k_lo[:, :, :, :, :].bitcast(F32), 0.0).then_inc(cleared0, 1)
            rest = prob_n[:, :, H0 * P:].rearrange("p r (h c) -> p r h c", h=H0)
            pool.memset(rest[:, :, :, REST:PAD], 0.0).then_inc(cleared0, 1)

            for step in order_of("Pool", order):
                kind = step[0]
                if kind == "split":
                    name, c = step[1:]
                    src, hi, lo = split_aps(name, c)
                    pool.wait_ge(hi_of[name], c + 1)
                    pool.tensor_tensor(lo, src, hi.bitcast(F32), ALU.subtract).then_inc(lo_of[name], 1)
                elif kind == "lnA":
                    b = step[2]
                    pool.wait_ge(cleared0, 1)
                    pool.wait_ge(var_ready, position[step])
                    pool.tensor_tensor(rstd[:, b, :], vareps[:, b, :], minus_half[:, :], ALU.pow).then_inc(rstd_ready, 1)
                elif kind == "bo":
                    b = step[1]
                    pool.wait_ge(loaded["const"], 16 * N_CONST)
                    pool.wait_ge(xn_ready, position[("lnB", 0, b)])
                    xb = X[:, b * T:(b + 1) * T, :]
                    pool.tensor_tensor(xb, xb, bo[:, :].unsqueeze(1).broadcast_to((P, T, P)), ALU.add).then_inc(bo_added, 1)
                elif kind == "norm":
                    b, t = step[1:]
                    r = (b * T + t) % 2
                    pool.wait_ge(rowinv_ready, position[step])
                    pool.wait_ge(cleared0, 4)
                    if b * T + t >= 2:
                        wait_filled(pool, ("pT", (b * T + t - 2) // T, (b * T + t - 2) % T, 2))
                    for dst, cols in ((prob_n[:, r, 0:H0 * P].rearrange("p (h c) -> p h c", h=H0), slice(0, P)),
                                      (rest[:, r, :, 0:REST], slice(P, CTX))):
                        w = cols.stop - cols.start
                        ins = pool.tensor_tensor(dst, prob[:, r, :, cols],
                                                 row_inv[:, b, t, :].unsqueeze(2).broadcast_to((P, H0, w)), ALU.mult)
                    ins.then_inc(prob_normed, 1)
                elif kind == "place_k1s":
                    g = step[1]
                    wait_moved(pool, ("k1", g))
                    pool.wait_ge(loaded["const"], 16 * N_CONST)
                    k = k_stack[:, g % 2, :].bitcast(F32).rearrange("p (b c) -> p b c", b=B)[:, :, P:CP]
                    pool.tensor_tensor(k1s[:, :, g, :, :], k.unsqueeze(2).broadcast_to((P, B, 4, PAD)),
                                       head_rows[:, :].unsqueeze(1).unsqueeze(3).broadcast_to((P, B, 4, PAD)), ALU.mult)\
                        .then_inc(k1s_placed, 1)
                elif kind == "h3":
                    n = hid_index[step[1:]]
                    wait_moved(pool, ("h1",) + step[1:])
                    wait_moved(pool, step)
                    if n - HIDS >= first_split:
                        pool.wait_ge(hid_split, n - HIDS - first_split + 1)
                    elif n >= HIDS:
                        wait_hid_used(pool, n - HIDS)
                    pool.tensor_tensor(hid[:, n % HIDS, :], act_s[:, n % 2, :], gated_u[:, n % 2, :], ALU.mult)\
                        .then_inc(hid_ready, 1)

        @block.scalar
        def _(act):
            for step in order_of("ACT", order):
                kind = step[0]
                if kind == "split":
                    name, c = step[1:]
                    src, hi, lo = split_aps(name, c)
                    wait_split_source(act, name, c)
                    if name == "w2_1":
                        wait_filled(act, ("expT", 0, G1 - 1, 4))
                    act.copy(hi, src).then_inc(hi_of[name], 1)
                elif kind == "xT":
                    b = step[2]
                    wait_filled(act, step)
                    act.copy(xT_hi[:, b, :], bank(step)).then_inc(xT_rounded, 1)
                elif kind == "kT":
                    p = step[1]
                    wait_filled(act, step)
                    act.wait_ge(cleared0, 2)
                    for j in range(2):
                        rows = slice(64 * j, 64 * j + 64)
                        act.copy(k_hi[rows, p, :, j, :], bank(step)[rows, 0:B * CP].rearrange("p (b c) -> p b c", b=B))\
                            .then_inc(kT_rounded, 1)
                elif kind == "q":
                    b, p = step[1:]
                    wait_filled(act, step)
                    act.mul(q_hi[:, b, p, :], bank(step), HEAD_SCALE0).then_inc(q_rounded, 1)
                elif kind == "score":
                    b, t, p = step[1:]
                    r = (b * T + t) % 2
                    act.wait_ge(negmax_ready, position[step])
                    if b * T + t >= 2 and p == 0:
                        act.wait_ge(prob_normed, b * T + t - 1)
                    for j in range(2):
                        h = 2 * p + j
                        ins = act.activation(prob[:, r, h, 0:CTX], bank(step)[:, j * CTX:(j + 1) * CTX], ACT.Exp,
                                             bias=neg_max0[:, b, t, h:h + 1], accum_out=row_sum[:, b, t, h:h + 1])
                    moved(ins, step)
                elif kind == "pT" and step[3] == 2:
                    b, t = step[1:3]
                    wait_filled(act, step)
                    if b == 1 and t == 0:
                        wait_filled(act, ("pv", 0, PAIRS - 1))
                    moved(act.copy(probT0[:, H0:H0 + 2, t * P:(t + 1) * P],
                                   bank(step)[:, 0:2 * P].rearrange("p (g n) -> p g n", g=2)), step)
                elif kind == "pv":
                    b, p = step[1:]
                    wait_filled(act, step)
                    if b == 1:
                        wait_filled(act, ("wo", 0))
                    moved(act.copy(outT0[:, p, :], bank(step)), step)
                elif kind == "gate" and step[1] == 1:
                    wait_filled(act, step)
                    if step[2] > 0:
                        act.wait_ge(cw_ready, 1)
                    moved(act.activation(e_neg[:, :, :], bank(step)[:, 0:T * E0].rearrange("p (t e) -> p t e", t=T),
                                         ACT.Exp, scale=-1.0), step)
                elif kind == "route" and step[1] == 3 and step[3] == 0:
                    b = step[2]
                    act.wait_ge(diff_ready, b + 1)
                    act.activation(e_diff[:, :, :], diff[:, :, :], ACT.Exp).then_inc(e_diff_ready, 1)
                elif kind == "cwT":
                    s, b = step[1:]
                    wait_filled(act, step)
                    if s == 3:
                        act.wait_ge(cw_stored, 16 * position[("cwT", 1, b)])
                    moved(act.copy(cwT_sb[0:EXPERTS[s], b, :], bank(step)[0:EXPERTS[s], :]), step)
                elif kind == "h1":
                    n = hid_index[step[1:]]
                    wait_filled(act, step)
                    if n >= 2:
                        act.wait_ge(hid_ready, n - 1)
                    moved(act.activation(act_s[:, n % 2, :], bank(step), ACT.Silu), step)
                elif kind == "hsplit":
                    n = hid_index[step[1:]]
                    m = n - first_split
                    act.wait_ge(hid_ready, n + 1)
                    if m >= 2:
                        wait_hid_used(act, n - 2)
                    else:
                        wait_filled(act, ("expT", 0, G1 - 1, 4))
                    act.copy(hid_hi[:, m % 2, :], hid[:, n % HIDS, :]).then_inc(hid_rounded, 1)
                elif kind == "ycopy":
                    b = step[2]
                    wait_filled(act, ("y", 3, b))
                    wait_filled(act, ("wo1", 1) if b == 0 else ("yT", 3, 0))
                    moved(act.copy(yT[:, :], bank(("y", 3, b))), ("y", 3, b))
                elif kind == "k1":
                    g = step[1]
                    wait_filled(act, step)
                    if g >= 2:
                        wait_moved(act, ("k1", g - 2))
                    act.copy(rounded[:, g % 2, 0:B * CP], bank(step)[:, 0:B * CP]).then_inc(k1_rounded, 1)
                elif kind == "place_k1":
                    g, j = step[1:]
                    wait_moved(act, ("k1", g))
                    act.wait_ge(loaded["const"], 16 * N_CONST)
                    k = k_stack[:, g % 2, :].bitcast(F32).rearrange("p (b c) -> p b c", b=B)
                    act.mul(k1[:, :, g, j, :], k[:, :, 0:CTX], head_rows[:, j:j + 1]).then_inc(k1_placed, 1)
                elif kind == "q1":
                    b, g = step[1:]
                    wait_filled(act, step)
                    if (b, g) == (0, 0):
                        wait_moved(act, ("k1", G1 - 2))
                        wait_moved(act, ("k1", G1 - 1))
                    if g >= 2:
                        wait_moved(act, ("q1", b, g - 2))
                    elif b == 1:
                        wait_moved(act, ("q1", 0, g + 2))
                    act.copy(rounded[:, g % 2, :], bank(step)).then_inc(q1_rounded, 1)
                elif kind == "mT":
                    b = step[1]
                    wait_filled(act, step)
                    if b == 1:
                        act.wait_ge(nm_placed[0], 16 * 8)
                    act.copy(nmT_hi[:, :], bank(step)[0:H1, :]).then_inc(nm_rounded, 1)
                elif kind == "expT":
                    b, g, j = step[1:]
                    wait_filled(act, step)
                    n = b * G1 + g
                    if n >= 2:
                        wait_filled(act, ("pv1", (n - 2) // G1, (n - 2) % G1))
                    else:
                        wait_filled(act, ("y", 1, 1))
                    moved(act.activation(probT1[:, n % 2, j, :], bank(step), ACT.Exp, scale=HEAD_SCALE1), step)
                elif kind == "onT":
                    b = step[1]
                    wait_filled(act, step)
                    if b == 1:
                        wait_filled(act, ("wo1", 0))
                    moved(act.copy(onT[:, :], bank(step)), step)

        @block.vector
        def _(dve):
            steps = [0]

            def chain(ins):
                ins.then_inc(dve_step, 1)
                steps[0] += 1
                dve.wait_ge(dve_step, steps[0])

            def note(ins):
                ins.then_inc(dve_step, 1)
                steps[0] += 1

            def settle():
                dve.wait_ge(dve_step, steps[0])

            for step in order_of("DVE", order):
                kind = step[0]
                if kind == "lnA":
                    s, b = step[1:]
                    if s == 0:
                        dve.wait_ge(loaded[f"x{b}"], 16)
                    settle()
                    for t in range(T):
                        note(dve.bn_stats(stats[:, b, t, :], X[:, b * T + t, :]))
                    settle()
                    for t in range(T):
                        note(dve.bn_aggr(mv[:, b, t, :], stats[:, b, t, :]))
                    settle()
                    dve.tensor_scalar(vareps[:, b, :], mv[:, b, :, 1], EPS, None, ALU.add).then_inc(var_ready, 1)
                elif kind == "lnB":
                    s, b = step[1:]
                    dve.wait_ge(rstd_ready, position[("lnA", s, b)])
                    for t in range(T):
                        ins = dve.tensor_scalar(xn[:, b, t, :], X[:, b * T + t, :], mv[:, b, t, 0:1], rstd[:, b, t:t + 1],
                                                ALU.subtract, ALU.mult)
                    ins.then_inc(xn_ready, 1)
                elif kind == "xT":
                    b = step[2]
                    dve.wait_ge(xT_rounded, position[step])
                    moved(dve.tensor_tensor(xT_lo[:, b, :], bank(step), xT_hi[:, b, :].bitcast(F32), ALU.subtract), step)
                elif kind == "kT":
                    p = step[1]
                    dve.wait_ge(cleared0, 3)
                    for j in range(2):
                        dve.wait_ge(kT_rounded, 2 * p + j + 1)
                        rows = slice(64 * j, 64 * j + 64)
                        ins = dve.tensor_tensor(
                            k_lo[rows, p, :, j, :], bank(step)[rows, 0:B * CP].rearrange("p (b c) -> p b c", b=B),
                            k_hi[rows, p, :, j, :].bitcast(F32), ALU.subtract)
                    moved(ins, step)
                elif kind == "q":
                    b, p = step[1:]
                    dve.wait_ge(q_rounded, position[step])
                    moved(dve.scalar_tensor_tensor(q_lo[:, b, p, :], bank(step), HEAD_SCALE0,
                                                   q_hi[:, b, p, :].bitcast(F32), ALU.mult, ALU.subtract), step)
                elif kind in ("vf", "vf1"):
                    b = step[1]
                    wait_filled(dve, step)
                    moved(dve.tensor_copy((v0 if kind == "vf" else v1)[:, b, :], bank(step)), step)
                elif kind in ("vs", "vs1"):
                    b = step[1]
                    wait_filled(dve, step)
                    dve.wait_ge(loaded["const"], 16 * N_CONST)
                    if kind == "vs":
                        dst = vs0[:, b, :, :].rearrange("p (g q) c -> p g q c", q=2)
                        src = bank(step).rearrange("p (g q c) -> p g q c", g=2, q=2)
                        mask = vs0_mask[:, :, :].unsqueeze(1).broadcast_to((P, 2, 2, P))
                    else:
                        dst = vs1[:, b, :, :]
                        src = bank(step).rearrange("p (g c) -> p g c", g=G1)
                        mask = vs1_mask[:, :].unsqueeze(1).broadcast_to((P, G1, P))
                    moved(dve.tensor_tensor(dst, src, mask, ALU.mult), step)
                elif kind == "score":
                    b, t, p = step[1:]
                    wait_filled(dve, step)
                    dve.tensor_reduce(neg_max0[:, b, t, 2 * p:2 * p + 2],
                                      bank(step)[:, 0:2 * CTX].rearrange("p (j c) -> p j c", j=2), AX, ALU.max, negate=True)\
                        .then_inc(negmax_ready, 1)
                elif kind == "norm":
                    b, t = step[1:]
                    for p in range(PAIRS):
                        wait_moved(dve, ("score", b, t, p))
                    dve.reciprocal(row_inv[:, b, t, :], row_sum[:, b, t, :]).then_inc(rowinv_ready, 1)
                elif kind == "pT" and step[3] < 2:
                    b, t, k = step[1:]
                    wait_filled(dve, step)
                    if b == 1 and t == 0:
                        wait_filled(dve, ("pv", 0, PAIRS - 1))
                    moved(dve.tensor_copy(probT0[:, 4 * k:4 * k + 4, t * P:(t + 1) * P],
                                          bank(step).rearrange("p (h n) -> p h n", h=4)), step)
                elif kind in ("wo", "wo1", "res"):
                    b = step[-1]
                    key = ("y" if step[1] == 1 else "yT",) + step[1:] if kind == "res" else step
                    wait_filled(dve, key)
                    if kind == "wo":
                        dve.wait_ge(bo_added, position[("bo", b)])
                    xb = X[:, b * T:(b + 1) * T, :]
                    settle()
                    moved(dve.tensor_tensor(xb, bank(key).rearrange("p (t d) -> p t d", t=T), xb, ALU.add), key)
                    wait_moved(dve, key)
                elif kind == "hsplit":
                    n = hid_index[step[1:]]
                    m = n - first_split
                    dve.wait_ge(hid_rounded, m + 1)
                    dve.tensor_tensor(hid_lo[:, m % 2, :], hid[:, n % HIDS, :], hid_hi[:, m % 2, :].bitcast(F32), ALU.subtract)\
                        .then_inc(hid_split, 1)
                elif kind == "gate" and step[1] == 3:
                    b = step[2]
                    wait_filled(dve, step)
                    dve.wait_ge(loaded["const"], 16 * N_CONST)
                    settle()
                    moved(dve.tensor_tensor(cand[:, :, 0:E1], bank(step)[:, 0:T * E1].rearrange("p (t e) -> p t e", t=T),
                                            gate_bias[:, :].unsqueeze(1).broadcast_to((P, T, E1)), ALU.add), step)
                    wait_moved(dve, step)
                elif kind == "route":
                    s, b, part = step[1:]
                    if s == 1 and part == 0:
                        wait_moved(dve, ("gate", s, b))
                        dve.wait_ge(loaded["const"], 16 * N_CONST)
                        chain(dve.tensor_scalar(e_neg[:, :, :], e_neg[:, :, :], 1.0, None, ALU.add))
                        chain(dve.reciprocal(sc[:, :, :], e_neg[:, :, :]))
                        quad = sc[:, :, :].rearrange("p t (g h w) -> p (t g) h w", g=NG, w=2)
                        note(dve.tensor_tensor(pair_max[:, :, :], quad[:, :, :, 0], quad[:, :, :, 1], ALU.max))
                        note(dve.tensor_tensor(pair_sum[:, :, :], quad[:, :, :, 0], quad[:, :, :, 1], ALU.add))
                        settle()
                        gs = g_score[:, :, :].rearrange("p t g -> p (t g)")
                        gc = g_cross[:, :, :].rearrange("p t g -> p (t g)")
                        note(dve.tensor_tensor(gc, pair_max[:, :, 0], pair_max[:, :, 1], ALU.add))
                        note(dve.tensor_tensor(gs, pair_sum[:, :, 0], pair_sum[:, :, 1], ALU.max))
                        settle()
                        chain(dve.tensor_tensor(gs, gs, gc, ALU.max))
                    elif s == 1 and part == 1:
                        own = g_score[:, :, :].unsqueeze(3).broadcast_to((P, T, NG, NG))
                        other = g_score[:, :, :].unsqueeze(2).broadcast_to((P, T, NG, NG))
                        bt = beats[:, :, :].rearrange("p (t g) h -> p t g h", t=T)
                        ti = ties[:, :, :].rearrange("p (t g) h -> p t g h", t=T)
                        first = lower_first[:, :, :].unsqueeze(1).broadcast_to((P, T, NG, NG))
                        note(dve.tensor_tensor(bt, other, own, ALU.is_gt))
                        note(dve.tensor_tensor(ti, other, own, ALU.is_equal))
                        settle()
                        chain(dve.tensor_tensor(ti, ti, first, ALU.mult))
                        chain(dve.tensor_tensor(beats[:, :, :], beats[:, :, :], ties[:, :, :], ALU.add))
                    elif s == 1 and part == 2:
                        settle()
                        chain(dve.tensor_reduce(rank[:, :, :].rearrange("p t g -> p (t g)"), beats[:, :, :], AX, ALU.add))
                        chain(dve.tensor_scalar(allowed[:, :, :], rank[:, :, :], 2.0, None, ALU.is_lt))
                        note(dve.tensor_scalar(penalty[:, :, :], allowed[:, :, :], -1.0, None, ALU.add))
                        wide = lambda x: x[:, :, :].unsqueeze(3).broadcast_to((P, T, NG, E0 // NG))
                        cg = cand[:, :, 0:E0].rearrange("p t (g e) -> p t g e", g=NG)
                        chain(dve.tensor_tensor(cg, sc[:, :, :].rearrange("p t (g e) -> p t g e", g=NG), wide(allowed), ALU.mult))
                        note(dve.tensor_tensor(cg, cg, wide(penalty), ALU.add))
                    n_e, topk, sentinel, gone = (E0, TOPK0, -2.0, -3.0) if s == 1 else (E1, TOPK1, -3.0e38, -3.2e38)
                    last = ROUTE_PARTS[s] - 1
                    if part == last - 1:
                        settle()
                        note(dve.memset(cand[:, :, n_e:n_e + 8], sentinel))
                        settle()
                        for t in range(T):
                            note(dve.max(top[:, t, :], cand[:, t, 0:n_e]))
                        settle()
                        if s == 3:
                            dve.tensor_tensor(diff[:, :, :], cand[:, :, 0:E1], top[:, :, 0:1].broadcast_to((P, T, E1)), ALU.subtract)\
                                .then_inc(diff_ready, 1)
                        note(dve.memset(top[:, :, topk:8], sentinel))
                        settle()
                        for t in range(T):
                            note(dve.match_replace(replaced[:, t, 0:n_e + 8], top[:, t, :], cand[:, t, 0:n_e + 8], gone))
                        settle()
                    if part == last:
                        settle()
                        chain(dve.tensor_tensor(chosen[:, :, 0:n_e], replaced[:, :, 0:n_e], cand[:, :, 0:n_e], ALU.not_equal))
                        if s == 3:
                            dve.wait_ge(e_diff_ready, b + 1)
                        weight = sc[:, :, :] if s == 1 else e_diff[:, :, :]
                        chain(dve.tensor_tensor(w_un[:, :, 0:n_e], weight, chosen[:, :, 0:n_e], ALU.mult))
                        chain(dve.tensor_reduce(w_sum[:, :], w_un[:, :, 0:n_e], AX, ALU.add))
                        if s == 1:
                            chain(dve.tensor_scalar(w_sum[:, :], w_sum[:, :], 1e-6, None, ALU.add))
                        chain(dve.reciprocal(w_inv[:, :], w_sum[:, :]))
                        dve.tensor_tensor(cw[:, b, :, 0:n_e], w_un[:, :, 0:n_e],
                                          w_inv[:, :].unsqueeze(2).broadcast_to((P, T, n_e)), ALU.mult).then_inc(cw_ready, 1)
                        dve.wait_ge(cw_ready, position[("cwT", s, b)])
                elif kind == "h3":
                    s, b, i = step[1:]
                    n = hid_index[step[1:]]
                    key = step
                    if n >= 2:
                        dve.wait_ge(hid_ready, n - 1)
                    wait_filled(dve, key)
                    if i < N_SHARED[s]:
                        ins = dve.tensor_copy(gated_u[:, n % 2, :], bank(key))
                    else:
                        slot = slot_of(s, i)
                        dve.wait_ge(spread_loaded[slot // 2], spread_count(s, b))
                        ins = dve.tensor_tensor(gated_u[:, n % 2, :], bank(key), spread[:, slot, :], ALU.mult)
                    moved(ins, key)
                elif kind == "k1":
                    g = step[1]
                    dve.wait_ge(k1_rounded, g + 1)
                    if g >= 2:
                        dve.wait_ge(k1_placed, 4 * (g - 1))
                        dve.wait_ge(k1s_placed, g - 1)
                    else:
                        dve.wait_ge(lo_of["wq1"], 1)
                    moved(dve.scalar_tensor_tensor(k_stack[:, g % 2, :], rounded[:, g % 2, 0:B * CP].bitcast(F32), lo_rows[:, 1:2],
                                                   bank(step)[:, 0:B * CP], ALU.mult, ALU.add), step)
                elif kind == "q1":
                    b, g = step[1:]
                    dve.wait_ge(q1_rounded, position[step])
                    moved(dve.scalar_tensor_tensor(q1[:, b, g, :], rounded[:, g % 2, :].bitcast(F32), lo_rows[:, 0:1],
                                                   bank(step), ALU.mult, ALU.add), step)
                elif kind == "score1":
                    b, t, g, half = step[1:]
                    wait_filled(dve, step)
                    moved(dve.tensor_reduce(neg_max1[:, b, t, 2 * half:2 * half + 2, g],
                                            bank(step)[:, 0:2 * CTX].rearrange("p (j c) -> p j c", j=2), AX, ALU.max, negate=True),
                          step)
                elif kind == "mT":
                    b = step[1]
                    dve.wait_ge(nm_rounded, b + 1)
                    moved(dve.tensor_tensor(nmT_lo[:, :], bank(step)[0:H1, :], nmT_hi[:, :].bitcast(F32), ALU.subtract), step)
                elif kind == "pv1":
                    b, g = step[1:]
                    wait_filled(dve, step)
                    if b * G1 + g >= 2:
                        n = b * G1 + g - 2
                        wait_filled(dve, ("oT", n // G1, n % G1))
                    dve.wait_ge(k1_placed, 4 * G1)
                    dve.wait_ge(k1s_placed, G1)
                    moved(dve.tensor_copy(od[:, g % 2, :], bank(step)), step)
                elif kind == "oT":
                    b, g = step[1:]
                    wait_filled(dve, step)
                    if b == 1 and g == 0:
                        wait_filled(dve, ("onT", 0))
                    v = bank(step).rearrange("p (t j c) -> p t j c", t=T, j=4)
                    settle()
                    chain(dve.reciprocal(den_inv[:, g % 2, :, :], v[:, :, :, DH1]))
                    moved(dve.tensor_tensor(on[:, :, g * 32:(g + 1) * 32].rearrange("p t (j c) -> p t j c", j=4),
                                            v[:, :, :, 0:DH1],
                                            den_inv[:, g % 2, :, :].unsqueeze(3).broadcast_to((P, T, 4, DH1)), ALU.mult), step)

        @block.tensor
        def _(pe):
            def product3(dst, w_hi, w_lo, m_hi, m_lo):
                pe.matmul(dst, w_hi, m_hi, start=True, stop=False)
                pe.matmul(dst, w_hi, m_lo, start=False, stop=False)
                return pe.matmul(dst, w_lo, m_hi, start=False, stop=True)

            for step in order_of("PE", order):
                kind = step[0]
                if step in uses:
                    wait_bank_free(pe, step)
                if kind == "kT":
                    p = step[1]
                    pe.wait_ge(loaded["ctx"], 32)
                    filled(pe.matmul(bank(step)[:, 0:B * CP], wk0[:, p * P:(p + 1) * P],
                                     ctxT[0:CD, :, :].rearrange("k b c -> k (b c)"), start=True, stop=True), step)
                elif kind in ("vf", "vf1", "vs", "vs1"):
                    b = step[1]
                    if kind in ("vf", "vs"):
                        pe.wait_ge(loaded["ctx"], 32)
                        pe.wait_ge(loaded["ctxv"], 32)
                        w, k = wv0[:, :], CD
                    else:
                        pe.wait_ge(loaded["wqkv1"], 64)
                        w, k = wv1[:, :], CD + 1
                    rows = ctxT[0:k, b, 0:P] if kind in ("vf", "vf1") else ctxT_rest[0:k, b, :]
                    filled(pe.matmul(bank(step), rows, w, start=True, stop=True), step)
                elif kind == "xT":
                    s, b = step[1:]
                    pe.wait_ge(loaded["ident"], 16)
                    pe.wait_ge(xn_ready, position[step])
                    for t in range(T):
                        ins = pe.transpose(bank(step)[:, t * P:(t + 1) * P], xn[:, b, t, :], ident[:, :])
                    filled(ins, step)
                elif kind == "q":
                    b, p = step[1:]
                    pe.wait_ge(lo_of["wq0"], 1)
                    wait_moved(pe, ("xT", 0, b))
                    c = slice(p * P, (p + 1) * P)
                    filled(product3(bank(step), wq_hi0[:, c], wq_lo0[:, c], xT_hi[:, b, :], xT_lo[:, b, :]), step)
                elif kind == "score":
                    b, t, p = step[1:]
                    wait_moved(pe, ("q", b, p))
                    wait_moved(pe, ("kT", p))
                    c = slice(t * P, (t + 1) * P)
                    dst = bank(step)[:, 0:2 * CTX].rearrange("p (j c) -> p j c", j=2)
                    filled(product3(dst, q_hi[:, b, p, c], q_lo[:, b, p, c], k_hi[:, p, b, :, 0:CTX], k_lo[:, p, b, :, 0:CTX]), step)
                elif kind == "pT":
                    b, t, k = step[1:]
                    r = (b * T + t) % 2
                    pe.wait_ge(prob_normed, position[("norm", b, t)])
                    for m in range(4 if k < 2 else 2):
                        at = (4 * k + m) * P if k < 2 else H0 * P + 4 * m * PAD
                        src = prob_n[:, r, at:at + P]
                        ins = pe.transpose(bank(step)[:, m * P:(m + 1) * P], src, ident[:, :])
                    filled(ins, step)
                elif kind == "pv":
                    b, p = step[1:]
                    for k in range(3):
                        wait_moved(pe, ("pT", b, T - 1, k))
                    wait_moved(pe, ("vf", b))
                    wait_moved(pe, ("vs", b))
                    pe.matmul(bank(step), vs0[:, b, p, :], probT0[:, H0 + p // 2, :], start=True, stop=False, skip_group_check=True)
                    for j in range(2):
                        h = 2 * p + j
                        ins = pe.matmul(bank(step)[64 * j:64 * j + 64, :], v0[:, b, h * DH0:(h + 1) * DH0], probT0[:, h, :],
                                        start=False, stop=True, skip_group_check=True)
                    filled(ins, step)
                elif kind == "wo":
                    b = step[1]
                    pe.wait_ge(loaded["wo0"], 16)
                    for p in range(PAIRS):
                        wait_moved(pe, ("pv", b, p))
                        for t in range(T):
                            ins = pe.matmul(bank(step)[:, t * P:(t + 1) * P], outT0[:, p, t * P:(t + 1) * P], wo0[:, p, :],
                                            start=(p == 0 and t == 0), stop=(p == PAIRS - 1), skip_group_check=True)
                    filled(ins, step)
                elif kind == "gate":
                    s, b = step[1:]
                    wait_moved(pe, ("xT", s, b))
                    pe.wait_ge(lo_of["gates"], 1)
                    n_e = EXPERTS[s]
                    c = slice(0, E0) if s == 1 else slice(E0, E0 + E1)
                    for t in range(T):
                        x = slice(t * P, (t + 1) * P)
                        ins = product3(bank(step)[:, t * n_e:(t + 1) * n_e], xT_hi[:, b, x], xT_lo[:, b, x],
                                       gates_hi[:, c], gates_lo[:, c])
                    filled(ins, step)
                elif kind == "cwT":
                    s, b = step[1:]
                    pe.wait_ge(cw_ready, position[step])
                    for t in range(T):
                        ins = pe.transpose(bank(step)[0:EXPERTS[s], t * P:(t + 1) * P], cw[:, b, t, 0:EXPERTS[s]], ident[:, :])
                    filled(ins, step)
                elif kind in ("h1", "h3"):
                    s, b, i = step[1:]
                    hi, lo, name = w13[s]
                    w = 2 * i + (kind == "h3")
                    wait_moved(pe, ("xT", s, b))
                    pe.wait_ge(lo_of[name], w // CHUNK + 1)
                    filled(product3(bank(step), hi[:, w, :], lo[:, w, :], xT_hi[:, b, :], xT_lo[:, b, :]), step)
                elif kind == "down":
                    s, b, i = step[1:]
                    n = hid_index[(s, b, i)]
                    key = ("y", s, b)
                    if i == 0:
                        wait_bank_free(pe, key)
                    last = i == N_HID[s] - 1
                    if s == 1:
                        pe.wait_ge(loaded["w2_0"], 16)
                        pe.wait_ge(hid_ready, n + 1)
                        for t in range(T):
                            ins = pe.matmul(bank(key)[:, t * P:(t + 1) * P], hid[:, n % HIDS, t * P:(t + 1) * P], w2_0[:, i, :],
                                            start=(i == 0 and t == 0), stop=last, skip_group_check=True)
                    else:
                        pe.wait_ge(lo_of["w2_1"], i // CHUNK + 1)
                        m = n - first_split
                        pe.wait_ge(hid_split, m + 1)
                        pe.matmul(bank(key), w2_hi1[:, i, :], hid_hi[:, m % 2, :], start=(i == 0), stop=False)
                        pe.matmul(bank(key), w2_lo1[:, i, :], hid_hi[:, m % 2, :], start=False, stop=False)
                        ins = pe.matmul(bank(key), w2_hi1[:, i, :], hid_lo[:, m % 2, :], start=False, stop=last)
                    if last:
                        filled(ins, key)
                    else:
                        ins.then_inc(hid_used, 1)
                elif kind == "yT":
                    wait_moved(pe, ("y",) + step[1:])
                    for t in range(T):
                        ins = pe.transpose(bank(step)[:, t * P:(t + 1) * P], yT[:, t * P:(t + 1) * P], ident[:, :])
                    filled(ins, step)
                elif kind == "k1":
                    g = step[1]
                    pe.wait_ge(loaded["wqkv1"], 64)
                    filled(pe.matmul(bank(step)[:, 0:B * CP], wk1[:, g, :], ctxT[:, :, :].rearrange("k b c -> k (b c)"),
                                     start=True, stop=True), step)
                elif kind == "q1":
                    b, g = step[1:]
                    wait_moved(pe, ("xT", 2, b))
                    pe.wait_ge(lo_of["wq1"], 1)
                    c = slice(g * P, (g + 1) * P)
                    filled(product3(bank(step), wq_hi1[:, c], wq_lo1[:, c], xT_hi[:, b, :], xT_lo[:, b, :]), step)
                elif kind == "score1":
                    b, t, g, half = step[1:]
                    wait_moved(pe, ("q1", b, g))
                    pe.wait_ge(k1_placed, 4 * (g + 1))
                    filled(pe.matmul(bank(step)[:, 0:2 * CTX].rearrange("p (j c) -> p j c", j=2), q1[:, b, g, t * P:(t + 1) * P],
                                     k1[:, b, g, 2 * half:2 * half + 2, 0:CTX], start=True, stop=True), step)
                elif kind == "mT":
                    b = step[1]
                    for g in range(G1):
                        for half in range(2):
                            wait_moved(pe, ("score1", b, T - 1, g, half))
                    for t in range(T):
                        ins = pe.transpose(bank(step)[0:H1, t * P:(t + 1) * P],
                                           neg_max1[:, b, t, :, :].rearrange("p j g -> p (j g)"), ident[:, :])
                    filled(ins, step)
                elif kind == "expT":
                    b, g, j = step[1:]
                    pe.wait_ge(nm_placed[b], 16 * 8)
                    pe.wait_ge(k1s_placed, g + 1)
                    w = k1[:, b, g, j, 0:P] if j < 4 else k1s[:, b, g, :, :].rearrange("p j c -> p (j c)")
                    filled(pe.matmul(bank(step), w, q1[:, b, g, :], start=True, stop=True), step)
                elif kind == "pv1":
                    b, g = step[1:]
                    r = (b * G1 + g) % 2
                    wait_moved(pe, ("vf1", b))
                    wait_moved(pe, ("vs1", b))
                    wait_moved(pe, ("expT", b, g, 4))
                    pe.matmul(bank(step), vs1[:, b, g, :], probT1[:, r, 4, :], start=True, stop=False, skip_group_check=True)
                    for j in range(4):
                        wait_moved(pe, ("expT", b, g, j))
                        rows = slice(PAD * j, PAD * j + PAD)
                        ins = pe.matmul(bank(step)[rows, :], v1[:, b, g * P + PAD * j:g * P + PAD * (j + 1)], probT1[:, r, j, :],
                                        start=False, stop=True, skip_group_check=True, tile_position=(0, PAD * j))
                    filled(ins, step)
                elif kind == "oT":
                    b, g = step[1:]
                    wait_moved(pe, ("pv1", b, g))
                    for t in range(T):
                        ins = pe.transpose(bank(step)[:, t * P:(t + 1) * P], od[:, g % 2, t * P:(t + 1) * P], ident[:, :])
                    filled(ins, step)
                elif kind == "onT":
                    b = step[1]
                    wait_moved(pe, ("oT", b, G1 - 1))
                    wait_moved(pe, ("oT", b, G1 - 2))
                    for t in range(T):
                        ins = pe.transpose(bank(step)[:, t * P:(t + 1) * P], on[:, t, :], ident[:, :])
                    filled(ins, step)
                elif kind == "wo1":
                    b = step[1]
                    wait_moved(pe, ("onT", b))
                    for t in range(T):
                        ins = pe.matmul(bank(step)[:, t * P:(t + 1) * P], onT[:, t * P:(t + 1) * P], wo1[:, :],
                                        start=(t == 0), stop=True, skip_group_check=True)
                    filled(ins, step)


def lay_out(x, ctx_768, L0_xattn_Wq, L0_xattn_Wk, L0_xattn_Wv, L0_xattn_Wo, L0_xattn_bo, L0_ffn_w_gate, L0_ffn_w1_e,
            L0_ffn_w3_e, L0_ffn_w2_e, L0_ffn_w1_s, L0_ffn_w3_s, L0_ffn_w2_s, L1_xattn_Wq, L1_xattn_Wk, L1_xattn_Wv,
            L1_xattn_Wo, L1_ffn_router_w, L1_ffn_experts_bias, L1_ffn_w1, L1_ffn_w3, L1_ffn_w2, L1_ffn_sw1, L1_ffn_sw3,
            L1_ffn_sw2):
    f = np.float32
    d = {}
    d["x"] = x.reshape(B * T, P, P).transpose(1, 0, 2)
    ctxT = np.ones((CD + 1, B, CP), f)
    ctxT[:CD, :, :CTX] = ctx_768.transpose(2, 0, 1)
    ctxT[:CD, :, CTX:] = ctxT[:CD, :, CTX - 1:CTX]
    d["ctxT"] = ctxT
    d["ctxT_rest"] = np.tile(ctxT[:, :, P:], (1, 1, 4))
    d["wq0"], d["wk0"], d["wv0"] = L0_xattn_Wq, L0_xattn_Wk, L0_xattn_Wv
    d["wo0"] = L0_xattn_Wo.reshape(PAIRS, P, P).transpose(1, 0, 2)
    d["bo"] = np.broadcast_to(L0_xattn_bo, (P, P))
    d["gates"] = np.concatenate([L0_ffn_w_gate.T, L1_ffn_router_w.T], axis=1)
    d["gate_bias"] = np.broadcast_to(L1_ffn_experts_bias, (P, E1))
    d["ident"] = np.eye(P, dtype=f)
    d["lower_first"] = np.broadcast_to(np.tril(np.ones((NG, NG), f), -1), (P, NG, NG))
    lo_rows = np.zeros((4, PAD, 2), f)
    lo_rows[:, DH1:2 * DH1, 0] = -1.0
    lo_rows[:, 2 * DH1:3 * DH1, 1] = -1.0
    d["lo_rows"] = lo_rows.reshape(P, 2)

    row = np.arange(P)
    real = (row % PAD < REST)[:, None]
    d["vs0_mask"] = np.stack([real & (row[:, None] // PAD == 2 * q + row // DH0) for q in range(2)], axis=1).astype(f)
    d["vs1_mask"] = (real & (row[:, None] // PAD == row // PAD)).astype(f)
    d["head_rows"] = (row[:, None] // PAD == np.arange(4)).astype(f)

    def hidden(shared1, shared3, expert1, expert3):
        w = [np.concatenate(pair, axis=1).reshape(P, -1, P) for pair in ((shared1, expert1), (shared3, expert3))]
        return np.stack(w, axis=2).reshape(P, -1, P)

    d["w13_0"] = hidden(L0_ffn_w1_s.T, L0_ffn_w3_s.T, L0_ffn_w1_e.transpose(2, 0, 1).reshape(P, -1),
                        L0_ffn_w3_e.transpose(2, 0, 1).reshape(P, -1))
    d["w2_0"] = np.concatenate([L0_ffn_w2_s.T, L0_ffn_w2_e.transpose(0, 2, 1).reshape(-1, P)]).reshape(-1, P, P).transpose(1, 0, 2)
    d["w13_1"] = hidden(L1_ffn_sw1[0], L1_ffn_sw3[0], L1_ffn_w1.transpose(1, 0, 2).reshape(P, -1),
                        L1_ffn_w3.transpose(1, 0, 2).reshape(P, -1))
    d["w2_1"] = np.concatenate([L1_ffn_sw2[0], L1_ffn_w2.reshape(-1, P)]).reshape(-1, P, P).transpose(1, 0, 2)

    def groups(w, copies, ones_at):
        rows = w.shape[0] + (1 if ones_at else 0)
        g = np.zeros((rows, H1, PAD), f)
        for r in range(copies):
            g[:w.shape[0], :, r * DH1:(r + 1) * DH1] = w.reshape(w.shape[0], H1, DH1)
        for c in ones_at:
            g[-1, :, c] = 1.0
        return g.reshape(rows, G1 * P)

    d["wq1"] = groups(L1_xattn_Wq, 3, ())
    d["wk1"] = groups(L1_xattn_Wk, 3, (3 * DH1, 3 * DH1 + 1)).reshape(CD + 1, G1, P)
    d["wv1"] = groups(L1_xattn_Wv, 1, (DH1,))
    d["wo1"] = L1_xattn_Wo
    return {k: np.ascontiguousarray(v) for k, v in d.items()}


def kernel(**inputs):
    import concourse.bacc as bacc
    from concourse.bass_utils import run_bass_kernel_spmd

    nc = bacc.Bacc("TRN2", target_bir_lowering=False, num_devices=1)
    arrays = {"in_" + k: v for k, v in lay_out(**{k: np.asarray(v) for k, v in inputs.items()}).items()}
    aps = {k[3:]: nc.dram_tensor(k, v.shape, mybir.dt.from_np(v.dtype), kind="ExternalInput").ap() for k, v in arrays.items()}
    out = nc.dram_tensor(OUT_NAME, (P, B * T, P), F32, kind="ExternalOutput").ap()
    build(nc, aps, out)
    got = run_bass_kernel_spmd(nc, [arrays], core_ids=[0]).results[0][OUT_NAME]
    return got.transpose(1, 0, 2).reshape(B, TOK, P)
```

```python
from contextlib import ExitStack

import numpy as np

import concourse.bass as bass
from concourse import mybir

F32 = mybir.dt.float32
F32R = mybir.dt.float32r
ACT = mybir.ActivationFunctionType
ALU = mybir.AluOpType
AX = mybir.AxisListType.X

P = 128
B = 2
T = 4
TOK = T * P
CTX, CD = 154, 96
REST = CTX - P
PAD = 32
CP = P + PAD
EPS = 1e-5

H0, DH0 = 8, 64
PAIRS = H0 // 2
H1, DH1 = 16, 8
G1 = H1 // 4
E0, F0 = 16, 64
E1, F1 = 8, 256
NG, TOPK0, TOPK1 = 4, 4, 2
N_HID = {1: 1 + E0 * F0 // P, 3: 2 + E1 * F1 // P}
N_SHARED = {1: 1, 3: 2}
EXPERTS = {1: E0, 3: E1}
SLOTS = 8
HIDS = 4
CHUNK = 6
ROUTE_PARTS = {1: 4, 3: 2}
OUT_NAME = "out"


def all_steps():
    batches, groups = range(B), range(G1)
    per_batch = lambda kind: [(kind, b) for b in batches]
    per_sublayer = lambda kind, subs: [(kind, s, b) for s in subs for b in batches]
    hidden = lambda kind, subs: [(kind, s, b, i) for s in subs for b in batches for i in range(N_HID[s])]
    chunks = lambda name, tiles: [("split", name, c) for c in range(tiles // CHUNK)]
    steps = [("split", "wq0", 0), ("split", "gates", 0)] + chunks("w13_0", 2 * N_HID[1])
    steps += [("split", "wq1", 0)] + chunks("w13_1", 2 * N_HID[3]) + chunks("w2_1", N_HID[3])
    for kind in ("lnA", "lnB", "xT"):
        steps += per_sublayer(kind, (0, 1, 2, 3))
    steps += [("kT", p) for p in range(PAIRS)]
    for kind in ("q", "pv"):
        steps += [(kind, b, p) for b in batches for p in range(PAIRS)]
    for kind in ("vf", "vs", "wo", "bo"):
        steps += per_batch(kind)
    steps += [("score", b, t, p) for b in batches for t in range(T) for p in range(PAIRS)]
    steps += [("norm", b, t) for b in batches for t in range(T)]
    steps += [("pT", b, t, k) for b in batches for t in range(T) for k in range(3)]
    for kind in ("gate", "cwT", "res"):
        steps += per_sublayer(kind, (1, 3))
    steps += [("route", s, b, part) for s in (1, 3) for b in batches for part in range(ROUTE_PARTS[s])]
    for kind in ("h1", "h3", "down"):
        steps += hidden(kind, (1, 3))
    steps += hidden("hsplit", (3,)) + per_sublayer("ycopy", (3,)) + per_sublayer("yT", (3,))
    for kind in ("k1", "place_k1s"):
        steps += [(kind, g) for g in groups]
    steps += [("place_k1", g, j) for g in groups for j in range(4)]
    for kind in ("vf1", "vs1", "mT", "onT", "wo1"):
        steps += per_batch(kind)
    for kind in ("q1", "pv1", "oT"):
        steps += [(kind, b, g) for b in batches for g in groups]
    steps += [("score1", b, t, g, half) for b in batches for t in range(T) for g in groups for half in range(2)]
    steps += [("expT", b, g, j) for b in batches for g in groups for j in range(5)]
    return steps


PROGRAM = {
    "PE":
        "kT kT xT kT kT xT q q vf score q q score vf q score score vs q " + 3 * "score " + "vs " +
        2 * "score q score " + "score " + 2 * "pT score score pT " + 3 * "score pT " + 2 * "pT score score " +
        3 * "pT score " + "score pv pv pv score score pT pv pT score score wo pT score " + 5 * "pT " +
        "xT pT pT pT h3 gate pT h1 h1 pv pv pv cwT pv h3 h3 wo h1 h1 down h1 h1 h3 down xT vs1 k1 h3 h3 gate h3 h3 "
        "k1 h1 h1 " + 4 * "down " + "h3 h3 h1 h1 cwT " + 3 * "down " +
        "h1 h1 down vs1 h3 k1 k1 h3 h3 h3 xT vf1 h3 h3 q1 q1 h1 h1 q1 q1 " + 3 * "down " + 3 * "score1 " + "down " +
        4 * "score1 score1 h1 " + "score1 " + 2 * "score1 h3 score1 score1 down " + 2 * "score1 down score1 score1 " +
        8 * "score1 " + "xT mT vf1 q1 q1 q1 q1 " + 6 * "score1 " + 4 * "expT score1 " + 3 * "score1 " +
        4 * "expT score1 " + "score1 pv1 " + 3 * "score1 " + 4 * "expT " + 4 * "score1 expT " + "score1 " +
        3 * "score1 expT " + 3 * "score1 " + "pv1 mT oT pv1 expT oT pv1 oT oT onT " + 4 * "expT " + "wo1 " +
        5 * "expT " + "pv1 " + 6 * "expT " +
        "xT expT expT oT expT expT pv1 gate expT pv1 h1 h1 h1 cwT h3 h3 pv1 h1 oT oT h3 h3 h3 oT h3 down h1 onT "
        "down h3 h3 h1 h1 h1 wo1 down down h1 h3 h3 h1 h1 down down h3 xT h3 down h3 h1 gate h1 down h1 h1 down h3 "
        "h3 down cwT h3 h3 h3 " + 2 * "h1 down down h1 " + "h1 down h3 h3 h3 h3 down down h1 h1 h1 h1 " +
        2 * "down h3 h3 " +
        "down h1 down h1 h1 down down h3 h3 down h3 down h1 down h1 h1 h1 down h3 h3 down h1 h1 down h3 h3 h3 down "
        "h1 h3 h1 down down h3 h1 down yT " + 3 * "down " + "yT ",
    "ACT":
        "split kT kT split xT kT kT xT q split q split split q q " + 3 * "score q score score " + "q " + 4 * "score " +
        3 * "pT score score score " + "score pT " + 4 * "score " + "pv pv " + 2 * "pv score score " +
        "pT score pT xT pT gate pT h1 h1 pv pv pv cwT pv h1 h1 split h1 xT split h1 split split k1 gate place_k1 "
        "place_k1 k1 place_k1 place_k1 h1 h1 h1 h1 cwT place_k1 " + 3 * "split " +
        "place_k1 h1 h1 place_k1 place_k1 k1 k1 " + 4 * "place_k1 " + "xT " + 4 * "place_k1 " + 2 * "q1 q1 h1 h1 " +
        "h1 h1 xT mT q1 q1 q1 q1 " + 16 * "expT " + "mT " + 4 * "expT " + 3 * "split " + "onT " + 14 * "expT " + "xT " +
        6 * "expT " + "route h1 cwT h1 hsplit h1 h1 hsplit hsplit h1 onT hsplit h1 " + 2 * "h1 h1 hsplit hsplit " +
        "h1 xT hsplit h1 h1 hsplit route h1 h1 hsplit cwT hsplit " + 2 * "h1 hsplit hsplit h1 " + "h1 " +
        3 * "hsplit " + "h1 h1 h1 ycopy " + 2 * "hsplit h1 hsplit " + "h1 h1 " + 4 * "hsplit " + "h1 h1 " +
        4 * "h1 hsplit " + "hsplit h1 " + 2 * "h1 hsplit hsplit " + "ycopy ",
    "DVE":
        "lnA lnA lnB kT kT lnB xT kT kT xT " + 2 * "q q vf score " + "score score q vs " + 3 * "score " + "norm q vs " +
        3 * "score " + "q score norm score pT q score score pT norm score score pT score pT score score norm pT pT " +
        4 * "score " + "norm pT score pT " + 3 * "score " +
        "norm score score norm pT pT score score wo score lnA pT norm pT lnB pT pT xT pT pT h3 " + 4 * "route " +
        "wo lnA h3 h3 lnB h3 xT vs1 h3 h3 k1 h3 route h3 " + 3 * "route " +
        "h3 k1 h3 res lnA vs1 k1 lnB h3 h3 k1 xT vf1 h3 h3 q1 q1 q1 h3 q1 h3 " + 13 * "score1 " +
        2 * "h3 score1 score1 score1 " + 3 * "score1 " + "res score1 lnA " + 4 * "score1 " + "lnB " + 5 * "score1 " +
        "xT mT vf1 " + 2 * "q1 q1 score1 " + 16 * "score1 " + "pv1 " + 14 * "score1 " +
        "pv1 oT mT pv1 oT pv1 oT oT wo1 lnA lnB pv1 xT oT pv1 gate route route pv1 h3 h3 hsplit pv1 oT oT hsplit h3 "
        "h3 oT " + 2 * "h3 hsplit " + "h3 h3 wo1 lnA hsplit hsplit h3 lnB " + 2 * "h3 hsplit " +
        "xT h3 hsplit h3 gate route hsplit route h3 " + 3 * "h3 hsplit " + 2 * "hsplit h3 hsplit " + "h3 " +
        4 * "h3 hsplit " + "h3 h3 " + 3 * "hsplit " + 3 * "h3 hsplit " + 2 * "hsplit h3 h3 hsplit " + 3 * "h3 hsplit " +
        "res hsplit hsplit res ",
    "Pool":
        "lnA split lnA bo split bo " + 3 * "split " + 7 * "norm " +
        "lnA norm h3 lnA h3 h3 h3 split split h3 h3 place_k1s split split h3 h3 h3 place_k1s h3 split split lnA "
        "split " + 2 * "place_k1s h3 h3 " + "h3 h3 h3 h3 lnA " + 3 * "split " + "lnA " + 8 * "h3 " + "lnA " + 28 * "h3 ",
    "SP":
        "cwT wo split cwT split mT mT cwT cwT res res ",
}


def takes(engine, step):
    kind = step[0]
    if engine == "SP":
        return (kind in ("cwT", "mT") or step in (("wo", 1), ("split", "w13_1", 2), ("split", "w2_1", 0))
                or (kind == "res" and step[1] == 3))
    if engine == "PE":
        return True
    if kind == "pT":
        return (engine == "ACT") == (step[3] == 2)
    if kind == "gate":
        return (engine == "ACT") == (step[1] == 1)
    if kind == "route":
        return engine == "DVE" or step[1:] == (3, step[2], 0)
    return True


def order_of(engine):
    left = {}
    for step in all_steps():
        if takes(engine, step):
            left.setdefault(step[0], []).append(step)
    return [left[kind].pop(0) for kind in PROGRAM[engine].split()]


RING = {
    "score": (0, 1, 2, 3), "h1": (0, 1, 2, 3), "h3": (0, 1, 2, 3), ("expT", 0): (0, 1, 2, 3),
    ("expT", 1): (0, 1, 2, 3), ("q1", 1): (0, 1, 2, 3),
    "kT": (4, 5), "pT": (4, 5), "gate": (4, 5), "cwT": (4, 5), "k1": (4, 5), "vf1": (4, 5), "vs1": (4, 5),
    "mT": (4, 5), "onT": (4, 5), "q": (4, 5), "yT": (4, 5), ("q1", 0): (4, 5), ("oT", 0): (4, 5),
    ("oT", 1): (4, 5),
    "xT": (6,), "wo1": (6,), ("pv1", 1): (6,),
    "vf": (6, 7), "vs": (6, 7), "pv": (6, 7), "wo": (6, 7), ("pv1", 0): (6, 7),
    "y": (7,),
    ("score1", 0): (4, 5, 6),
    ("score1", 1): (4, 5, 7),
}


def count_uses(order):
    uses, turn, count = {}, {}, {}
    for step in order:
        key = step
        if step[0] == "down":
            if step[3] > 0:
                continue
            key = ("y",) + step[1:3]
        ring = RING.get(key[:2], RING.get(key[0]))
        if ring is not None:
            n = turn.get(ring, 0)
            turn[ring] = n + 1
            bank = ring[n % len(ring)]
            count[bank] = count.get(bank, 0) + 1
            uses[key] = (bank, count[bank])
    return uses


def build(nc, a, out):
    uses = count_uses(order_of("PE"))
    position, seen = {}, {}
    for step in all_steps():
        seen[step[0]] = seen.get(step[0], 0) + 1
        position[step] = seen[step[0]]

    with ExitStack() as ctx:
        def sb(name, shape, dt=F32, at=ctx):
            return at.enter_context(nc.sbuf_tensor(name, shape, dt))

        def sem(name):
            return ctx.enter_context(nc.semaphore(name))

        psum = ctx.enter_context(nc.psum_tensor("psum", [P, 8, 512], F32))

        X = sb("X", [P, B * T, P])
        xn = sb("xn", [P, B, T, P])
        xT_hi = sb("xT_hi", [P, B, TOK], F32R)
        xT_lo = sb("xT_lo", [P, B, TOK], F32R)
        w_src = sb("w_src", [P, N_HID[1] * 2, P])
        spread = sb("spread", [P, SLOTS, TOK])
        act_s = sb("act_s", [P, 2, TOK])
        gated_u = sb("gated_u", [P, 2, TOK])
        hid = sb("hid", [P, HIDS, TOK])
        ident = sb("ident", [P, P])
        bo = sb("bo", [P, P])
        ctxT = sb("ctxT", [CD + 1, B, CP])
        ctxT_rest = sb("ctxT_rest", [CD + 1, B, P])
        gates_src = sb("gates_src", [P, E0 + E1])
        gates_hi = sb("gates_hi", [P, E0 + E1], F32R)
        gates_lo = sb("gates_lo", [P, E0 + E1], F32R)
        gate_bias = sb("gate_bias", [P, E1])
        vs0_mask = sb("vs0_mask", [P, 2, P])
        vs1_mask = sb("vs1_mask", [P, P])
        head_rows = sb("head_rows", [P, 4])
        lower_first = sb("lower_first", [P, NG, NG])
        lo_rows = sb("lo_rows", [P, 2])
        stats = sb("stats", [P, B, T, 6])
        mv = sb("mv", [P, B, T, 2])
        vareps = sb("vareps", [P, B, T])
        rstd = sb("rstd", [P, B, T])
        minus_half = sb("minus_half", [P, T])
        neg_max0 = sb("neg_max0", [P, B, T, H0])
        row_sum = sb("row_sum", [P, B, T, H0])
        row_inv = sb("row_inv", [P, B, T, H0])
        neg_max1 = sb("neg_max1", [P, B, T, 4, G1])
        den_inv = sb("den_inv", [P, 2, T, 4])
        e_neg = sb("e_neg", [P, T, E0])
        sc = sb("sc", [P, T, E0])
        pair_max = sb("pair_max", [P, T * NG, 2])
        pair_sum = sb("pair_sum", [P, T * NG, 2])
        g_score = sb("g_score", [P, T, NG])
        g_cross = sb("g_cross", [P, T, NG])
        beats = sb("beats", [P, T * NG, NG])
        ties = sb("ties", [P, T * NG, NG])
        rank = sb("rank", [P, T, NG])
        allowed = sb("allowed", [P, T, NG])
        penalty = sb("penalty", [P, T, NG])
        cand = sb("cand", [P, T, E0 + 8])
        replaced = sb("replaced", [P, T, E0 + 8])
        top = sb("top", [P, T, 8])
        chosen = sb("chosen", [P, T, E0])
        diff = sb("diff", [P, T, E1])
        e_diff = sb("e_diff", [P, T, E1])
        w_un = sb("w_un", [P, T, E0])
        w_sum = sb("w_sum", [P, T])
        w_inv = sb("w_inv", [P, T])
        cw = sb("cw", [P, B, T, E0])
        cwT_sb = sb("cwT_sb", [E0, TOK])

        with ExitStack() as r:
            w13_hi0 = sb("w13_hi0", [P, 2 * N_HID[1], P], F32R, r)
            w13_lo0 = sb("w13_lo0", [P, 2 * N_HID[1], P], F32R, r)
            w2_0 = sb("w2_0", [P, N_HID[1], P], F32, r)
            with ExitStack() as r2:
                wk0 = sb("wk0", [CD, H0 * DH0], F32, r2)
                wv0 = sb("wv0", [CD, H0 * DH0], F32, r2)
                wo0 = sb("wo0", [P, PAIRS, P], F32, r2)
                q_hi = sb("q_hi", [P, B, PAIRS, TOK], F32R, r2)
                q_lo = sb("q_lo", [P, B, PAIRS, TOK], F32R, r2)
                k_hi = sb("k_hi", [P, PAIRS, B, 2, CP], F32R, r2)
                k_lo = sb("k_lo", [P, PAIRS, B, 2, CP], F32R, r2)
                v0 = sb("v0", [P, B, H0 * DH0], F32, r2)
                vs0 = sb("vs0", [P, B, PAIRS, P], F32, r2)
                prob = sb("prob", [P, 2, H0, CTX], F32, r2)
                prob_n = sb("prob_n", [P, 2, H0 * CP], F32, r2)
                probT0 = sb("probT0", [P, H0 + 2, TOK], F32, r2)
                with ExitStack() as r3:
                    wq_src0 = sb("wq_src0", [P, H0 * DH0], F32, r3)
                    wq_hi0 = sb("wq_hi0", [P, H0 * DH0], F32R, r3)
                    wq_lo0 = sb("wq_lo0", [P, H0 * DH0], F32R, r3)
                outT0 = sb("outT0", [P, PAIRS, TOK], F32, r2)
            with ExitStack() as r2:
                w13_hi1 = sb("w13_hi1", [P, 2 * N_HID[3], P], F32R, r2)
                w13_lo1 = sb("w13_lo1", [P, 2 * N_HID[3], P], F32R, r2)
                w2_lo1 = sb("w2_lo1", [P, N_HID[3], P], F32R, r2)
                wq_hi1 = sb("wq_hi1", [P, G1 * P], F32R, r2)
                wq_lo1 = sb("wq_lo1", [P, G1 * P], F32R, r2)
                wk1 = sb("wk1", [CD + 1, G1, P], F32, r2)
                wv1 = sb("wv1", [CD + 1, G1 * P], F32, r2)
                wo1 = sb("wo1", [P, P], F32, r2)
                k1 = sb("k1", [P, B, G1, 4, CTX], F32R, r2)
                k1s = sb("k1s", [P, B, G1, 4, PAD], F32R, r2)
                q1 = sb("q1", [P, B, G1, TOK], F32R, r2)
                rounded = sb("rounded", [P, 2, TOK], F32R, r2)
                v1 = sb("v1", [P, B, G1 * P], F32, r2)
                vs1 = sb("vs1", [P, B, G1, P], F32, r2)
                nmT_hi = sb("nmT_hi", [H1, TOK], F32R, r2)
                nmT_lo = sb("nmT_lo", [H1, TOK], F32R, r2)
                with ExitStack() as r3:
                    wq_src1 = sb("wq_src1", [P, G1 * P], F32, r3)
                with ExitStack() as r3:
                    k_stack = sb("k_stack", [P, 2, B * CP], F32R, r3)
                od = sb("od", [P, 2, TOK], F32, r2)
                on = sb("on", [P, T, P], F32, r2)
        with ExitStack() as r:
            probT1 = sb("probT1", [P, 2, 5, TOK], F32, r)
            onT = sb("onT", [P, TOK], F32, r)

        k1_b0 = k1[:, 0, :, :, :].rearrange("p g j c -> p (g j c)")
        w2_hi1 = k1_b0[:, 0:N_HID[3] * P].rearrange("p (i d) -> p i d", d=P)
        hid_hi, hid_lo = q1[:, 0, 0:2, :], q1[:, 0, 2:4, :]
        yT = onT

        cw_dram = {(s, b): nc.dram_tensor(f"cw_{s}_{b}", (EXPERTS[s], TOK), F32).ap() for s in (1, 3) for b in range(B)}

        bank_ready = [sem(f"bank_ready{k}") for k in range(8)]
        bank_read = [sem(f"bank_read{k}") for k in range(8)]
        loaded = {n: sem(f"loaded_{n}") for n in (
            "x0", "x1", "ident", "const", "ctx", "ctxv", "wq0", "w13_0", "w2_0", "wo0", "wqkv1", "w13_1", "w2_1")}
        hi_of = {n: sem(f"hi_{n}") for n in ("wq0", "gates", "w13_0", "wq1", "w13_1", "w2_1")}
        lo_of = {n: sem(f"lo_{n}") for n in ("wq0", "gates", "w13_0", "wq1", "w13_1", "w2_1")}
        cleared0 = sem("cleared0")
        var_ready = sem("var_ready")
        rstd_ready = sem("rstd_ready")
        xn_ready = sem("xn_ready")
        xT_rounded = sem("xT_rounded")
        bo_added = sem("bo_added")
        kT_rounded = sem("kT_rounded")
        q_rounded = sem("q_rounded")
        negmax_ready = sem("negmax_ready")
        rowinv_ready = sem("rowinv_ready")
        prob_normed = sem("prob_normed")
        diff_ready = sem("diff_ready")
        e_diff_ready = sem("e_diff_ready")
        cw_ready = sem("cw_ready")
        cw_stored = sem("cw_stored")
        spread_loaded = [sem(f"spread_loaded{c}") for c in range(SLOTS // 2)]
        hid_ready = sem("hid_ready")
        hid_used = sem("hid_used")
        hid_rounded = sem("hid_rounded")
        hid_split = sem("hid_split")
        k1_rounded = sem("k1_rounded")
        k1_placed = sem("k1_placed")
        k1s_placed = sem("k1s_placed")
        q1_rounded = sem("q1_rounded")
        nm_rounded = sem("nm_rounded")
        nm_placed = [sem(f"nm_placed{b}") for b in range(B)]
        out_stored = sem("out_stored")
        dve_step = sem("dve_step")

        def bank(key):
            return psum[:, uses[key][0], :]

        def wait_filled(eng, key):
            k, n = uses[key]
            eng.wait_ge(bank_ready[k], n)

        def wait_moved(eng, key):
            k, n = uses[key]
            eng.wait_ge(bank_read[k], n)

        def wait_bank_free(eng, key):
            k, n = uses[key]
            if n > 1:
                eng.wait_ge(bank_read[k], n - 1)

        def filled(ins, key):
            ins.then_inc(bank_ready[uses[key][0]], 1)

        def moved(ins, key):
            ins.then_inc(bank_read[uses[key][0]], 1)

        HEAD_SCALE0 = float(DH0) ** -0.5
        HEAD_SCALE1 = float(DH1) ** -0.5
        splits = {"wq0": (wq_src0, wq_hi0, wq_lo0), "gates": (gates_src, gates_hi, gates_lo), "wq1": (wq_src1, wq_hi1, wq_lo1)}
        w13 = {1: (w13_hi0, w13_lo0, "w13_0"), 3: (w13_hi1, w13_lo1, "w13_1")}
        n_src = 2 * N_HID[1] // CHUNK
        N_CONST, N_WQKV1, N_NM = 8, 4, 8

        def split_aps(name, c):
            if name in splits:
                s, h, l = splits[name]
                return s[:, :], h[:, :], l[:, :]
            h, l = {"w13_0": (w13_hi0, w13_lo0), "w13_1": (w13_hi1, w13_lo1), "w2_1": (w2_hi1, w2_lo1)}[name]
            at = slice(c * CHUNK, (c + 1) * CHUNK)
            cs = c % n_src
            return w_src[:, cs * CHUNK:(cs + 1) * CHUNK, :], h[:, at, :], l[:, at, :]

        def wait_split_source(eng, name, c):
            if name == "w13_1":
                eng.wait_ge(loaded[name], 16 * (c // n_src + 1))
            else:
                eng.wait_ge(loaded[{"gates": "const", "wq1": "wqkv1"}.get(name, name)],
                            {"gates": 16 * N_CONST, "wq1": 16 * N_WQKV1}.get(name, 16))

        hid_index = {step[1:]: n for n, step in enumerate(step for step in all_steps() if step[0] == "h1")}
        tiles = list(hid_index)
        first_split = hid_index[(3, 0, 0)]

        def wait_hid_used(eng, n):
            s, b, i = tiles[n]
            if i == N_HID[s] - 1:
                wait_filled(eng, ("y", s, b))
            else:
                eng.wait_ge(hid_used, sum(t[2] < N_HID[t[0]] - 1 for t in tiles[:n + 1]))

        def slot_of(s, i):
            e = i - N_SHARED[s]
            return e if s == 1 else e // 2

        def spread_count(s, b):
            return 16 * (2 * (b + 1) if s == 1 else 2 * B + b + 1)

        block = ctx.enter_context(nc.Block())

        @block.sync
        def _(sp):
            def load(dst, src, name):
                sp.dma_start(dst, src).then_inc(loaded[name], 16)

            load(X[:, 0:T, :], a["x"][:, 0:T, :], "x0")
            load(ident[:, :], a["ident"], "ident")
            load(ctxT[:, :, :], a["ctxT"], "ctx")
            load(wk0[:, :], a["wk0"], "ctx")
            load(wq_src0[:, :], a["wq0"], "wq0")
            load(X[:, T:2 * T, :], a["x"][:, T:2 * T, :], "x1")
            for dst, name in ((bo[:, :], "bo"), (gates_src[:, :], "gates"),
                              (gate_bias[:, :], "gate_bias"), (lower_first[:, :, :], "lower_first"),
                              (lo_rows[:, :], "lo_rows"), (vs0_mask[:, :, :], "vs0_mask"), (vs1_mask[:, :], "vs1_mask"),
                              (head_rows[:, :], "head_rows")):
                load(dst, a[name], "const")
            load(ctxT_rest[:, :, :], a["ctxT_rest"], "ctxv")
            load(wv0[:, :], a["wv0"], "ctxv")
            load(wo0[:, :, :], a["wo0"], "wo0")
            load(w_src[:, :, :], a["w13_0"], "w13_0")
            load(w2_0[:, :, :], a["w2_0"], "w2_0")

            def spread_weights(s, b):
                wait_moved(sp, ("cwT", s, b))
                sp.dma_start(cw_dram[s, b], cwT_sb[0:EXPERTS[s], :]).then_inc(cw_stored, 16)
                sp.wait_ge(cw_stored, 16 * position[("cwT", s, b)])
                for c in range(SLOTS // 2):
                    last = {(1, 0): None, (1, 1): (1, 0, 2 * c + 2), (3, 0): (1, 1, 2 * c + 2),
                            (3, 1): (3, 0, 2 + 4 * c + 3)}[s, b]
                    if last is not None:
                        wait_moved(sp, ("h3",) + last)
                    for half in range(2 if s == 1 else 1):
                        if s == 1:
                            rows = cw_dram[s, b].rearrange("(i two) n -> two i n", two=2)[half, 2 * c:2 * c + 2, :]
                            dst = spread[64 * half:64 * half + 64, 2 * c:2 * c + 2, :]
                            src = rows.unsqueeze(0).broadcast_to((64, 2, TOK))
                        else:
                            rows = cw_dram[s, b][2 * c:2 * c + 2, :]
                            dst = spread[:, 2 * c:2 * c + 2, :]
                            src = rows.unsqueeze(0).broadcast_to((P, 2, TOK))
                        sp.dma_start(dst, src).then_inc(spread_loaded[c], 16)

            for step in order_of("SP"):
                if step == ("wo", 1):
                    wait_filled(sp, ("wo", 1))
                    load(wq_src1[:, :], a["wq1"], "wqkv1")
                    load(wk1[:, :, :], a["wk1"], "wqkv1")
                    load(wv1[:, :], a["wv1"], "wqkv1")
                    load(wo1[:, :], a["wo1"], "wqkv1")
                    sp.wait_ge(lo_of["w13_0"], n_src)
                    load(w_src[:, :, :], a["w13_1"][:, 0:2 * N_HID[1], :], "w13_1")
                if step == ("split", "w13_1", n_src - 1):
                    sp.wait_ge(lo_of["w13_1"], n_src)
                    load(w_src[:, :, :], a["w13_1"][:, 2 * N_HID[1]:, :], "w13_1")
                if step == ("split", "w2_1", 0):
                    sp.wait_ge(lo_of["w13_1"], 2 * n_src)
                    load(w_src[:, :, :], a["w2_1"], "w2_1")
                if step[0] == "cwT":
                    spread_weights(*step[1:])
                if step[0] == "mT":
                    b = step[1]
                    wait_moved(sp, step)
                    for part, rows in ((0, nmT_hi), (1, nmT_lo)):
                        for j in range(4):
                            r = PAD * j + 3 * DH1 + part
                            sp.dma_start(q1[r:r + 1, b, :, :].bitcast(F32), rows[G1 * j:G1 * (j + 1), :].bitcast(F32))\
                                .then_inc(nm_placed[b], 16)
                if step[0] == "res" and step[1] == 3:
                    b = step[2]
                    wait_moved(sp, ("yT", 3, b))
                    sp.dma_start(out[:, b * T:(b + 1) * T, :], X[:, b * T:(b + 1) * T, :]).then_inc(out_stored, 16)
            sp.wait_ge(out_stored, 16 * B)

        @block.gpsimd
        def _(pool):
            pool.memset(minus_half[:, :], -0.5).then_inc(cleared0, 1)
            pool.memset(k_hi[:, :, :, :, :].bitcast(F32), 0.0).then_inc(cleared0, 1)
            pool.memset(k_lo[:, :, :, :, :].bitcast(F32), 0.0).then_inc(cleared0, 1)
            rest = prob_n[:, :, H0 * P:].rearrange("p r (h c) -> p r h c", h=H0)
            pool.memset(rest[:, :, :, REST:PAD], 0.0).then_inc(cleared0, 1)

            for step in order_of("Pool"):
                kind = step[0]
                if kind == "split":
                    name, c = step[1:]
                    src, hi, lo = split_aps(name, c)
                    pool.wait_ge(hi_of[name], c + 1)
                    pool.tensor_tensor(lo, src, hi.bitcast(F32), ALU.subtract).then_inc(lo_of[name], 1)
                elif kind == "lnA":
                    b = step[2]
                    pool.wait_ge(cleared0, 1)
                    pool.wait_ge(var_ready, position[step])
                    pool.tensor_tensor(rstd[:, b, :], vareps[:, b, :], minus_half[:, :], ALU.pow).then_inc(rstd_ready, 1)
                elif kind == "bo":
                    b = step[1]
                    pool.wait_ge(loaded["const"], 16 * N_CONST)
                    pool.wait_ge(xn_ready, position[("lnB", 0, b)])
                    xb = X[:, b * T:(b + 1) * T, :]
                    pool.tensor_tensor(xb, xb, bo[:, :].unsqueeze(1).broadcast_to((P, T, P)), ALU.add).then_inc(bo_added, 1)
                elif kind == "norm":
                    b, t = step[1:]
                    r = (b * T + t) % 2
                    pool.wait_ge(rowinv_ready, position[step])
                    pool.wait_ge(cleared0, 4)
                    if b * T + t >= 2:
                        wait_filled(pool, ("pT", (b * T + t - 2) // T, (b * T + t - 2) % T, 2))
                    for dst, cols in ((prob_n[:, r, 0:H0 * P].rearrange("p (h c) -> p h c", h=H0), slice(0, P)),
                                      (rest[:, r, :, 0:REST], slice(P, CTX))):
                        w = cols.stop - cols.start
                        ins = pool.tensor_tensor(dst, prob[:, r, :, cols],
                                                 row_inv[:, b, t, :].unsqueeze(2).broadcast_to((P, H0, w)), ALU.mult)
                    ins.then_inc(prob_normed, 1)
                elif kind == "place_k1s":
                    g = step[1]
                    wait_moved(pool, ("k1", g))
                    pool.wait_ge(loaded["const"], 16 * N_CONST)
                    k = k_stack[:, g % 2, :].bitcast(F32).rearrange("p (b c) -> p b c", b=B)[:, :, P:CP]
                    pool.tensor_tensor(k1s[:, :, g, :, :], k.unsqueeze(2).broadcast_to((P, B, 4, PAD)),
                                       head_rows[:, :].unsqueeze(1).unsqueeze(3).broadcast_to((P, B, 4, PAD)), ALU.mult)\
                        .then_inc(k1s_placed, 1)
                elif kind == "h3":
                    n = hid_index[step[1:]]
                    wait_moved(pool, ("h1",) + step[1:])
                    wait_moved(pool, step)
                    if n - HIDS >= first_split:
                        pool.wait_ge(hid_split, n - HIDS - first_split + 1)
                    elif n >= HIDS:
                        wait_hid_used(pool, n - HIDS)
                    pool.tensor_tensor(hid[:, n % HIDS, :], act_s[:, n % 2, :], gated_u[:, n % 2, :], ALU.mult)\
                        .then_inc(hid_ready, 1)

        @block.scalar
        def _(act):
            for step in order_of("ACT"):
                kind = step[0]
                if kind == "split":
                    name, c = step[1:]
                    src, hi, lo = split_aps(name, c)
                    wait_split_source(act, name, c)
                    if name == "w2_1":
                        wait_filled(act, ("expT", 0, G1 - 1, 4))
                    act.copy(hi, src).then_inc(hi_of[name], 1)
                elif kind == "xT":
                    b = step[2]
                    wait_filled(act, step)
                    act.copy(xT_hi[:, b, :], bank(step)).then_inc(xT_rounded, 1)
                elif kind == "kT":
                    p = step[1]
                    wait_filled(act, step)
                    act.wait_ge(cleared0, 2)
                    for j in range(2):
                        rows = slice(64 * j, 64 * j + 64)
                        act.copy(k_hi[rows, p, :, j, :], bank(step)[rows, 0:B * CP].rearrange("p (b c) -> p b c", b=B))\
                            .then_inc(kT_rounded, 1)
                elif kind == "q":
                    b, p = step[1:]
                    wait_filled(act, step)
                    act.mul(q_hi[:, b, p, :], bank(step), HEAD_SCALE0).then_inc(q_rounded, 1)
                elif kind == "score":
                    b, t, p = step[1:]
                    r = (b * T + t) % 2
                    act.wait_ge(negmax_ready, position[step])
                    if b * T + t >= 2 and p == 0:
                        act.wait_ge(prob_normed, b * T + t - 1)
                    for j in range(2):
                        h = 2 * p + j
                        ins = act.activation(prob[:, r, h, 0:CTX], bank(step)[:, j * CTX:(j + 1) * CTX], ACT.Exp,
                                             bias=neg_max0[:, b, t, h:h + 1], accum_out=row_sum[:, b, t, h:h + 1])
                    moved(ins, step)
                elif kind == "pT" and step[3] == 2:
                    b, t = step[1:3]
                    wait_filled(act, step)
                    if b == 1 and t == 0:
                        wait_filled(act, ("pv", 0, PAIRS - 1))
                    moved(act.copy(probT0[:, H0:H0 + 2, t * P:(t + 1) * P],
                                   bank(step)[:, 0:2 * P].rearrange("p (g n) -> p g n", g=2)), step)
                elif kind == "pv":
                    b, p = step[1:]
                    wait_filled(act, step)
                    if b == 1:
                        wait_filled(act, ("wo", 0))
                    moved(act.copy(outT0[:, p, :], bank(step)), step)
                elif kind == "gate" and step[1] == 1:
                    wait_filled(act, step)
                    if step[2] > 0:
                        act.wait_ge(cw_ready, 1)
                    moved(act.activation(e_neg[:, :, :], bank(step)[:, 0:T * E0].rearrange("p (t e) -> p t e", t=T),
                                         ACT.Exp, scale=-1.0), step)
                elif kind == "route" and step[1] == 3 and step[3] == 0:
                    b = step[2]
                    act.wait_ge(diff_ready, b + 1)
                    act.activation(e_diff[:, :, :], diff[:, :, :], ACT.Exp).then_inc(e_diff_ready, 1)
                elif kind == "cwT":
                    s, b = step[1:]
                    wait_filled(act, step)
                    if position[step] > 1:
                        act.wait_ge(cw_stored, 16 * (position[step] - 1))
                    moved(act.copy(cwT_sb[0:EXPERTS[s], :], bank(step)[0:EXPERTS[s], :]), step)
                elif kind == "h1":
                    n = hid_index[step[1:]]
                    wait_filled(act, step)
                    if n >= 2:
                        act.wait_ge(hid_ready, n - 1)
                    moved(act.activation(act_s[:, n % 2, :], bank(step), ACT.Silu), step)
                elif kind == "hsplit":
                    n = hid_index[step[1:]]
                    m = n - first_split
                    act.wait_ge(hid_ready, n + 1)
                    if m >= 2:
                        wait_hid_used(act, n - 2)
                    else:
                        wait_filled(act, ("expT", 0, G1 - 1, 4))
                    act.copy(hid_hi[:, m % 2, :], hid[:, n % HIDS, :]).then_inc(hid_rounded, 1)
                elif kind == "ycopy":
                    b = step[2]
                    wait_filled(act, ("y", 3, b))
                    wait_filled(act, ("wo1", 1) if b == 0 else ("yT", 3, 0))
                    moved(act.copy(yT[:, :], bank(("y", 3, b))), ("y", 3, b))
                elif kind == "k1":
                    g = step[1]
                    wait_filled(act, step)
                    if g >= 2:
                        wait_moved(act, ("k1", g - 2))
                    act.copy(rounded[:, g % 2, 0:B * CP], bank(step)[:, 0:B * CP]).then_inc(k1_rounded, 1)
                elif kind == "place_k1":
                    g, j = step[1:]
                    wait_moved(act, ("k1", g))
                    act.wait_ge(loaded["const"], 16 * N_CONST)
                    k = k_stack[:, g % 2, :].bitcast(F32).rearrange("p (b c) -> p b c", b=B)
                    act.mul(k1[:, :, g, j, :], k[:, :, 0:CTX], head_rows[:, j:j + 1]).then_inc(k1_placed, 1)
                elif kind == "q1":
                    b, g = step[1:]
                    wait_filled(act, step)
                    if (b, g) == (0, 0):
                        wait_moved(act, ("k1", G1 - 2))
                        wait_moved(act, ("k1", G1 - 1))
                    if g >= 2:
                        wait_moved(act, ("q1", b, g - 2))
                    elif b == 1:
                        wait_moved(act, ("q1", 0, g + 2))
                    act.copy(rounded[:, g % 2, :], bank(step)).then_inc(q1_rounded, 1)
                elif kind == "mT":
                    b = step[1]
                    wait_filled(act, step)
                    if b == 1:
                        act.wait_ge(nm_placed[0], 16 * N_NM)
                    act.copy(nmT_hi[:, :], bank(step)[0:H1, :]).then_inc(nm_rounded, 1)
                elif kind == "expT":
                    b, g, j = step[1:]
                    wait_filled(act, step)
                    n = b * G1 + g
                    if n >= 2:
                        wait_filled(act, ("pv1", (n - 2) // G1, (n - 2) % G1))
                    else:
                        wait_filled(act, ("y", 1, 1))
                    moved(act.activation(probT1[:, n % 2, j, :], bank(step), ACT.Exp, scale=HEAD_SCALE1), step)
                elif kind == "onT":
                    b = step[1]
                    wait_filled(act, step)
                    if b == 1:
                        wait_filled(act, ("wo1", 0))
                    moved(act.copy(onT[:, :], bank(step)), step)

        @block.vector
        def _(dve):
            steps = [0]

            def chain(ins):
                ins.then_inc(dve_step, 1)
                steps[0] += 1
                dve.wait_ge(dve_step, steps[0])

            def note(ins):
                ins.then_inc(dve_step, 1)
                steps[0] += 1

            def settle():
                dve.wait_ge(dve_step, steps[0])

            for step in order_of("DVE"):
                kind = step[0]
                if kind == "lnA":
                    s, b = step[1:]
                    if s == 0:
                        dve.wait_ge(loaded[f"x{b}"], 16)
                    settle()
                    for t in range(T):
                        note(dve.bn_stats(stats[:, b, t, :], X[:, b * T + t, :]))
                    settle()
                    for t in range(T):
                        note(dve.bn_aggr(mv[:, b, t, :], stats[:, b, t, :]))
                    settle()
                    dve.tensor_scalar(vareps[:, b, :], mv[:, b, :, 1], EPS, None, ALU.add).then_inc(var_ready, 1)
                elif kind == "lnB":
                    s, b = step[1:]
                    dve.wait_ge(rstd_ready, position[("lnA", s, b)])
                    for t in range(T):
                        ins = dve.tensor_scalar(xn[:, b, t, :], X[:, b * T + t, :], mv[:, b, t, 0:1], rstd[:, b, t:t + 1],
                                                ALU.subtract, ALU.mult)
                    ins.then_inc(xn_ready, 1)
                elif kind == "xT":
                    b = step[2]
                    dve.wait_ge(xT_rounded, position[step])
                    moved(dve.tensor_tensor(xT_lo[:, b, :], bank(step), xT_hi[:, b, :].bitcast(F32), ALU.subtract), step)
                elif kind == "kT":
                    p = step[1]
                    dve.wait_ge(cleared0, 3)
                    for j in range(2):
                        dve.wait_ge(kT_rounded, 2 * p + j + 1)
                        rows = slice(64 * j, 64 * j + 64)
                        ins = dve.tensor_tensor(
                            k_lo[rows, p, :, j, :], bank(step)[rows, 0:B * CP].rearrange("p (b c) -> p b c", b=B),
                            k_hi[rows, p, :, j, :].bitcast(F32), ALU.subtract)
                    moved(ins, step)
                elif kind == "q":
                    b, p = step[1:]
                    dve.wait_ge(q_rounded, position[step])
                    moved(dve.scalar_tensor_tensor(q_lo[:, b, p, :], bank(step), HEAD_SCALE0,
                                                   q_hi[:, b, p, :].bitcast(F32), ALU.mult, ALU.subtract), step)
                elif kind in ("vf", "vf1"):
                    b = step[1]
                    wait_filled(dve, step)
                    moved(dve.tensor_copy((v0 if kind == "vf" else v1)[:, b, :], bank(step)), step)
                elif kind in ("vs", "vs1"):
                    b = step[1]
                    wait_filled(dve, step)
                    dve.wait_ge(loaded["const"], 16 * N_CONST)
                    if kind == "vs":
                        dst = vs0[:, b, :, :].rearrange("p (g q) c -> p g q c", q=2)
                        src = bank(step).rearrange("p (g q c) -> p g q c", g=2, q=2)
                        mask = vs0_mask[:, :, :].unsqueeze(1).broadcast_to((P, 2, 2, P))
                    else:
                        dst = vs1[:, b, :, :]
                        src = bank(step).rearrange("p (g c) -> p g c", g=G1)
                        mask = vs1_mask[:, :].unsqueeze(1).broadcast_to((P, G1, P))
                    moved(dve.tensor_tensor(dst, src, mask, ALU.mult), step)
                elif kind == "score":
                    b, t, p = step[1:]
                    wait_filled(dve, step)
                    dve.tensor_reduce(neg_max0[:, b, t, 2 * p:2 * p + 2],
                                      bank(step)[:, 0:2 * CTX].rearrange("p (j c) -> p j c", j=2), AX, ALU.max, negate=True)\
                        .then_inc(negmax_ready, 1)
                elif kind == "norm":
                    b, t = step[1:]
                    for p in range(PAIRS):
                        wait_moved(dve, ("score", b, t, p))
                    dve.reciprocal(row_inv[:, b, t, :], row_sum[:, b, t, :]).then_inc(rowinv_ready, 1)
                elif kind == "pT" and step[3] < 2:
                    b, t, k = step[1:]
                    wait_filled(dve, step)
                    if b == 1 and t == 0:
                        wait_filled(dve, ("pv", 0, PAIRS - 1))
                    moved(dve.tensor_copy(probT0[:, 4 * k:4 * k + 4, t * P:(t + 1) * P],
                                          bank(step).rearrange("p (h n) -> p h n", h=4)), step)
                elif kind in ("wo", "wo1", "res"):
                    b = step[-1]
                    key = ("y" if step[1] == 1 else "yT",) + step[1:] if kind == "res" else step
                    wait_filled(dve, key)
                    if kind == "wo":
                        dve.wait_ge(bo_added, position[("bo", b)])
                    xb = X[:, b * T:(b + 1) * T, :]
                    settle()
                    moved(dve.tensor_tensor(xb, bank(key).rearrange("p (t d) -> p t d", t=T), xb, ALU.add), key)
                    wait_moved(dve, key)
                elif kind == "hsplit":
                    n = hid_index[step[1:]]
                    m = n - first_split
                    dve.wait_ge(hid_rounded, m + 1)
                    dve.tensor_tensor(hid_lo[:, m % 2, :], hid[:, n % HIDS, :], hid_hi[:, m % 2, :].bitcast(F32), ALU.subtract)\
                        .then_inc(hid_split, 1)
                elif kind == "gate" and step[1] == 3:
                    b = step[2]
                    wait_filled(dve, step)
                    dve.wait_ge(loaded["const"], 16 * N_CONST)
                    settle()
                    moved(dve.tensor_tensor(cand[:, :, 0:E1], bank(step)[:, 0:T * E1].rearrange("p (t e) -> p t e", t=T),
                                            gate_bias[:, :].unsqueeze(1).broadcast_to((P, T, E1)), ALU.add), step)
                    wait_moved(dve, step)
                elif kind == "route":
                    s, b, part = step[1:]
                    if s == 1 and part == 0:
                        wait_moved(dve, ("gate", s, b))
                        dve.wait_ge(loaded["const"], 16 * N_CONST)
                        chain(dve.tensor_scalar(e_neg[:, :, :], e_neg[:, :, :], 1.0, None, ALU.add))
                        chain(dve.reciprocal(sc[:, :, :], e_neg[:, :, :]))
                        quad = sc[:, :, :].rearrange("p t (g h w) -> p (t g) h w", g=NG, w=2)
                        note(dve.tensor_tensor(pair_max[:, :, :], quad[:, :, :, 0], quad[:, :, :, 1], ALU.max))
                        note(dve.tensor_tensor(pair_sum[:, :, :], quad[:, :, :, 0], quad[:, :, :, 1], ALU.add))
                        settle()
                        gs = g_score[:, :, :].rearrange("p t g -> p (t g)")
                        gc = g_cross[:, :, :].rearrange("p t g -> p (t g)")
                        note(dve.tensor_tensor(gc, pair_max[:, :, 0], pair_max[:, :, 1], ALU.add))
                        note(dve.tensor_tensor(gs, pair_sum[:, :, 0], pair_sum[:, :, 1], ALU.max))
                        settle()
                        chain(dve.tensor_tensor(gs, gs, gc, ALU.max))
                    elif s == 1 and part == 1:
                        own = g_score[:, :, :].unsqueeze(3).broadcast_to((P, T, NG, NG))
                        other = g_score[:, :, :].unsqueeze(2).broadcast_to((P, T, NG, NG))
                        bt = beats[:, :, :].rearrange("p (t g) h -> p t g h", t=T)
                        ti = ties[:, :, :].rearrange("p (t g) h -> p t g h", t=T)
                        first = lower_first[:, :, :].unsqueeze(1).broadcast_to((P, T, NG, NG))
                        note(dve.tensor_tensor(bt, other, own, ALU.is_gt))
                        note(dve.tensor_tensor(ti, other, own, ALU.is_equal))
                        settle()
                        chain(dve.tensor_tensor(ti, ti, first, ALU.mult))
                        chain(dve.tensor_tensor(beats[:, :, :], beats[:, :, :], ties[:, :, :], ALU.add))
                    elif s == 1 and part == 2:
                        settle()
                        chain(dve.tensor_reduce(rank[:, :, :].rearrange("p t g -> p (t g)"), beats[:, :, :], AX, ALU.add))
                        chain(dve.tensor_scalar(allowed[:, :, :], rank[:, :, :], 2.0, None, ALU.is_lt))
                        note(dve.tensor_scalar(penalty[:, :, :], allowed[:, :, :], -1.0, None, ALU.add))
                        wide = lambda x: x[:, :, :].unsqueeze(3).broadcast_to((P, T, NG, E0 // NG))
                        cg = cand[:, :, 0:E0].rearrange("p t (g e) -> p t g e", g=NG)
                        chain(dve.tensor_tensor(cg, sc[:, :, :].rearrange("p t (g e) -> p t g e", g=NG), wide(allowed), ALU.mult))
                        note(dve.tensor_tensor(cg, cg, wide(penalty), ALU.add))
                    n_e, topk, sentinel, gone = (E0, TOPK0, -2.0, -3.0) if s == 1 else (E1, TOPK1, -3.0e38, -3.2e38)
                    last = ROUTE_PARTS[s] - 1
                    if part == last - 1:
                        settle()
                        note(dve.memset(cand[:, :, n_e:n_e + 8], sentinel))
                        settle()
                        for t in range(T):
                            note(dve.max(top[:, t, :], cand[:, t, 0:n_e]))
                        settle()
                        if s == 3:
                            dve.tensor_tensor(diff[:, :, :], cand[:, :, 0:E1], top[:, :, 0:1].broadcast_to((P, T, E1)), ALU.subtract)\
                                .then_inc(diff_ready, 1)
                        note(dve.memset(top[:, :, topk:8], sentinel))
                        settle()
                        for t in range(T):
                            note(dve.match_replace(replaced[:, t, 0:n_e + 8], top[:, t, :], cand[:, t, 0:n_e + 8], gone))
                        settle()
                    if part == last:
                        settle()
                        chain(dve.tensor_tensor(chosen[:, :, 0:n_e], replaced[:, :, 0:n_e], cand[:, :, 0:n_e], ALU.not_equal))
                        if s == 3:
                            dve.wait_ge(e_diff_ready, b + 1)
                        weight = sc[:, :, :] if s == 1 else e_diff[:, :, :]
                        chain(dve.tensor_tensor(w_un[:, :, 0:n_e], weight, chosen[:, :, 0:n_e], ALU.mult))
                        chain(dve.tensor_reduce(w_sum[:, :], w_un[:, :, 0:n_e], AX, ALU.add))
                        if s == 1:
                            chain(dve.tensor_scalar(w_sum[:, :], w_sum[:, :], 1e-6, None, ALU.add))
                        chain(dve.reciprocal(w_inv[:, :], w_sum[:, :]))
                        dve.tensor_tensor(cw[:, b, :, 0:n_e], w_un[:, :, 0:n_e],
                                          w_inv[:, :].unsqueeze(2).broadcast_to((P, T, n_e)), ALU.mult).then_inc(cw_ready, 1)
                        dve.wait_ge(cw_ready, position[("cwT", s, b)])
                elif kind == "h3":
                    s, b, i = step[1:]
                    n = hid_index[step[1:]]
                    if n >= 2:
                        dve.wait_ge(hid_ready, n - 1)
                    wait_filled(dve, step)
                    if i < N_SHARED[s]:
                        ins = dve.tensor_copy(gated_u[:, n % 2, :], bank(step))
                    else:
                        slot = slot_of(s, i)
                        dve.wait_ge(spread_loaded[slot // 2], spread_count(s, b))
                        ins = dve.tensor_tensor(gated_u[:, n % 2, :], bank(step), spread[:, slot, :], ALU.mult)
                    moved(ins, step)
                elif kind == "k1":
                    g = step[1]
                    dve.wait_ge(k1_rounded, g + 1)
                    if g >= 2:
                        dve.wait_ge(k1_placed, 4 * (g - 1))
                        dve.wait_ge(k1s_placed, g - 1)
                    else:
                        dve.wait_ge(lo_of["wq1"], 1)
                    moved(dve.scalar_tensor_tensor(k_stack[:, g % 2, :], rounded[:, g % 2, 0:B * CP].bitcast(F32), lo_rows[:, 1:2],
                                                   bank(step)[:, 0:B * CP], ALU.mult, ALU.add), step)
                elif kind == "q1":
                    b, g = step[1:]
                    dve.wait_ge(q1_rounded, position[step])
                    moved(dve.scalar_tensor_tensor(q1[:, b, g, :], rounded[:, g % 2, :].bitcast(F32), lo_rows[:, 0:1],
                                                   bank(step), ALU.mult, ALU.add), step)
                elif kind == "score1":
                    b, t, g, half = step[1:]
                    wait_filled(dve, step)
                    moved(dve.tensor_reduce(neg_max1[:, b, t, 2 * half:2 * half + 2, g],
                                            bank(step)[:, 0:2 * CTX].rearrange("p (j c) -> p j c", j=2), AX, ALU.max, negate=True),
                          step)
                elif kind == "mT":
                    b = step[1]
                    dve.wait_ge(nm_rounded, b + 1)
                    moved(dve.tensor_tensor(nmT_lo[:, :], bank(step)[0:H1, :], nmT_hi[:, :].bitcast(F32), ALU.subtract), step)
                elif kind == "pv1":
                    b, g = step[1:]
                    wait_filled(dve, step)
                    if b * G1 + g >= 2:
                        n = b * G1 + g - 2
                        wait_filled(dve, ("oT", n // G1, n % G1))
                    dve.wait_ge(k1_placed, 4 * G1)
                    dve.wait_ge(k1s_placed, G1)
                    moved(dve.tensor_copy(od[:, g % 2, :], bank(step)), step)
                elif kind == "oT":
                    b, g = step[1:]
                    wait_filled(dve, step)
                    if b == 1 and g == 0:
                        wait_filled(dve, ("onT", 0))
                    v = bank(step).rearrange("p (t j c) -> p t j c", t=T, j=4)
                    settle()
                    chain(dve.reciprocal(den_inv[:, g % 2, :, :], v[:, :, :, DH1]))
                    moved(dve.tensor_tensor(on[:, :, g * 32:(g + 1) * 32].rearrange("p t (j c) -> p t j c", j=4),
                                            v[:, :, :, 0:DH1],
                                            den_inv[:, g % 2, :, :].unsqueeze(3).broadcast_to((P, T, 4, DH1)), ALU.mult), step)

        @block.tensor
        def _(pe):
            def product3(dst, w_hi, w_lo, m_hi, m_lo):
                pe.matmul(dst, w_hi, m_hi, start=True, stop=False)
                pe.matmul(dst, w_hi, m_lo, start=False, stop=False)
                return pe.matmul(dst, w_lo, m_hi, start=False, stop=True)

            for step in order_of("PE"):
                kind = step[0]
                if step in uses:
                    wait_bank_free(pe, step)
                if kind == "kT":
                    p = step[1]
                    pe.wait_ge(loaded["ctx"], 32)
                    filled(pe.matmul(bank(step)[:, 0:B * CP], wk0[:, p * P:(p + 1) * P],
                                     ctxT[0:CD, :, :].rearrange("k b c -> k (b c)"), start=True, stop=True), step)
                elif kind in ("vf", "vf1", "vs", "vs1"):
                    b = step[1]
                    if kind in ("vf", "vs"):
                        pe.wait_ge(loaded["ctx"], 32)
                        pe.wait_ge(loaded["ctxv"], 32)
                        w, k = wv0[:, :], CD
                    else:
                        pe.wait_ge(loaded["wqkv1"], 16 * N_WQKV1)
                        w, k = wv1[:, :], CD + 1
                    rows = ctxT[0:k, b, 0:P] if kind in ("vf", "vf1") else ctxT_rest[0:k, b, :]
                    filled(pe.matmul(bank(step), rows, w, start=True, stop=True), step)
                elif kind == "xT":
                    s, b = step[1:]
                    pe.wait_ge(loaded["ident"], 16)
                    pe.wait_ge(xn_ready, position[step])
                    for t in range(T):
                        ins = pe.transpose(bank(step)[:, t * P:(t + 1) * P], xn[:, b, t, :], ident[:, :])
                    filled(ins, step)
                elif kind == "q":
                    b, p = step[1:]
                    pe.wait_ge(lo_of["wq0"], 1)
                    wait_moved(pe, ("xT", 0, b))
                    c = slice(p * P, (p + 1) * P)
                    filled(product3(bank(step), wq_hi0[:, c], wq_lo0[:, c], xT_hi[:, b, :], xT_lo[:, b, :]), step)
                elif kind == "score":
                    b, t, p = step[1:]
                    wait_moved(pe, ("q", b, p))
                    wait_moved(pe, ("kT", p))
                    c = slice(t * P, (t + 1) * P)
                    dst = bank(step)[:, 0:2 * CTX].rearrange("p (j c) -> p j c", j=2)
                    filled(product3(dst, q_hi[:, b, p, c], q_lo[:, b, p, c],
                                    k_hi[:, p, b, :, 0:CTX], k_lo[:, p, b, :, 0:CTX]), step)
                elif kind == "pT":
                    b, t, k = step[1:]
                    r = (b * T + t) % 2
                    pe.wait_ge(prob_normed, position[("norm", b, t)])
                    for m in range(4 if k < 2 else 2):
                        at = (4 * k + m) * P if k < 2 else H0 * P + 4 * m * PAD
                        src = prob_n[:, r, at:at + P]
                        ins = pe.transpose(bank(step)[:, m * P:(m + 1) * P], src, ident[:, :])
                    filled(ins, step)
                elif kind == "pv":
                    b, p = step[1:]
                    for k in range(3):
                        wait_moved(pe, ("pT", b, T - 1, k))
                    wait_moved(pe, ("vf", b))
                    wait_moved(pe, ("vs", b))
                    pe.matmul(bank(step), vs0[:, b, p, :], probT0[:, H0 + p // 2, :],
                              start=True, stop=False, skip_group_check=True)
                    for j in range(2):
                        h = 2 * p + j
                        ins = pe.matmul(bank(step)[64 * j:64 * j + 64, :], v0[:, b, h * DH0:(h + 1) * DH0], probT0[:, h, :],
                                        start=False, stop=True, skip_group_check=True)
                    filled(ins, step)
                elif kind == "wo":
                    b = step[1]
                    pe.wait_ge(loaded["wo0"], 16)
                    for p in range(PAIRS):
                        wait_moved(pe, ("pv", b, p))
                        for t in range(T):
                            ins = pe.matmul(bank(step)[:, t * P:(t + 1) * P], outT0[:, p, t * P:(t + 1) * P], wo0[:, p, :],
                                            start=(p == 0 and t == 0), stop=(p == PAIRS - 1), skip_group_check=True)
                    filled(ins, step)
                elif kind == "gate":
                    s, b = step[1:]
                    wait_moved(pe, ("xT", s, b))
                    pe.wait_ge(lo_of["gates"], 1)
                    n_e = EXPERTS[s]
                    c = slice(0, E0) if s == 1 else slice(E0, E0 + E1)
                    for t in range(T):
                        x = slice(t * P, (t + 1) * P)
                        ins = product3(bank(step)[:, t * n_e:(t + 1) * n_e], xT_hi[:, b, x], xT_lo[:, b, x],
                                       gates_hi[:, c], gates_lo[:, c])
                    filled(ins, step)
                elif kind == "cwT":
                    s, b = step[1:]
                    pe.wait_ge(cw_ready, position[step])
                    for t in range(T):
                        ins = pe.transpose(bank(step)[0:EXPERTS[s], t * P:(t + 1) * P], cw[:, b, t, 0:EXPERTS[s]], ident[:, :])
                    filled(ins, step)
                elif kind in ("h1", "h3"):
                    s, b, i = step[1:]
                    hi, lo, name = w13[s]
                    w = 2 * i + (kind == "h3")
                    wait_moved(pe, ("xT", s, b))
                    pe.wait_ge(lo_of[name], w // CHUNK + 1)
                    filled(product3(bank(step), hi[:, w, :], lo[:, w, :], xT_hi[:, b, :], xT_lo[:, b, :]), step)
                elif kind == "down":
                    s, b, i = step[1:]
                    n = hid_index[(s, b, i)]
                    key = ("y", s, b)
                    if i == 0:
                        wait_bank_free(pe, key)
                    last = i == N_HID[s] - 1
                    if s == 1:
                        pe.wait_ge(loaded["w2_0"], 16)
                        pe.wait_ge(hid_ready, n + 1)
                        for t in range(T):
                            ins = pe.matmul(bank(key)[:, t * P:(t + 1) * P], hid[:, n % HIDS, t * P:(t + 1) * P], w2_0[:, i, :],
                                            start=(i == 0 and t == 0), stop=last, skip_group_check=True)
                    else:
                        pe.wait_ge(lo_of["w2_1"], i // CHUNK + 1)
                        m = n - first_split
                        pe.wait_ge(hid_split, m + 1)
                        pe.matmul(bank(key), w2_hi1[:, i, :], hid_hi[:, m % 2, :], start=(i == 0), stop=False)
                        pe.matmul(bank(key), w2_lo1[:, i, :], hid_hi[:, m % 2, :], start=False, stop=False)
                        ins = pe.matmul(bank(key), w2_hi1[:, i, :], hid_lo[:, m % 2, :], start=False, stop=last)
                    if last:
                        filled(ins, key)
                    else:
                        ins.then_inc(hid_used, 1)
                elif kind == "yT":
                    wait_moved(pe, ("y",) + step[1:])
                    for t in range(T):
                        ins = pe.transpose(bank(step)[:, t * P:(t + 1) * P], yT[:, t * P:(t + 1) * P], ident[:, :])
                    filled(ins, step)
                elif kind == "k1":
                    g = step[1]
                    pe.wait_ge(loaded["wqkv1"], 16 * N_WQKV1)
                    filled(pe.matmul(bank(step)[:, 0:B * CP], wk1[:, g, :], ctxT[:, :, :].rearrange("k b c -> k (b c)"),
                                     start=True, stop=True), step)
                elif kind == "q1":
                    b, g = step[1:]
                    wait_moved(pe, ("xT", 2, b))
                    pe.wait_ge(lo_of["wq1"], 1)
                    c = slice(g * P, (g + 1) * P)
                    filled(product3(bank(step), wq_hi1[:, c], wq_lo1[:, c], xT_hi[:, b, :], xT_lo[:, b, :]), step)
                elif kind == "score1":
                    b, t, g, half = step[1:]
                    wait_moved(pe, ("q1", b, g))
                    pe.wait_ge(k1_placed, 4 * (g + 1))
                    filled(pe.matmul(bank(step)[:, 0:2 * CTX].rearrange("p (j c) -> p j c", j=2), q1[:, b, g, t * P:(t + 1) * P],
                                     k1[:, b, g, 2 * half:2 * half + 2, 0:CTX], start=True, stop=True), step)
                elif kind == "mT":
                    b = step[1]
                    for g in range(G1):
                        for half in range(2):
                            wait_moved(pe, ("score1", b, T - 1, g, half))
                    for t in range(T):
                        ins = pe.transpose(bank(step)[0:H1, t * P:(t + 1) * P],
                                           neg_max1[:, b, t, :, :].rearrange("p j g -> p (j g)"), ident[:, :])
                    filled(ins, step)
                elif kind == "expT":
                    b, g, j = step[1:]
                    pe.wait_ge(nm_placed[b], 16 * N_NM)
                    pe.wait_ge(k1s_placed, g + 1)
                    w = k1[:, b, g, j, 0:P] if j < 4 else k1s[:, b, g, :, :].rearrange("p j c -> p (j c)")
                    filled(pe.matmul(bank(step), w, q1[:, b, g, :], start=True, stop=True), step)
                elif kind == "pv1":
                    b, g = step[1:]
                    r = (b * G1 + g) % 2
                    wait_moved(pe, ("vf1", b))
                    wait_moved(pe, ("vs1", b))
                    wait_moved(pe, ("expT", b, g, 4))
                    pe.matmul(bank(step), vs1[:, b, g, :], probT1[:, r, 4, :], start=True, stop=False, skip_group_check=True)
                    for j in range(4):
                        wait_moved(pe, ("expT", b, g, j))
                        rows = slice(PAD * j, PAD * j + PAD)
                        ins = pe.matmul(bank(step)[rows, :], v1[:, b, g * P + PAD * j:g * P + PAD * (j + 1)], probT1[:, r, j, :],
                                        start=False, stop=True, skip_group_check=True, tile_position=(0, PAD * j))
                    filled(ins, step)
                elif kind == "oT":
                    b, g = step[1:]
                    wait_moved(pe, ("pv1", b, g))
                    for t in range(T):
                        ins = pe.transpose(bank(step)[:, t * P:(t + 1) * P], od[:, g % 2, t * P:(t + 1) * P], ident[:, :])
                    filled(ins, step)
                elif kind == "onT":
                    b = step[1]
                    wait_moved(pe, ("oT", b, G1 - 1))
                    wait_moved(pe, ("oT", b, G1 - 2))
                    for t in range(T):
                        ins = pe.transpose(bank(step)[:, t * P:(t + 1) * P], on[:, t, :], ident[:, :])
                    filled(ins, step)
                elif kind == "wo1":
                    b = step[1]
                    wait_moved(pe, ("onT", b))
                    for t in range(T):
                        ins = pe.matmul(bank(step)[:, t * P:(t + 1) * P], onT[:, t * P:(t + 1) * P], wo1[:, :],
                                        start=(t == 0), stop=True, skip_group_check=True)
                    filled(ins, step)


def lay_out(x, ctx_768, L0_xattn_Wq, L0_xattn_Wk, L0_xattn_Wv, L0_xattn_Wo, L0_xattn_bo, L0_ffn_w_gate, L0_ffn_w1_e,
            L0_ffn_w3_e, L0_ffn_w2_e, L0_ffn_w1_s, L0_ffn_w3_s, L0_ffn_w2_s, L1_xattn_Wq, L1_xattn_Wk, L1_xattn_Wv,
            L1_xattn_Wo, L1_ffn_router_w, L1_ffn_experts_bias, L1_ffn_w1, L1_ffn_w3, L1_ffn_w2, L1_ffn_sw1, L1_ffn_sw3,
            L1_ffn_sw2):
    f = np.float32
    d = {}
    d["x"] = x.reshape(B * T, P, P).transpose(1, 0, 2)
    ctxT = np.ones((CD + 1, B, CP), f)
    ctxT[:CD, :, :CTX] = ctx_768.transpose(2, 0, 1)
    ctxT[:CD, :, CTX:] = ctxT[:CD, :, CTX - 1:CTX]
    d["ctxT"] = ctxT
    d["ctxT_rest"] = np.tile(ctxT[:, :, P:], (1, 1, 4))
    d["wq0"], d["wk0"], d["wv0"] = L0_xattn_Wq, L0_xattn_Wk, L0_xattn_Wv
    d["wo0"] = L0_xattn_Wo.reshape(PAIRS, P, P).transpose(1, 0, 2)
    d["bo"] = np.broadcast_to(L0_xattn_bo, (P, P))
    d["gates"] = np.concatenate([L0_ffn_w_gate.T, L1_ffn_router_w.T], axis=1)
    d["gate_bias"] = np.broadcast_to(L1_ffn_experts_bias, (P, E1))
    d["ident"] = np.eye(P, dtype=f)
    d["lower_first"] = np.broadcast_to(np.tril(np.ones((NG, NG), f), -1), (P, NG, NG))
    lo_rows = np.zeros((4, PAD, 2), f)
    lo_rows[:, DH1:2 * DH1, 0] = -1.0
    lo_rows[:, 2 * DH1:3 * DH1, 1] = -1.0
    d["lo_rows"] = lo_rows.reshape(P, 2)

    row = np.arange(P)
    real = (row % PAD < REST)[:, None]
    d["vs0_mask"] = np.stack([real & (row[:, None] // PAD == 2 * q + row // DH0) for q in range(2)], axis=1).astype(f)
    d["vs1_mask"] = (real & (row[:, None] // PAD == row // PAD)).astype(f)
    d["head_rows"] = (row[:, None] // PAD == np.arange(4)).astype(f)

    def hidden(shared1, shared3, expert1, expert3):
        w = [np.concatenate(pair, axis=1).reshape(P, -1, P) for pair in ((shared1, expert1), (shared3, expert3))]
        return np.stack(w, axis=2).reshape(P, -1, P)

    d["w13_0"] = hidden(L0_ffn_w1_s.T, L0_ffn_w3_s.T, L0_ffn_w1_e.transpose(2, 0, 1).reshape(P, -1),
                        L0_ffn_w3_e.transpose(2, 0, 1).reshape(P, -1))
    w2_0 = np.concatenate([L0_ffn_w2_s.T, L0_ffn_w2_e.transpose(0, 2, 1).reshape(-1, P)])
    d["w2_0"] = w2_0.reshape(-1, P, P).transpose(1, 0, 2)
    d["w13_1"] = hidden(L1_ffn_sw1[0], L1_ffn_sw3[0], L1_ffn_w1.transpose(1, 0, 2).reshape(P, -1),
                        L1_ffn_w3.transpose(1, 0, 2).reshape(P, -1))
    w2_1 = np.concatenate([L1_ffn_sw2[0], L1_ffn_w2.reshape(-1, P)])
    d["w2_1"] = w2_1.reshape(-1, P, P).transpose(1, 0, 2)

    def groups(w, copies, ones_at):
        rows = w.shape[0] + (1 if ones_at else 0)
        g = np.zeros((rows, H1, PAD), f)
        for r in range(copies):
            g[:w.shape[0], :, r * DH1:(r + 1) * DH1] = w.reshape(w.shape[0], H1, DH1)
        for c in ones_at:
            g[-1, :, c] = 1.0
        return g.reshape(rows, G1 * P)

    d["wq1"] = groups(L1_xattn_Wq, 3, ())
    d["wk1"] = groups(L1_xattn_Wk, 3, (3 * DH1, 3 * DH1 + 1)).reshape(CD + 1, G1, P)
    d["wv1"] = groups(L1_xattn_Wv, 1, (DH1,))
    d["wo1"] = L1_xattn_Wo
    return {k: np.ascontiguousarray(v) for k, v in d.items()}


def kernel(**inputs):
    import concourse.bacc as bacc
    from concourse.bass_utils import run_bass_kernel_spmd

    nc = bacc.Bacc("TRN2", target_bir_lowering=False, num_devices=1)
    arrays = {"in_" + k: v for k, v in lay_out(**{k: np.asarray(v) for k, v in inputs.items()}).items()}
    aps = {k[3:]: nc.dram_tensor(k, v.shape, mybir.dt.from_np(v.dtype), kind="ExternalInput").ap() for k, v in arrays.items()}
    out = nc.dram_tensor(OUT_NAME, (P, B * T, P), F32, kind="ExternalOutput").ap()
    build(nc, aps, out)
    got = run_bass_kernel_spmd(nc, [arrays], core_ids=[0]).results[0][OUT_NAME]
    return got.transpose(1, 0, 2).reshape(B, TOK, P)
```
